# Optimizing a Trainium2 kernel written in Bass

```python
import numpy as np
import jax
import jax.numpy as jnp

def _softmax(x, axis=-1):
    return jax.nn.softmax(x, axis=axis)

def _gelu(x):
    return jax.nn.gelu(x, approximate=True)

def _silu(x):
    return jax.nn.silu(x)

def _sigmoid(x):
    return jax.nn.sigmoid(x)

def _layernorm(x, axis=-1, eps=1e-05):
    m = jnp.mean(x, axis=axis, keepdims=True)
    v = jnp.var(x, axis=axis, keepdims=True)
    return (x - m) / jnp.sqrt(v + eps)

def _scatter_add(tgt, idx, src, axis=0):
    return tgt.at[idx].add(src)

def _segment_sum(src, seg, n):
    return jax.ops.segment_sum(src, seg, n)
kernel_name = 'mk_gnn_preln_d2_gnn_r8_e5564d'

def setup_inputs(seed: int=0):
    np.random.seed(seed)
    _w = jnp.asarray

    def _rec_inputs():
        import jax
        import jax.numpy as jnp
        _gk = jax.random.key(seed)
        x = -0.000202 + 1 * jax.random.normal(jax.random.fold_in(_gk, 1), (6250, 128), jnp.float32)
        _s = jax.random.randint(jax.random.fold_in(_gk, 2), (100000,), 0, 6250, jnp.int32)
        _d = jax.random.randint(jax.random.fold_in(_gk, 3), (100000,), 0, 6250, jnp.int32)
        _loop = jnp.arange(6250, dtype=jnp.int32)
        src = jnp.concatenate([_s, _d, _loop])
        dst = jnp.concatenate([_d, _s, _loop])
        _o = jnp.argsort(dst, stable=True)
        src = src[_o]
        dst = dst[_o]
        edge_type_9 = jax.random.randint(jax.random.fold_in(_gk, 13), (206250,), 0, 9, jnp.int32)
        return (x, src, dst, edge_type_9)
    x, src, dst, edge_type_9 = _rec_inputs()

    def _L0_gnn_setup():
        import jax, jax.numpy as jnp
        import numpy as np
        N_NODES = 6250
        N_EDGES = 75000
        D_IN = 128
        D_OUT = 128
        key = jax.random.key(seed)
        k1, k2, k3, k4, k5 = jax.random.split(key, 5)
        feature = jax.random.normal(k1, (N_NODES, D_IN), dtype=jnp.float32)
        edge_src = jax.random.randint(k2, (N_EDGES,), 0, N_NODES, dtype=jnp.int64)
        edge_dst = jax.random.randint(k3, (N_EDGES,), 0, N_NODES, dtype=jnp.int64)
        W = jax.random.normal(k4, (D_OUT, D_IN), dtype=jnp.float32) * (1.0 / np.sqrt(D_IN))
        b = jax.random.normal(k5, (D_OUT,), dtype=jnp.float32) * 0.01
        return {'feature': feature, 'edge_src': edge_src, 'edge_dst': edge_dst, 'W': W, 'b': b}
    _L0_gnn_all = _L0_gnn_setup()
    _L0_gnn_in = {k: v for k, v in _L0_gnn_all.items() if k in ('W', 'b')}
    del _L0_gnn_all

    def _L1_gnn_setup():
        import jax, jax.numpy as jnp
        import numpy as np
        NUM_EDGE_TYPES = 8
        HIDDEN = 128
        N_NODES = 6250
        N_EDGES = 75000

        def _gru_cell(x, h, W_ih, W_hh, b_ih, b_hh):
            H = h.shape[-1]
            gi = x @ W_ih.T + b_ih
            gh = h @ W_hh.T + b_hh
            i_r, i_z, i_n = (gi[:, :H], gi[:, H:2 * H], gi[:, 2 * H:])
            h_r, h_z, h_n = (gh[:, :H], gh[:, H:2 * H], gh[:, 2 * H:])
            r = jax.nn.sigmoid(i_r + h_r)
            z = jax.nn.sigmoid(i_z + h_z)
            n = jnp.tanh(i_n + r * h_n)
            return (1.0 - z) * n + z * h
        key = jax.random.key(seed)
        ks = jax.random.split(key, 10)
        H = HIDDEN
        h = jax.random.normal(ks[0], (N_NODES, H), dtype=jnp.float32)
        edge_index = jax.random.randint(ks[1], (2, N_EDGES), 0, N_NODES, dtype=jnp.int32)
        edge_type = jax.random.randint(ks[2], (N_EDGES,), 0, NUM_EDGE_TYPES + 1, dtype=jnp.int32)
        s = 1.0 / np.sqrt(H)
        W_msg = jax.random.uniform(ks[3], (H, H), jnp.float32, -s, s)
        b_msg = jax.random.uniform(ks[4], (H,), jnp.float32, -s, s)
        edge_embed = jax.random.normal(ks[5], (NUM_EDGE_TYPES + 1, H), dtype=jnp.float32)
        W_ih = jax.random.uniform(ks[6], (3 * H, H), jnp.float32, -s, s)
        W_hh = jax.random.uniform(ks[7], (3 * H, H), jnp.float32, -s, s)
        b_ih = jax.random.uniform(ks[8], (3 * H,), jnp.float32, -s, s)
        b_hh = jax.random.uniform(ks[9], (3 * H,), jnp.float32, -s, s)
        return {'h': h, 'edge_index': edge_index, 'edge_type': edge_type, 'num_nodes': N_NODES, 'W_msg': W_msg, 'b_msg': b_msg, 'edge_embed': edge_embed, 'W_ih': W_ih, 'W_hh': W_hh, 'b_ih': b_ih, 'b_hh': b_hh}
    _L1_gnn_all = _L1_gnn_setup()
    _L1_gnn_in = {k: v for k, v in _L1_gnn_all.items() if k in ('W_msg', 'b_msg', 'edge_embed', 'W_ih', 'W_hh', 'b_ih', 'b_hh')}
    del _L1_gnn_all
    return {'x': x, 'src': src, 'dst': dst, 'edge_type_9': edge_type_9, 'L0_gnn_W': _L0_gnn_in['W'], 'L0_gnn_b': _L0_gnn_in['b'], 'L1_gnn_W_msg': _L1_gnn_in['W_msg'], 'L1_gnn_b_msg': _L1_gnn_in['b_msg'], 'L1_gnn_edge_embed': _L1_gnn_in['edge_embed'], 'L1_gnn_W_ih': _L1_gnn_in['W_ih'], 'L1_gnn_W_hh': _L1_gnn_in['W_hh'], 'L1_gnn_b_ih': _L1_gnn_in['b_ih'], 'L1_gnn_b_hh': _L1_gnn_in['b_hh']}

def reference(x, src, dst, edge_type_9, L0_gnn_W, L0_gnn_b, L1_gnn_W_msg, L1_gnn_b_msg, L1_gnn_edge_embed, L1_gnn_W_ih, L1_gnn_W_hh, L1_gnn_b_ih, L1_gnn_b_hh):
    import jax
    import jax.numpy as jnp

    def _L0_gnn_ref(feature, edge_src, edge_dst, W, b):
        import jax, jax.numpy as jnp
        import numpy as np
        N_NODES = 6250
        N_EDGES = 75000
        D_IN = 128
        D_OUT = 128
        N = feature.shape[0]
        deg = jax.ops.segment_sum(jnp.ones(edge_src.shape, dtype=feature.dtype), edge_src, num_segments=N)
        norm = jnp.power(jnp.clip(deg, 1.0, None), -0.5)[:, None]
        feat = feature * norm
        msgs = feat[edge_src]
        h = jax.ops.segment_sum(msgs, edge_dst, num_segments=N)
        h = jax.nn.relu(h)
        return h @ W.T + b

    def _L1_gnn_ref(h, edge_index, edge_type, num_nodes, W_msg, b_msg, edge_embed, W_ih, W_hh, b_ih, b_hh):
        import jax, jax.numpy as jnp
        import numpy as np
        NUM_EDGE_TYPES = 8
        HIDDEN = 128
        N_NODES = 6250
        N_EDGES = 75000

        def _gru_cell(x, h, W_ih, W_hh, b_ih, b_hh):
            H = h.shape[-1]
            gi = x @ W_ih.T + b_ih
            gh = h @ W_hh.T + b_hh
            i_r, i_z, i_n = (gi[:, :H], gi[:, H:2 * H], gi[:, 2 * H:])
            h_r, h_z, h_n = (gh[:, :H], gh[:, H:2 * H], gh[:, 2 * H:])
            r = jax.nn.sigmoid(i_r + h_r)
            z = jax.nn.sigmoid(i_z + h_z)
            n = jnp.tanh(i_n + r * h_n)
            return (1.0 - z) * n + z * h
        src = edge_index[0]
        dst = edge_index[1]
        src_h = h[src] @ W_msg.T + b_msg
        emb = edge_embed[jnp.clip(edge_type, 0, NUM_EDGE_TYPES)]
        msg = src_h + emb
        messages = jax.ops.segment_sum(msg, dst, num_segments=num_nodes)
        h_new = _gru_cell(messages, h[:num_nodes], W_ih, W_hh, b_ih, b_hh)
        result = jnp.zeros_like(h).at[:num_nodes].set(h_new)
        return result
    edge_index = jnp.stack([src, dst])
    h = jnp.maximum(_layernorm(x, axis=-1), 0.0)
    x = x + _L0_gnn_ref(h, src, dst, L0_gnn_W, L0_gnn_b)
    h = jnp.maximum(_layernorm(x, axis=-1), 0.0)
    x = x + _L1_gnn_ref(h, edge_index, edge_type_9, 6250, L1_gnn_W_msg, L1_gnn_b_msg, L1_gnn_edge_embed, L1_gnn_W_ih, L1_gnn_W_hh, L1_gnn_b_ih, L1_gnn_b_hh)
    return x

_drawn_inputs = setup_inputs


def setup_inputs(seed=0):
    import zlib

    import numpy as np

    out = dict(_drawn_inputs(seed))
    spreads = {}
    factors = {'L0_gnn_b': 8.0, 'L1_gnn_W_hh': 3.217, 'L1_gnn_b_ih': 22.111, 'L1_gnn_b_hh': 22.352}
    for name, (base, spread) in spreads.items():
        noise = np.random.default_rng([zlib.crc32(name.encode()), seed]).standard_normal(out[name].shape)
        drawn = base * np.exp(spread * noise) if base else spread * noise
        out[name] = jnp.asarray(drawn.astype(out[name].dtype))
    for name, factor in factors.items():
        out[name] = (out[name] * factor).astype(out[name].dtype)
    return out
```

```python
import numpy as np
from contextlib import ExitStack, contextmanager

import concourse.bass as bass
from concourse import mybir

F32, F16, I32 = mybir.dt.float32, mybir.dt.float16, mybir.dt.int32
ALU = mybir.AluOpType
ACT = mybir.ActivationFunctionType
AX = mybir.AxisListType.X

N, D, E, TYPES = 6250, 128, 206250, 9
LO = 125
BLOCKS = N // LO
EPS = 1e-5

CH = 250
CHUNKS = N // CH
CB = CH // LO

WIN = 5
WINDOWS = N // WIN
GROUPS = 10
EDGES_MAX = 256
HALVES = EDGES_MAX // 128
TA, TB = 3, 3
SLOTS = BLOCKS + TB
PITCH = SLOTS + 1
WCOLS = WIN * SLOTS
CHWIN = CH // WIN
PAIRS = CHWIN // 2
BATCH = 20
BATCHES = CHWIN * HALVES // BATCH
PSLOTS = 3
CHT = CHWIN * HALVES

PARTE = E // LO
SHIFT = 25
RROWS = E // SHIFT
HALO = EDGES_MAX
HEADS, HLEN = 375, 550
SEARCH = GROUPS + 1
SBITS, DBITS = 13, 13
SMASK = (1 << SBITS) - 1
NOWHERE = SMASK
MAGIC = 12582912.0
HSCALE = 4096.0
PARTS = [(0, 14), (14, 27), (27, 40), (40, SLOTS)]
PARTS0 = PARTS[:-1] + [(40, BLOCKS)]


SEMAPHORES = """
heads_in pad_set edges_in packed runs_out x_in0 x_in1 x_in2 x_in3 x_in4 weights_in sq_sum eps_set
wm_norm var0 std0 nmr0 h0_done turned meta_act meta_dve consts heads_f heads_all squares scaled g_col flags
flag_sum fields g0 rows_i cand_in run_i runs_in x_b v_prep flag_set x1 aggr psX hst h1 psT tbs psM pvar pstd
pnm h1T tab_hi x1_kept tab_lo msg rz nin psRZ psN hnew result psO nn out deg deg_root onehot evac built degree
adj_out0 adj_out1 mch used0 used1 degrees tab0 tab0_hi emb_in norm tab0_zero tab1_zero v_fast v_general v_build g_seen flat_in tab_zero sum_zero gemb_out h0_scaled table_out table1_out g1 ghist ghot gerows gturned0 gturned1 sum_in0 sum_in1 gadded0 gadded1 gindex0 gindex1 grows0 grows1 gsums0 gsums1 gdiag0 gdiag1 gacross0 gacross1 gsame0 gsame1 gproduct0 gproduct1 load0_0_0
load0_0_1 load0_0_2 load0_0_3 load0_1_0 load0_1_1 load0_1_2 load0_1_3 load1_0_0 load1_0_1 load1_0_2 load1_0_3
load1_1_0 load1_1_1 load1_1_2 load1_1_3
""".split()


class Chain:

    def __init__(self, eng, sem):
        self.eng, self.sem, self.base, self.k = eng, sem, 0, 0

    def did(self, ins):
        ins.then_inc(self.sem, 1)
        self.k += 1
        return ins

    def wait(self):
        self.eng.wait_ge(self.sem, self.base + self.k)

    @contextmanager
    def loop(self, i, times, steps):
        before = self.base + self.k
        self.base, self.k = before + steps * i, 0
        yield
        assert self.k == steps, (self.k, steps)
        self.base, self.k = before + steps * times, 0


def over_chunks(eng, body, chain=None, steps=0, first=1):
    for c in range(first):
        body(c, c % 2)
    n = (CHUNKS - first) // 2
    with eng.Fori(0, n) as i:
        if chain is not None:
            with chain.loop(i, n, 2 * steps):
                body(2 * i + first, 1)
                body(2 * i + first + 1, 0)
        else:
            body(2 * i + first, 1)
            body(2 * i + first + 1, 0)


def over_tiles(eng, body, chain=None, steps=0):
    body(0)
    with eng.Fori(0, PARTE - 1) as i:
        if chain is not None:
            with chain.loop(i, PARTE - 1, steps):
                body(i + 1)
        else:
            body(i + 1)


def positive(eng, sem, value):
    if not isinstance(value, int) or value > 0:
        eng.wait_ge(sem, value)


def gnn(nc, x, src, dst, typ, w0t, b0, wmt, bm, emb, wiht, whht, bih, bhh, out):
    ctx = ExitStack()
    sems = {name: ctx.enter_context(nc.semaphore(name)) for name in SEMAPHORES}

    def sem(name):
        return sems[name]

    def sb(name, shape, dt):
        return ctx.enter_context(nc.sbuf_tensor(name, shape, dt))

    def dram(name, shape, dt):
        return nc.dram_tensor(name, shape, dt).ap()

    with ctx:
        adj_d = dram("adjacency", (CHUNKS, 128, SLOTS * CH), F16)
        runs_d = dram("edge_runs", (RROWS, EDGES_MAX), I32)
        table_d = dram("rows", (N, D), F32)
        sum_d = [dram(f"row_sums{L}", (N + LO, D), F32) for L in range(2)]
        emb_d = dram("scaled_embedding", (TYPES, D), F32)

        x_sb = sb("x_sb", [128, BLOCKS, D], F32)
        h_sb = sb("h_sb", [128, BLOCKS * D], F32)
        h0 = h_sb[:, :].rearrange("p (b f) -> p b f", f=D)
        h1T = h_sb[:, 0:N]
        ring = sb("ring", [128, 2, SLOTS * CH], F16)
        adj = [ring[:, k, :].rearrange("p (h n) -> p h n", n=CH) for k in range(2)]
        tab = [sb(f"tab{k}", [128, SLOTS * 2 * D], F16) for k in range(2)]
        tabv = [t[:, :].rearrange("p (h s f) -> p h s f", s=2, f=D) for t in tab]
        combo = sb("combo", [128, 2, BATCH, WIN * PITCH], F16)
        lohot = sb("lohot", [128, 2, BATCH, 128], F16)
        ring32 = ring[:, :, :].rearrange("p a n -> p (a n)").bitcast(I32)
        comb32 = combo[:, :, :, :].rearrange("p a k n -> p (a k n)").bitcast(I32)
        W = PARTE + HALO
        raw = ring32[:, 0:3 * W].rearrange("p (a n) -> p a n", a=3)
        packed = ring32[:, 3 * W:4 * W]
        ptmp = ring32[:, 4 * W:5 * W]
        GE = GROUPS * EDGES_MAX
        runs = ring32[:, 5 * W:5 * W + GE]
        cand = tab[0][:, 0:2 * SEARCH * HLEN].bitcast(I32).rearrange("p (g n) -> p g n", g=SEARCH)
        below = tab[1][:, 0:2 * SEARCH * HLEN].bitcast(F32).rearrange("p (g n) -> p g n", g=SEARCH)
        unsorted = tab[1][:, 0:2 * PARTE].bitcast(F32)
        ui = [ring32[:, k * GE:(k + 1) * GE] for k in range(3)]
        uf = [a.bitcast(F32) for a in ui] + [comb32[:, k * GE:(k + 1) * GE].bitcast(F32) for k in range(2)]
        fields = tab[0][:, 0:4 * GE].rearrange("p (k n) -> p k n", k=4)
        TILES = WINDOWS * HALVES
        GH = GROUPS * HALVES
        metav = tab[1][:, 0:4 * TILES].rearrange("p (k w s) -> p k w s", k=4, s=GH)
        meta = tab[1][:, 0:4 * TILES].rearrange("p (k t) -> p k t", k=4)

        mch = sb("mch", [128, 2, 2, CHT, 2], F16)
        mch_s = sb("mch_s", [128, 2, 2, CHT], F16)
        iota_w = sb("iota_w", [128, WIN * PITCH], F16)
        iota_lo = sb("iota_lo", [128, 128], F16)
        iota_s = sb("iota_s", [128, WIN, TB], F16)
        iota_t = sb("iota_t", [128, TA], F16)
        ident = sb("ident", [128, 128], F32)
        identh = sb("identh", [128, 128], F16)
        zeroh = sb("zeroh", [128, 512], F16)
        zeroh2 = sb("ghot", [128, 192], F16)
        ones = sb("ones", [128, 128], F32)
        thr = sb("thr", [128, SEARCH], F32)
        heads_i = sb("heads_i", [1, HEADS], I32)
        heads = sb("heads", [1, HEADS], F32)
        cnt = sb("cnt", [128, SEARCH], F32)
        row = sb("row", [128, SEARCH], F32)
        row_i = sb("row_i", [128, SEARCH], I32)
        start = sb("start", [128, SEARCH], F32)
        run0 = sb("run0", [128, GROUPS], F32)
        run_i = sb("run_i", [128, GROUPS], I32)
        need = sb("need", [128, GROUPS], F32)
        flags = sb("flags", [128, 4], F32)
        flag_i = sb("flag_i", [1, 1], I32)
        mv = sb("mv", [128, BLOCKS, 2], F32)
        rstd = sb("rstd", [128, BLOCKS], F32)
        nmr = sb("nmr", [128, BLOCKS], F32)
        epst = sb("epst", [128, 1], F32)
        deg = sb("deg", [128, BLOCKS], F32)
        norm = sb("norm", [128, BLOCKS], F32)
        w0_sb = sb("w0_sb", [128, D], F32)
        b0_sb = sb("b0_sb", [128, D], F32)
        wm_sb = sb("wm_sb", [128, D], F32)
        bm_sb = sb("bm_sb", [128, D], F32)
        wih_sb = sb("wih_sb", [128, 3 * D], F32)
        whh_sb = sb("whh_sb", [128, 3 * D], F32)
        bg_i = sb("bg_i", [128, 3], F32)
        bg_h = sb("bg_h", [128, 3], F32)
        bg = sb("bg", [128, 2], F32)
        gsc = sb("gsc", [128, D], F32)
        ginv = sb("ginv", [128, 1], F32)
        embs = sb("embs", [TYPES, D], F32)
        embh = sb("embh", [TYPES, 2, D], F16)
        pst = sb("pst", [128, CB, 6], F32)
        pmv = sb("pmv", [128, CB, 2], F32)
        pm2 = sb("pm2", [128, CB], F32)
        prs = sb("prs", [128, CB], F32)
        pnm = sb("pnm", [128, CB], F32)

        lohot32 = lohot[:, :, :, :].rearrange("p a k n -> p (a k n)").bitcast(F32)

        def carve(words, at, *shape):
            n = int(np.prod(shape))
            a = words[:, at:at + n]
            if len(shape) > 1:
                a = a.rearrange("p (a b) -> p a b", a=shape[0])
            return a, at + n

        scr, at = carve(lohot32, 0, HEADS)
        stats, at = carve(lohot32, at, BLOCKS, 6)
        emb_sb, at = carve(lohot32, at, TYPES, D)
        sq, at = carve(lohot32, at, D)
        gtmp, at = carve(lohot32, at, D)
        late = comb32.bitcast(F32)
        x1s, at = carve(late, 2048, CB, D)
        h1s, at = carve(late, at, CB, D)
        tbs, at = carve(late, at, CB, D)
        rz, at = carve(late, at, 2, CH)
        aggr, at = carve(late, at, CH)
        hst, at = carve(late, at, CH)
        msgs, at = carve(late, at, CH)
        nin, at = carve(late, at, CH)
        nn, at = carve(late, at, CH)
        hnew, at = carve(late, at, CH)

        ps = ctx.enter_context(nc.psum_tensor("ps", [128, 8, 512], F32))
        psD = [ps[:, k, 0:CH] for k in range(2)]
        psX = ps[0:LO, 2, 0:CB * D].rearrange("p (b f) -> p b f", f=D)
        psT = ps[:, 3, 0:CH]
        psM = ps[0:LO, 4, 0:CB * D].rearrange("p (b f) -> p b f", f=D)
        psRZ = ps[:, 2, :].rearrange("p (a n) -> p a n", a=2)[:, :, 0:CH]
        psN = ps[:, 3, :].rearrange("p (a n) -> p a n", a=2)[:, :, 0:CH]
        psO = psM
        psDeg = ps[:, 6, 0:BLOCKS * 10]
        psH = ps[:, 7, :]

        x_v = x.rearrange("(b p) f -> p b f", p=LO)
        out_v = out.rearrange("(b p) f -> p b f", p=LO)
        table_v = table_d.rearrange("(b p) f -> p b f", p=LO)
        XP = 5
        XB = BLOCKS // XP

        flat_i = ring32[:, 0:3 * PARTE].rearrange("p (a n) -> p a n", a=3)
        flat_f = ring32[:, 3 * PARTE:7 * PARTE].bitcast(F32).rearrange("p (a n) -> p a n", a=4)
        src_f, dst_f, q_f, lo_f = (flat_f[:, k, :] for k in range(4))
        gbuf = comb32[:, 0:2048].bitcast(F32)
        cut = lambda k, n: gbuf[:, 128 * k:128 * k + n]
        rows_in, erows_in, diag, same, lower, sums, before = (cut(k, 128) for k in range(7))
        small = cut(7, 8)
        count_c, dup_c, toward_c, trash_c = (small[:, k:k + 1] for k in range(4))
        ints = cut(8, 8).bitcast(I32)
        isrc, itype, idst = (ints[:, k:k + 1] for k in range(3))
        sum_in = cut(9, 256).rearrange("p (b f) -> p b f", f=D)
        psB = ps[:, 5, 0:128]
        psS = ps[:, 7, 0:128]
        NE = LO
        ghot = zeroh2[:, :]
        sum_v = [sum_d[L][0:N, :].rearrange("(b p) f -> p b f", p=LO) for L in range(2)]

        def spread(a, shape):
            return a.unsqueeze(2).broadcast_to(shape)


        def prepare_sync(sp):
            sp.dma_start(heads_i[:, :], dst.rearrange("(a n) -> n a", n=HLEN)[0:1, :],
                         allow_slow_non_contiguous=True).then_inc(sem("heads_in"), 16)
            sp.wait_ge(sem("pad_set"), 1)
            for k, a in enumerate((src, dst, typ)):
                halo = bass.AP(tensor=a.tensor, offset=a.offset, ap=[[PARTE, LO - 1], [1, W]])
                sp.dma_start(raw[0:LO - 1, k, :], halo).then_inc(sem("edges_in"), 16)
                sp.dma_start(raw[LO - 1:LO, k, 0:PARTE], a.rearrange("(p n) -> p n", p=LO)[LO - 1:LO, :])\
                  .then_inc(sem("edges_in"), 16)
            sp.wait_ge(sem("packed"), 1)
            base = packed[0:LO, :]
            rows = bass.AP(tensor=base.tensor, offset=base.offset,
                           ap=[list(base.ap[0]), [SHIFT, PARTE // SHIFT], [1, EDGES_MAX]])
            sp.dma_start(runs_d.rearrange("(p r) n -> p r n", p=LO), rows).then_inc(sem("runs_out"), 16)

        def prepare_scalar(act):
            row_of = lambda a: a.rearrange("(a n) -> a n", a=1)
            for k in range(XP):
                act.dma_start(x_sb[0:LO, k * XB:(k + 1) * XB, :], x_v[:, k * XB:(k + 1) * XB, :])\
                   .then_inc(sem(f"x_in{k}"), 16)
            for to, a in ((w0_sb, w0t), (wm_sb, wmt), (wih_sb, wiht), (whh_sb, whht), (bg_i, bih), (bg_h, bhh),
                          (embs, emb)):
                act.dma_start(to[:, :], a).then_inc(sem("weights_in"), 16)
            for to, a in ((b0_sb[:, :], b0), (bm_sb[:, :], bm),
                          (emb_sb[:, :, :].rearrange("p t f -> p (t f)"), emb.rearrange("t f -> (t f)"))):
                act.dma_start(to, a.partition_broadcast(128)).then_inc(sem("weights_in"), 16)
            act.wait_ge(sem("sq_sum"), 1)
            act.wait_ge(sem("eps_set"), 1)
            act.activation(gsc[:, :], psB, ACT.Sqrt).then_inc(sem("wm_norm"), 1)
            act.wait_ge(sem("var0"), 1)
            act.activation(rstd[0:LO, :], mv[0:LO, :, 1], ACT.Sqrt, bias=epst[0:LO, :]).then_inc(sem("std0"), 1)
            act.wait_ge(sem("nmr0"), 1)
            for b in range(BLOCKS):
                last = act.activation(h0[0:LO, b, :], x_sb[0:LO, b, :], ACT.Relu, bias=nmr[0:LO, b:b + 1],
                                      scale=rstd[0:LO, b:b + 1])
            last.then_inc(sem("h0_done"), 1)
            meta_copies(act, 1)

        META_K = 4 * GH // 5

        def meta_copies(eng, parity):
            for k in range(parity, META_K, 2):
                f, s = divmod(5 * k, GH)
                eng.wait_ge(sem("turned"), k + 1)
                i = ps[:, k % 4, :].bitcast(F16)[:, 0:5 * 128].rearrange("p (s w) -> p s w", w=128)[:, :, 0:LO]
                o = metav[:, f, :, s:s + 5].rearrange("p w s -> p s w")
                if parity:
                    eng.activation(o, i, ACT.Copy).then_inc(sem("meta_act"), 1)
                else:
                    eng.tensor_copy(o, i).then_inc(sem("meta_dve"), 1)

        def prepare_tensor(pe):
            pe.wait_ge(sem("consts"), 1)
            pe.wait_ge(sem("heads_f"), 1)
            pe.matmul(psH[:, 0:HEADS], ones[0:1, :], heads[:, :], start=True, stop=True).then_inc(sem("heads_all"), 1)
            pe.wait_ge(sem("squares"), 1)
            pe.matmul(psB, ones[:, :], sq[:, :], start=True, stop=True).then_inc(sem("sq_sum"), 1)
            pe.wait_ge(sem("scaled"), 1)
            pe.matmul(psH[:, 0:1], gsc[0:1, :], ones[0:1, 0:1], start=True, stop=True).then_inc(sem("g_col"), 1)
            pe.wait_ge(sem("flags"), 1)
            pe.matmul(ps[0:1, 6, 0:1], flags[0:LO, 2:3], ones[0:LO, 0:1], start=True, stop=True)\
              .then_inc(sem("flag_sum"), 1)
            for k in range(META_K):
                f, s = divmod(5 * k, GH)
                if s == 0:
                    pe.wait_ge(sem("fields"), f + 1)
                if k >= 4:
                    pe.wait_ge(sem("meta_act" if k % 2 else "meta_dve"), (k - 4) // 2 + 1)
                o = ps[:, k % 4, :].bitcast(F16)
                for j in range(5):
                    last = pe.transpose(o[:, 128 * j:128 * j + LO],
                                        fields[0:LO, f, 128 * (s + j):128 * (s + j + 1)], identh[0:LO, 0:LO])
                last.then_inc(sem("turned"), 1)

        def prepare_gpsimd(gp):
            gp.memset(raw[:, :, PARTE:W], NOWHERE).then_inc(sem("pad_set"), 1)
            gp.memset(ones[:, :], 1.0)
            gp.memset(ident[:, :], 0.0).then_inc(sem("g0"), 1)
            gp.memset(zeroh[:, :], 0.0)
            gp.wait_ge(sem("g0"), 1)
            gp.affine_select(out=ident[:, :], in_=ident[:, :], compare_op=ALU.not_equal, fill=1.0, base=0,
                             pattern=[[-1, 128]], channel_multiplier=1).then_inc(sem("g0"), 1)
            gp.iota(thr[:, :], [[WIN, SEARCH]], base=0, channel_multiplier=WIN * GROUPS,
                    allow_small_or_imprecise_dtypes=True)
            gp.iota(iota_w[:, :], [[1, WIN * PITCH]], base=0, channel_multiplier=0,
                    allow_small_or_imprecise_dtypes=True)
            gp.iota(iota_lo[:, :], [[1, 128]], base=0, channel_multiplier=0, allow_small_or_imprecise_dtypes=True)
            gp.iota(iota_s[:, :, :], [[TB, WIN], [1, TB]], base=0, channel_multiplier=0,
                    allow_small_or_imprecise_dtypes=True)
            gp.iota(iota_t[:, :], [[1, TA]], base=0, channel_multiplier=0, allow_small_or_imprecise_dtypes=True)
            gp.wait_ge(sem("g0"), 2)
            gp.tensor_copy(identh[:, :], ident[:, :]).then_inc(sem("consts"), 1)
            gp.wait_ge(sem("rows_i"), 1)
            for g in range(SEARCH):
                gp.indirect_dma_start(cand[0:LO, g, :], None, dst.rearrange("(a n) -> a n", n=HLEN),
                                      bass.IndirectOffsetOnAxis(row_i[0:LO, g:g + 1], 0))\
                  .then_inc(sem("cand_in"), 16)
            gp.wait_ge(sem("runs_out"), 16)
            gp.wait_ge(sem("run_i"), 1)
            for g in range(GROUPS):
                gp.indirect_dma_start(runs[0:LO, g * EDGES_MAX:(g + 1) * EDGES_MAX], None, runs_d,
                                      bass.IndirectOffsetOnAxis(run_i[0:LO, g:g + 1], 0))\
                  .then_inc(sem("runs_in"), 16)

        def prepare_vector(v):
            ch = Chain(v, sem("v_prep"))
            P = slice(0, LO)
            v.memset(epst[:, :], EPS).then_inc(sem("eps_set"), 1)
            v.wait_ge(sem("heads_in"), 16)
            v.tensor_copy(heads[:, :], heads_i[:, :]).then_inc(sem("heads_f"), 1)
            v.wait_ge(sem("weights_in"), 160)
            v.tensor_tensor(sq[:, :], wm_sb[:, :], wm_sb[:, :], ALU.mult).then_inc(sem("squares"), 1)
            v.wait_ge(sem("consts"), 1)
            v.wait_ge(sem("heads_all"), 1)
            for g in range(SEARCH):
                ch.did(v.tensor_scalar(scr[:, :], psH[:, 0:HEADS], thr[:, g:g + 1], None, ALU.is_lt, ALU.add,
                                       accum_out=cnt[:, g:g + 1]))
                ch.wait()
            ch.did(v.tensor_scalar(row[:, :], cnt[:, :], -1.0, 0.0, ALU.add, ALU.max))
            ch.wait()
            v.tensor_copy(row_i[:, :], row[:, :]).then_inc(sem("rows_i"), 1)
            v.wait_ge(sem("edges_in"), 96)
            ch.did(v.tensor_scalar(ptmp[P, :], raw[P, 2, :], 0.0, float(TYPES - 1), ALU.max, ALU.min))
            ch.did(v.scalar_tensor_tensor(packed[P, :], raw[P, 1, :], SBITS, raw[P, 0, :],
                                          ALU.logical_shift_left, ALU.bitwise_or))
            ch.wait()
            v.scalar_tensor_tensor(packed[P, :], ptmp[P, :], SBITS + DBITS, packed[P, :],
                                   ALU.logical_shift_left, ALU.bitwise_or).then_inc(sem("packed"), 1)
            for k in range(XP):
                v.wait_ge(sem(f"x_in{k}"), 16)
                for b in range(k * XB, (k + 1) * XB):
                    ch.did(v.bn_stats(stats[P, b, :], x_sb[P, b, :]))
            ch.wait()
            for b in range(BLOCKS):
                last = v.bn_aggr(mv[P, b, :], stats[P, b, :])
            last.then_inc(sem("var0"), 1)
            v.wait_ge(sem("cand_in"), 16 * SEARCH)
            ch.did(v.tensor_tensor(below[P, :, :], cand[P, :, :], spread(thr[P, :], [LO, SEARCH, HLEN]), ALU.is_lt))
            ch.wait()
            ch.did(v.tensor_reduce(cnt[P, :], below[P, :, :], AX, ALU.add))
            ch.wait()
            ch.did(v.scalar_tensor_tensor(start[P, :], row[P, :], float(HLEN), cnt[P, :], ALU.mult, ALU.add))
            ch.wait()
            ch.did(v.tensor_scalar(run0[P, :], start[P, 0:GROUPS], 1.0 / SHIFT, 0.5 / SHIFT - 0.5, ALU.mult, ALU.add))
            ch.wait()
            ch.did(v.tensor_scalar(run0[P, :], run0[P, :], MAGIC, MAGIC, ALU.add, ALU.subtract))
            ch.wait()
            ch.did(v.tensor_scalar(run0[P, :], run0[P, :], float(RROWS - 1), None, ALU.min))
            ch.wait()
            v.tensor_copy(run_i[P, :], run0[P, :]).then_inc(sem("run_i"), 1)
            ch.did(v.scalar_tensor_tensor(need[P, :], run0[P, :], -float(SHIFT), start[P, 1:SEARCH], ALU.mult, ALU.add))
            ch.wait()
            ch.did(v.tensor_reduce(flags[P, 0:1], need[P, :], AX, ALU.max))
            ch.did(v.tensor_tensor(unsorted[P, :], raw[P, 1, 1:PARTE + 1], raw[P, 1, 0:PARTE], ALU.is_lt))
            ch.wait()
            ch.did(v.tensor_reduce(flags[P, 1:2], unsorted[P, :], AX, ALU.max))
            ch.wait()
            v.scalar_tensor_tensor(flags[P, 2:3], flags[P, 0:1], float(EDGES_MAX), flags[P, 1:2],
                                   ALU.is_gt, ALU.add).then_inc(sem("flags"), 1)
            v.wait_ge(sem("std0"), 1)
            ch.did(v.reciprocal(rstd[P, :], rstd[P, :]))
            ch.wait()
            v.scalar_tensor_tensor(nmr[P, :], mv[P, :, 0], -1.0, rstd[P, :], ALU.mult, ALU.mult).then_inc(sem("nmr0"), 1)
            ch.did(v.tensor_reduce(gtmp[:, :], emb_sb[:, :, :].rearrange("p t f -> p f t"), AX, ALU.max,
                                   apply_absolute_value=True))
            ch.did(v.scalar_tensor_tensor(sq[:, :], bm_sb[:, :], -1.0, bm_sb[:, :], ALU.mult, ALU.max))
            ch.wait()
            ch.did(v.tensor_tensor(gtmp[:, :], gtmp[:, :], sq[:, :], ALU.add))
            v.wait_ge(sem("wm_norm"), 1)
            ch.wait()
            ch.did(v.scalar_tensor_tensor(gsc[:, :], gsc[:, :], 11.4, gtmp[:, :], ALU.mult, ALU.add))
            ch.wait()
            ch.did(v.tensor_scalar(gsc[:, :], gsc[:, :], 1e-20, 1.0 / 32768, ALU.add, ALU.mult))
            ch.wait()
            ch.did(v.reciprocal(gsc[:, :], gsc[:, :]))
            ch.wait()
            ch.did(v.tensor_tensor(wm_sb[:, :], wm_sb[:, :], gsc[:, :], ALU.mult))
            ch.did(v.tensor_tensor(bm_sb[:, :], bm_sb[:, :], gsc[:, :], ALU.mult))
            ch.did(v.tensor_tensor(embs[:, :], embs[:, :], gsc[0:TYPES, :], ALU.mult))
            ch.did(v.tensor_tensor(bg[:, :], bg_i[:, 0:2], bg_h[:, 0:2], ALU.add))
            ch.wait()
            ch.did(v.tensor_copy(embh[:, 0, :], embs[:, :]))
            ch.wait()
            v.tensor_tensor(embh[:, 1, :], embs[:, :], embh[:, 0, :], ALU.subtract).then_inc(sem("scaled"), 1)
            v.wait_ge(sem("g_col"), 1)
            ch.did(v.reciprocal(ginv[:, :], psH[:, 0:1]))
            v.wait_ge(sem("flag_sum"), 1)
            v.tensor_scalar(flag_i[:, :], ps[0:1, 6, 0:1], 0.0, None, ALU.is_gt).then_inc(sem("flag_set"), 1)
            v.wait_ge(sem("runs_in"), 16 * GROUPS)
            ch.wait()
            ch.did(v.tensor_scalar(ui[0][P, :], runs[P, :], SMASK, None, ALU.bitwise_and))
            ch.did(v.tensor_scalar(ui[1][P, :], runs[P, :], SBITS, SMASK, ALU.logical_shift_right, ALU.bitwise_and))
            ch.did(v.tensor_scalar(ui[2][P, :], runs[P, :], SBITS + DBITS, None, ALU.logical_shift_right))
            ch.wait()
            block_of(v, ch, uf[3][P, :], ui[0][P, :])
            v.scalar_tensor_tensor(fields[P, 0, :], uf[3][P, :], -float(LO), ui[0][P, :], ALU.mult, ALU.add)\
             .then_inc(sem("fields"), 1)
            group = lambda a: a.rearrange("p (g n) -> p g n", g=GROUPS)
            ch.did(v.tensor_tensor(group(uf[4][P, :]), group(ui[1][P, :]),
                                   spread(thr[P, 0:GROUPS], [LO, GROUPS, EDGES_MAX]), ALU.subtract))
            v.wait_ge(sem("fields"), 1)
            ch.wait()
            ch.did(v.scalar_tensor_tensor(uf[0][P, :], uf[4][P, :], float(PITCH), uf[3][P, :], ALU.mult, ALU.add))
            ch.wait()
            v.tensor_scalar(fields[P, 1, :], uf[0][P, :], -1.0, 1000.0, ALU.max, ALU.min).then_inc(sem("fields"), 1)
            ch.did(v.tensor_scalar(uf[1][P, :], ui[2][P, :], float(TB), None, ALU.is_ge))
            ch.wait()
            v.scalar_tensor_tensor(fields[P, 2, :], ui[2][P, :], float(2 * TB), uf[1][P, :], ALU.is_ge, ALU.add)\
             .then_inc(sem("fields"), 1)
            v.wait_ge(sem("fields"), 3)
            ch.did(v.scalar_tensor_tensor(uf[1][P, :], fields[P, 2, :], -float(TB), ui[2][P, :], ALU.mult, ALU.add))
            ch.wait()
            ch.did(v.scalar_tensor_tensor(uf[0][P, :], uf[4][P, :], float(TB), uf[1][P, :], ALU.mult, ALU.add))
            ch.wait()
            v.tensor_scalar(fields[P, 3, :], uf[0][P, :], -1.0, 1000.0, ALU.max, ALU.min).then_inc(sem("fields"), 1)
            meta_copies(v, 0)

        def block_of(v, ch, q, s):
            ch.did(v.tensor_scalar(q, s, 1.0 / LO, 0.5 / LO - 0.5, ALU.mult, ALU.add))
            ch.wait()
            ch.did(v.tensor_scalar(q, q, MAGIC, MAGIC, ALU.add, ALU.subtract))
            ch.wait()


        def blocks(n):
            return bass.ds(CB * n, CB) if not isinstance(n, int) else slice(CB * n, CB * n + CB)

        def nodes(n):
            return bass.ds(CH * n, CH) if not isinstance(n, int) else slice(CH * n, CH * n + CH)

        def post0_tensor(pe, n, t):
            if t == 0:
                positive(pe, sem("x1"), n)
                pe.wait_ge(sem("aggr"), n + 1)
                for j in range(CB):
                    last = pe.matmul(psX[:, j, :], aggr[:, LO * j:LO * (j + 1)], w0_sb[:, :], start=True, stop=True)
                last.then_inc(sem("psX"), 1)
            if t == 1:
                positive(pe, sem("hst"), n)
                pe.wait_ge(sem("h1"), n + 1)
                for j in range(CB):
                    last = pe.transpose(psT[:, LO * j:LO * (j + 1)], h1s[0:LO, j, :], ident[0:LO, 0:LO])
                last.then_inc(sem("psT"), 1)
            if t == 2:
                positive(pe, sem("tbs"), n)
                pe.wait_ge(sem("hst"), n + 1)
                for j in range(CB):
                    last = pe.matmul(psM[:, j, :], hst[:, LO * j:LO * (j + 1)], wm_sb[:, :], start=True, stop=True)
                last.then_inc(sem("psM"), 1)

        def post0_scalar(act, n, par, summed, split):
            P = slice(0, LO)
            summed(act, n)
            positive(act, sem("psX"), n)
            act.activation(aggr[:, :], psD[par], ACT.Relu, scale=1.0 / HSCALE).then_inc(sem("aggr"), 1)
            act.wait_ge(sem("pvar"), n + 1)
            act.activation(prs[P, :], pmv[P, :, 1], ACT.Sqrt, bias=epst[P, :]).then_inc(sem("pstd"), 1)
            act.wait_ge(sem("pnm"), n + 1)
            positive(act, sem("psT"), n)
            for j in range(CB):
                last = act.activation(h1s[P, j, :], x1s[P, j, :], ACT.Relu, bias=pnm[P, j:j + 1],
                                      scale=prs[P, j:j + 1])
            last.then_inc(sem("h1"), 1)
            act.wait_ge(sem("psT"), n + 1)
            positive(act, sem("psM"), n)
            positive(act, sem("h1T"), n)
            act.activation(hst[:, :], psT, ACT.Copy).then_inc(sem("hst"), 1)
            if split:
                act.wait_ge(sem("tbs"), n + 1)
                act.activation(tabv[1][P, blocks(n), 0, :], tbs[P, :, :], ACT.Copy).then_inc(sem("tab_hi"), 1)

        def post0_gpsimd(gp, n, split):
            gp.wait_ge(sem("x1"), n + 1)
            gp.tensor_copy(x_sb[0:LO, blocks(n), :], x1s[0:LO, :, :]).then_inc(sem("x1_kept"), 1)
            gp.wait_ge(sem("hst"), n + 1)
            gp.tensor_copy(h1T[:, nodes(n)], hst[:, :]).then_inc(sem("h1T"), 1)
            if split:
                gp.wait_ge(sem("tab_hi"), n + 1)
                gp.tensor_tensor(tabv[1][0:LO, blocks(n), 1, :], tbs[0:LO, :, :], tabv[1][0:LO, blocks(n), 0, :],
                                 ALU.subtract).then_inc(sem("tab_lo"), 1)

        def post0_vector(v, n, ch, spent):
            P = slice(0, LO)
            v.wait_ge(sem("psX"), n + 1)
            positive(v, sem("h1"), n)
            positive(v, sem("x1_kept"), n)
            v.tensor_tensor(x1s[P, :, :], psX, x_sb[P, blocks(n), :], ALU.add).then_inc(sem("x1"), 1)
            v.wait_ge(sem("x1"), n + 1)
            for j in range(CB):
                ch.did(v.bn_stats(pst[P, j, :], x1s[P, j, :]))
            ch.wait()
            ch.did(v.tensor_tensor(pmv[P, :, 0], pst[P, :, 1], pst[P, :, 4], ALU.add))
            ch.did(v.tensor_tensor(pmv[P, :, 1], pst[P, :, 1], pst[P, :, 4], ALU.subtract))
            ch.did(v.tensor_tensor(pm2[P, :], pst[P, :, 2], pst[P, :, 5], ALU.add))
            ch.wait()
            ch.did(v.scalar_tensor_tensor(pmv[P, :, 1], pmv[P, :, 1], 0.25, pmv[P, :, 1], ALU.mult, ALU.mult))
            ch.wait()
            v.scalar_tensor_tensor(pmv[P, :, 1], pm2[P, :], 1.0 / D, pmv[P, :, 1], ALU.mult, ALU.add)\
             .then_inc(sem("pvar"), 1)
            v.wait_ge(sem("pstd"), n + 1)
            ch.did(v.reciprocal(prs[P, :], prs[P, :]))
            ch.wait()
            v.scalar_tensor_tensor(pnm[P, :], pmv[P, :, 0], -0.5, prs[P, :], ALU.mult, ALU.mult).then_inc(sem("pnm"), 1)
            v.wait_ge(sem("psM"), n + 1)
            spent(n)
            v.tensor_tensor(tbs[P, :, :], psM, bm_sb[P, :].unsqueeze(1).broadcast_to([LO, CB, D]), ALU.add)\
             .then_inc(sem("tbs"), 1)

        def post1_tensor(pe, n, t):
            if t == 0:
                pe.wait_ge(sem("msg"), n + 1)
                positive(pe, sem("rz"), n)
                positive(pe, sem("nin"), n)
                for a in range(2):
                    w = slice(D * a, D * (a + 1))
                    pe.matmul(psRZ[:, a, :], wih_sb[:, w], msgs[:, :], start=True, stop=False)
                    last = pe.matmul(psRZ[:, a, :], whh_sb[:, w], h1T[:, nodes(n)], start=False, stop=True)
                last.then_inc(sem("psRZ"), 1)
                w = slice(2 * D, 3 * D)
                pe.matmul(psN[:, 0, :], wih_sb[:, w], msgs[:, :], start=True, stop=True)
                pe.matmul(psN[:, 1, :], whh_sb[:, w], h1T[:, nodes(n)], start=True, stop=True).then_inc(sem("psN"), 1)
            if t == 1:
                pe.wait_ge(sem("hnew"), n + 1)
                positive(pe, sem("result"), n)
                for j in range(CB):
                    last = pe.transpose(psO[:, j, :], hnew[:, LO * j:LO * (j + 1)], ident[:, :])
                last.then_inc(sem("psO"), 1)

        def post1_scalar(act, n, par, summed):
            summed(act, n)
            positive(act, sem("psN"), n)
            act.activation(msgs[:, :], psD[par], ACT.Copy, scale=ginv[:, 0:1]).then_inc(sem("msg"), 1)
            act.wait_ge(sem("psRZ"), n + 1)
            positive(act, sem("hnew"), n)
            for a in range(2):
                last = act.activation(rz[:, a, :], psRZ[:, a, :], ACT.Sigmoid, bias=bg[:, a:a + 1])
            last.then_inc(sem("rz"), 1)
            act.wait_ge(sem("nin"), n + 1)
            act.activation(nn[:, :], nin[:, :], ACT.Tanh, bias=bg_i[:, 2:3]).then_inc(sem("nn"), 1)

        def post1_vector(v, n, ch):
            v.wait_ge(sem("psN"), n + 1)
            v.wait_ge(sem("rz"), n + 1)
            ch.did(v.scalar_tensor_tensor(nin[:, :], psN[:, 1, :], bg_h[:, 2:3], rz[:, 0, :], ALU.add, ALU.mult))
            ch.wait()
            v.tensor_tensor(nin[:, :], nin[:, :], psN[:, 0, :], ALU.add).then_inc(sem("nin"), 1)
            v.wait_ge(sem("nn"), n + 1)
            positive(v, sem("psO"), n)
            ch.did(v.tensor_tensor(hnew[:, :], h1T[:, nodes(n)], nn[:, :], ALU.subtract))
            ch.wait()
            ch.did(v.tensor_tensor(hnew[:, :], rz[:, 1, :], hnew[:, :], ALU.mult))
            ch.wait()
            v.tensor_tensor(hnew[:, :], nn[:, :], hnew[:, :], ALU.add).then_inc(sem("hnew"), 1)
            v.wait_ge(sem("psO"), n + 1)
            v.tensor_tensor(x_sb[0:LO, blocks(n), :], psO, x_sb[0:LO, blocks(n), :], ALU.add).then_inc(sem("result"), 1)

        def store_result(sp, n):
            sp.wait_ge(sem("result"), n + 1)
            sp.dma_start(out_v[:, blocks(n), :], x_sb[0:LO, blocks(n), :]).then_inc(sem("out"), 16)


        def norm_vector(v, ch, reduced):
            reduced()
            ch.wait()
            P = slice(0, LO)
            v.tensor_scalar(deg[P, :], deg[P, :], 1.0, None, ALU.max).then_inc(sem("deg"), 1)
            v.wait_ge(sem("deg_root"), 1)
            ch.did(v.reciprocal(norm[P, :], norm[P, :]))
            ch.wait()
            ch.did(v.tensor_scalar(norm[P, :], norm[P, :], HSCALE, None, ALU.mult))
            ch.wait()

        def norm_scalar(act):
            act.wait_ge(sem("deg"), 1)
            act.activation(norm[0:LO, :], deg[0:LO, :], ACT.Sqrt).then_inc(sem("deg_root"), 1)

        def build_tensor(pe, c, par):
            for i in range(PAIRS):
                b, k0 = divmod(i * 2 * HALVES, BATCH)
                slot = (par + b) % 2
                if k0 == 0:
                    pe.wait_ge(sem("onehot"), BATCHES * c + b + 1)
                positive(pe, sem("evac"), PAIRS * c + (i - 2 if i >= 3 else i - 3 if i else 0))
                for w in range(2):
                    for half in range(HALVES):
                        k = k0 + HALVES * w + half
                        cols = combo[:, slot, k, :].rearrange("p (d h) -> p d h", h=PITCH)[:, :, 0:SLOTS]
                        last = pe.matmul(ps[:, 2 * (i % PSLOTS) + w, 0:WCOLS], lohot[:, slot, k, :], cols,
                                         start=half == 0, stop=half == HALVES - 1)
                last.then_inc(sem("built"), 1)
                if not (isinstance(c, int) and c == 0):
                    degree_tensor(pe, 1 - par, i)

        def degree_tensor(pe, par, j):
            last = pe.matmul(psDeg, identh[:, :], adj[par][:, 0:BLOCKS, 10 * j:10 * j + 10], start=False, stop=False,
                             skip_group_check=True)
            if j == PAIRS - 1:
                last.then_inc(sem("degree"), 1)

        def build_scalar(act, c, par):
            for i in range(PAIRS):
                act.wait_ge(sem("built"), PAIRS * c + i + 1)
                if i == 0:
                    positive(act, sem("degree"), c - 1)
                    if not (isinstance(c, int) and c == 0):
                        if par:
                            positive(act, sem("adj_out1"), 8 * (c - 1))
                        else:
                            act.wait_ge(sem("adj_out0"), 8 * c)
                s = 2 * (i % PSLOTS)
                act.activation(adj[par][:, :, 10 * i:10 * i + 10].rearrange("p h (w d) -> p h w d", d=WIN),
                               ps[:, s:s + 2, 0:WCOLS].rearrange("p w (d h) -> p h w d", h=SLOTS),
                               ACT.Copy).then_inc(sem("evac"), 1)

        def build_gpsimd(gp, c, par):
            positive(gp, sem("onehot"), BATCHES * (c - 1))
            at = bass.ds(CHT * c, CHT) if not isinstance(c, int) else slice(CHT * c, CHT * c + CHT)
            for k in range(2):
                gp.tensor_copy(mch[:, par, k, :, :], spread(meta[:, k, at], [128, CHT, 2]))
            gp.tensor_copy(mch_s[:, par, :, :], meta[:, 2:4, at]).then_inc(sem("mch"), 1)

        def build_vector(v, c, par, ch):
            for b in range(BATCHES):
                slot = (par + b) % 2
                if b == 0:
                    v.wait_ge(sem("mch"), c + 1)
                positive(v, sem("built"), PAIRS * c + 5 * b - 5)
                at = slice(BATCH * b, BATCH * (b + 1))
                def hot(o, iota, k):
                    n = o.shape[-1] // 2
                    ch.did(v.tensor_tensor(o.rearrange("p k (n t) -> p k n t", t=2),
                                           iota.rearrange("p (n t) -> p n t", t=2).unsqueeze(1)
                                               .broadcast_to([128, BATCH, n, 2]),
                                           mch[:, par, k, at, :].unsqueeze(2).broadcast_to([128, BATCH, n, 2]),
                                           ALU.is_equal))
                hot(lohot[:, slot, :, :], iota_lo[:, :], 0)
                hot(combo[:, slot, :, :], iota_w[:, :], 1)
                ch.wait()
                v.tensor_tensor(lohot[:, slot, :, LO:128], iota_t[:, :].unsqueeze(1).broadcast_to([128, BATCH, TA]),
                                spread(mch_s[:, par, 0, at], [128, BATCH, TA]), ALU.is_equal)
                v.tensor_tensor(
                    combo[:, slot, :, :].rearrange("p k (d h) -> p k d h", h=PITCH)[:, :, :, BLOCKS:SLOTS],
                    iota_s[:, :, :].unsqueeze(1).broadcast_to([128, BATCH, WIN, TB]),
                    mch_s[:, par, 1, at].unsqueeze(2).unsqueeze(3).broadcast_to([128, BATCH, WIN, TB]),
                    ALU.is_equal).then_inc(sem("onehot"), 1)

        def build_sync(sp, c, par):
            sp.wait_ge(sem("evac"), PAIRS * (c + 1))
            at = slice(c, c + 1) if isinstance(c, int) else bass.ds(c, 1)
            sp.dma_start(adj_d[at, :, :].rearrange("a p n -> (a p) n"), ring[:, par, :]).then_inc(sem(f"adj_out{par}"), 16)

        def load_sync(sp, L, c, par):
            at = slice(c, c + 1) if isinstance(c, int) else bass.ds(c, 1)
            for j, (a, b) in enumerate((PARTS0, PARTS)[L]):
                positive(sp, sem(f"used{L}"), 4 * (c - 2) + j + 1)
                sp.dma_start(ring[:, par, a * CH:b * CH],
                             adj_d[at, :, a * CH:b * CH].rearrange("a p n -> (a p) n"))\
                  .then_inc(sem(f"load{L}_{par}_{j}"), 16)

        def product_tensor(pe, L, c, par, between):
            parts = (PARTS0, PARTS)[L]
            for j, (a, b) in enumerate(parts):
                pe.wait_ge(sem(f"load{L}_{par}_{j}"), 8 * c + 8 + 8 * (1 - par))
                for h in range(a, b):
                    for s in range(2):
                        last = pe.matmul(psD[par], tabv[L][:, h, s, :], adj[par][:, h, :],
                                         start=h == 0 and s == 0, stop=h == parts[-1][1] - 1 and s == 1)
                last.then_inc(sem(f"used{L}"), 1)
                between(j)

        fast_summed = [lambda eng, n: eng.wait_ge(sem("used0"), 4 * n + 4),
                       lambda eng, n: eng.wait_ge(sem("used1"), 4 * n + 4)]

        def build_all_tensor(pe):
            pe.matmul(psDeg, zeroh[:, 0:128], zeroh[:, 0:BLOCKS * 10], start=True, stop=False, skip_group_check=True)
            pe.wait_ge(sem("meta_act"), META_K // 2)
            pe.wait_ge(sem("meta_dve"), META_K // 2)
            over_chunks(pe, lambda c, par: build_tensor(pe, c, par), first=3)
            pe.wait_ge(sem("evac"), PAIRS * CHUNKS)
            for j in range(PAIRS):
                degree_tensor(pe, 0, j)
            pe.matmul(psDeg, zeroh[:, 0:128], zeroh[:, 0:BLOCKS * 10], start=False, stop=True, skip_group_check=True)\
              .then_inc(sem("degrees"), 1)

        def fast_tensor(pe):
            for L, post, steps in ((0, post0_tensor, 3), (1, post1_tensor, 2)):
                if L == 0:
                    pe.wait_ge(sem("tab0"), BLOCKS)
                else:
                    pe.wait_ge(sem("tab_lo"), CHUNKS)
                    pe.wait_ge(sem("emb_in"), 16 * TA)

                def body(c, par):
                    def between(j):
                        if not (isinstance(c, int) and c == 0):
                            t = {0: 0, 1: 1, 2: 2} if steps == 3 else {1: 0, 3: 1}
                            if j in t:
                                post(pe, c - 1, t[j])
                    product_tensor(pe, L, c, par, between)

                over_chunks(pe, body)
                for t in range(steps):
                    post(pe, CHUNKS - 1, t)

        def fast_scalar(act):
            norm_scalar(act)
            act.wait_ge(sem("tab0_zero"), 1)
            act.wait_ge(sem("norm"), 1)
            for b in range(BLOCKS):
                act.activation(tabv[0][0:LO, b, 0, :], h0[0:LO, b, :], ACT.Copy, scale=norm[0:LO, b:b + 1])\
                   .then_inc(sem("tab0_hi"), 1)
            over_chunks(act, lambda c, par: post0_scalar(act, c, par, fast_summed[0], True))
            over_chunks(act, lambda c, par: post1_scalar(act, c, par, fast_summed[1]))

        def build_all_gpsimd(gp):
            gp.wait_ge(sem("meta_act"), META_K // 2)
            gp.wait_ge(sem("meta_dve"), META_K // 2)
            over_chunks(gp, lambda c, par: build_gpsimd(gp, c, par), first=3)
            gp.wait_ge(sem("h0_done"), 1)
            for k in range(XP):
                v = x_sb[0:LO, k * XB:(k + 1) * XB, :]
                last = gp.tensor_tensor(v, v, b0_sb[0:LO, :].unsqueeze(1).broadcast_to([LO, XB, D]), ALU.add)
            last.then_inc(sem("x_b"), 1)

        def fast_gpsimd(gp):
            gp.wait_ge(sem("turned"), META_K)
            gp.memset(tab[0][:, :].bitcast(I32), 0).then_inc(sem("tab0_zero"), 1)
            gp.wait_ge(sem("mch"), CHUNKS)
            gp.memset(tab[1][:, :].bitcast(I32), 0).then_inc(sem("tab1_zero"), 1)
            gp.wait_ge(sem("tab1_zero"), 1)
            over_chunks(gp, lambda c, par: post0_gpsimd(gp, c, True))

        def fast_vector(v):
            ch = Chain(v, sem("v_fast"))
            def reduced():
                v.wait_ge(sem("degrees"), 1)
                ch.did(v.tensor_reduce(deg[:, :], psDeg.rearrange("p (h n) -> p h n", n=10), AX, ALU.add))
            norm_vector(v, ch, reduced)
            v.memset(nmr[:, :], 0.0).then_inc(sem("norm"), 1)
            v.wait_ge(sem("tab0_zero"), 1)
            for b in range(BLOCKS):
                v.wait_ge(sem("tab0_hi"), b + 1)
                v.scalar_tensor_tensor(tabv[0][0:LO, b, 1, :], h0[0:LO, b, :], norm[0:LO, b:b + 1],
                                       tabv[0][0:LO, b, 0, :], ALU.mult, ALU.subtract).then_inc(sem("tab0"), 1)
            v.wait_ge(sem("x_b"), 1)
            spent = lambda n: positive(v, sem("tab_lo"), n)
            over_chunks(v, lambda c, par: post0_vector(v, c, ch, spent), ch, 7)
            over_chunks(v, lambda c, par: post1_vector(v, c, ch), ch, 3)

        def fast_sync(sp):
            sp.wait_ge(sem("tab1_zero"), 1)
            sp.wait_ge(sem("scaled"), 1)
            for k in range(TA):
                sp.dma_start(tabv[1][LO + k:LO + k + 1, BLOCKS:SLOTS, :, :],
                             embh[TB * k:TB * (k + 1), :, :]).then_inc(sem("emb_in"), 16)
            sp.wait_ge(sem("adj_out0"), 16 * ((CHUNKS + 1) // 2))
            sp.wait_ge(sem("adj_out1"), 16 * (CHUNKS // 2))
            sp.wait_ge(sem("degrees"), 1)
            over_chunks(sp, lambda c, par: load_sync(sp, 0, c, par), first=3)
            sp.wait_ge(sem("used0"), 4 * CHUNKS)
            over_chunks(sp, lambda c, par: load_sync(sp, 1, c, par), first=3)
            over_chunks(sp, lambda c, par: store_result(sp, c))
            sp.wait_ge(sem("emb_in"), 16 * TA)
            sp.wait_ge(sem("out"), 16 * CHUNKS)


        def general_sync(sp):
            sp.wait_ge(sem("adj_out0"), 16 * ((CHUNKS + 1) // 2))
            sp.wait_ge(sem("adj_out1"), 16 * (CHUNKS // 2))
            sp.wait_ge(sem("degrees"), 1)
            for k, a in enumerate((src, dst, typ)):
                sp.dma_start(flat_i[0:LO, k, :], a.rearrange("(p n) -> p n", p=LO)).then_inc(sem("flat_in"), 16)
            sp.wait_ge(sem("tab_zero"), 1)
            zero = tab[0][0:LO, :].bitcast(F32)[:, 0:(N + LO) // LO * D]
            for k in range(2):
                sp.dma_start(sum_d[k].rearrange("(p r) f -> p (r f)", p=LO), zero).then_inc(sem("sum_zero"), 16)
            sp.wait_ge(sem("scaled"), 1)
            sp.dma_start(emb_d, embs[:, :]).then_inc(sem("gemb_out"), 16)
            sp.wait_ge(sem("h0_scaled"), 1)
            sp.dma_start(table_v, h0[0:LO, :, :]).then_inc(sem("table_out"), 16)

            def sums_in(L, n):
                positive(sp, sem(f"gturned{L}"), n)
                sp.dma_start(sum_in[0:LO, :, :], sum_v[L][:, blocks(n), :]).then_inc(sem(f"sum_in{L}"), 16)

            def body0(n, par):
                sums_in(0, n)
                sp.wait_ge(sem("tbs"), n + 1)
                sp.dma_start(table_v[:, blocks(n), :], tbs[0:LO, :, :]).then_inc(sem("table1_out"), 16)

            sp.wait_ge(sem("gadded0"), 16 * PARTE)
            over_chunks(sp, body0)
            sp.wait_ge(sem("gadded1"), 16 * PARTE)

            def body1(n, par):
                sums_in(1, n)
                store_result(sp, n)

            over_chunks(sp, body1)
            sp.wait_ge(sem("out"), 16 * CHUNKS)

        def general_scalar(act):
            norm_scalar(act)
            done = lambda L: lambda eng, n: eng.wait_ge(sem(f"gturned{L}"), n + 1)
            over_chunks(act, lambda n, par: post0_scalar(act, n, par, done(0), False))
            over_chunks(act, lambda n, par: post1_scalar(act, n, par, done(1)))

        def general_gpsimd(gp):
            gp.wait_ge(sem("degrees"), 1)
            gp.memset(before[:, :], 1.0).then_inc(sem("g1"), 1)
            gp.memset(tab[0][:, :].bitcast(I32), 0).then_inc(sem("tab_zero"), 1)
            gp.wait_ge(sem("g1"), 1)
            gp.affine_select(out=before[:, :], in_=before[:, :], compare_op=ALU.is_gt, fill=0.0, base=0,
                             pattern=[[-1, 128]], channel_multiplier=1)
            gp.iota(trash_c, [[1, 1]], base=N, channel_multiplier=1,
                    allow_small_or_imprecise_dtypes=True).then_inc(sem("g1"), 1)
            gp.wait_ge(sem("sum_zero"), 32)
            gp.wait_ge(sem("gemb_out"), 16)
            for L in range(2):
                if L:
                    gp.wait_ge(sem("table1_out"), 16 * CHUNKS)
                else:
                    gp.wait_ge(sem("table_out"), 16)

                def tile(t):
                    gp.wait_ge(sem(f"gindex{L}"), t + 1)
                    gp.sem_inc(sem("g_seen"), 1)
                    gp.indirect_dma_start(rows_in[0:NE, :], None, table_d,
                                          bass.IndirectOffsetOnAxis(isrc[0:NE, :], 0)).then_inc(sem(f"grows{L}"), 16)
                    if L:
                        gp.indirect_dma_start(erows_in[0:NE, :], None, emb_d,
                                              bass.IndirectOffsetOnAxis(itype[0:NE, :], 0)).then_inc(sem("gerows"), 16)
                    gp.wait_ge(sem(f"gsums{L}"), t + 1)
                    gp.sem_inc(sem("g_seen"), 1)
                    gp.indirect_dma_start(sum_d[L], bass.IndirectOffsetOnAxis(idst[0:NE, :], 0),
                                          sums[0:NE, :], None, compute_op=ALU.add).then_inc(sem(f"gadded{L}"), 16)

                over_tiles(gp, tile)
                if L == 0:
                    over_chunks(gp, lambda n, par: post0_gpsimd(gp, n, False))

        def general_vector(v):
            ch = Chain(v, sem("v_general"))
            P = slice(0, LO)
            v.wait_ge(sem("flat_in"), 48)
            v.wait_ge(sem("g1"), 2)
            ch.did(v.tensor_copy(src_f[P, :], flat_i[P, 0, :]))
            ch.did(v.tensor_copy(dst_f[P, :], flat_i[P, 1, :]))
            ch.did(v.tensor_scalar(flat_i[P, 2, :], flat_i[P, 2, :], 0.0, float(TYPES - 1), ALU.max, ALU.min))
            ch.wait()
            block_of(v, ch, q_f[P, :], src_f[P, :])
            ch.did(v.scalar_tensor_tensor(lo_f[P, :], q_f[P, :], -float(LO), src_f[P, :], ALU.mult, ALU.add))
            ch.wait()
            with v.Fori(0, PARTE) as t:
                at = bass.ds(t, 1)
                v.wait_ge(sem("ghist"), t + 1)
                v.tensor_scalar(ghot[P, 0:LO], iota_lo[P, 0:LO], lo_f[P, at], None, ALU.is_equal)
                v.tensor_scalar(ghot[P, 128:128 + BLOCKS], iota_lo[P, 0:BLOCKS], q_f[P, at], None, ALU.is_equal)\
                 .then_inc(sem("ghot"), 1)

            def reduced():
                v.wait_ge(sem("ghist"), PARTE + 2)
                ch.did(v.tensor_copy(deg[P, :], psDeg[P, 0:BLOCKS]))
            norm_vector(v, ch, reduced)
            v.wait_ge(sem("h0_done"), 1)
            v.tensor_tensor(h0[P, :, :], h0[P, :, :], spread(norm[P, :], [LO, BLOCKS, D]), ALU.mult)\
             .then_inc(sem("h0_scaled"), 1)
            v.wait_ge(sem("x_b"), 1)
            for L in range(2):
                def tile(t):
                    at = bass.ds(t, 1) if not isinstance(t, int) else slice(t, t + 1)
                    positive(v, sem(f"gadded{L}"), 16 * t)
                    v.tensor_copy(itype[P, :], flat_i[P, 2, at])
                    v.tensor_copy(isrc[P, :], flat_i[P, 0, at]).then_inc(sem(f"gindex{L}"), 1)
                    v.tensor_scalar(diag[P, 0:NE], ident[P, 0:NE], dst_f[P, at], None, ALU.mult)\
                     .then_inc(sem(f"gdiag{L}"), 1)
                    v.wait_ge(sem(f"gacross{L}"), t + 1)
                    v.tensor_scalar(same[P, 0:NE], psB[P, 0:NE], dst_f[P, at], None, ALU.is_equal)\
                     .then_inc(sem(f"gsame{L}"), 1)
                    v.wait_ge(sem(f"gsame{L}"), t + 1)
                    ch.did(v.tensor_tensor(lower[P, 0:NE], same[P, 0:NE], before[P, 0:NE], ALU.mult))
                    ch.wait()
                    ch.did(v.tensor_reduce(count_c[P, :], lower[P, 0:NE], AX, ALU.max))
                    ch.did(v.tensor_tensor(toward_c[P, :], trash_c[P, :], dst_f[P, at], ALU.subtract))
                    ch.wait()
                    ch.did(v.tensor_tensor(dup_c[P, :], toward_c[P, :], count_c[P, :], ALU.mult))
                    ch.wait()
                    ch.did(v.tensor_tensor(idst[P, :], dup_c[P, :], dst_f[P, at], ALU.add))
                    v.wait_ge(sem(f"gproduct{L}"), t + 1)
                    ch.wait()
                    v.tensor_copy(sums[P, :], psS[P, :]).then_inc(sem(f"gsums{L}"), 1)

                over_tiles(v, tile, ch, 5)
                if L:
                    v.wait_ge(sem("h1T"), CHUNKS)
                if L == 0:
                    spent = lambda n: positive(v, sem("table1_out"), 16 * n)
                    over_chunks(v, lambda n, par: post0_vector(v, n, ch, spent), ch, 7)
                else:
                    over_chunks(v, lambda n, par: post1_vector(v, n, ch), ch, 3)

        def general_tensor(pe):
            psHist = ps[0:LO, 6, 0:BLOCKS]
            pe.matmul(psHist, zeroh[0:LO, 0:LO], zeroh[0:LO, 0:BLOCKS], start=True, stop=False,
                      skip_group_check=True).then_inc(sem("ghist"), 1)
            with pe.Fori(0, PARTE) as t:
                pe.wait_ge(sem("ghot"), t + 1)
                pe.matmul(psHist, ghot[0:LO, 0:LO], ghot[0:LO, 128:128 + BLOCKS], start=False, stop=False,
                          skip_group_check=True).then_inc(sem("ghist"), 1)
            pe.matmul(psHist, zeroh[0:LO, 0:LO], zeroh[0:LO, 0:BLOCKS], start=False, stop=True,
                      skip_group_check=True).then_inc(sem("ghist"), 1)
            for L, post, steps in ((0, post0_tensor, 3), (1, post1_tensor, 2)):
                def tile(t):
                    pe.wait_ge(sem(f"gdiag{L}"), t + 1)
                    pe.matmul(psB[0:NE, 0:NE], ones[0:NE, 0:NE], diag[0:NE, 0:NE], start=True, stop=True)\
                      .then_inc(sem(f"gacross{L}"), 1)
                    pe.wait_ge(sem(f"gsame{L}"), t + 1)
                    pe.wait_ge(sem(f"grows{L}"), 16 * t + 16)
                    last = pe.matmul(psS[0:NE, :], same[0:NE, 0:NE], rows_in[0:NE, :], start=True, stop=L == 0)
                    if L:
                        pe.wait_ge(sem("gerows"), 16 * t + 16)
                        last = pe.matmul(psS[0:NE, :], same[0:NE, 0:NE], erows_in[0:NE, :], start=False, stop=True)
                    last.then_inc(sem(f"gproduct{L}"), 1)

                over_tiles(pe, tile)

                if L:
                    pe.wait_ge(sem("h1T"), CHUNKS)

                def body(n, par):
                    pe.wait_ge(sem(f"sum_in{L}"), 16 * n + 16)
                    for j in range(CB):
                        last = pe.transpose(psD[par][:, LO * j:LO * (j + 1)], sum_in[0:LO, j, :], ident[0:LO, 0:LO])
                    last.then_inc(sem(f"gturned{L}"), 1)
                    for k in range(steps):
                        post(pe, n, k)

                over_chunks(pe, body)

        block = ctx.enter_context(nc.Block())

        def branch(eng, fast, general):
            eng.wait_ge(sem("flag_set"), 1)
            flag = eng.value_load(flag_i[0:1, 0:1], min_val=0, max_val=1)
            with eng.If(flag == 0):
                fast(eng)
            with eng.Else():
                general(eng)

        @block.sync
        def _(sp):
            prepare_sync(sp)
            over_chunks(sp, lambda c, par: build_sync(sp, c, par), first=3)
            branch(sp, fast_sync, general_sync)

        @block.scalar
        def _(act):
            prepare_scalar(act)
            over_chunks(act, lambda c, par: build_scalar(act, c, par), first=3)
            branch(act, fast_scalar, general_scalar)

        @block.gpsimd
        def _(gp):
            prepare_gpsimd(gp)
            build_all_gpsimd(gp)
            branch(gp, fast_gpsimd, general_gpsimd)

        @block.vector
        def _(v):
            prepare_vector(v)
            v.wait_ge(sem("meta_act"), META_K // 2)
            ch = Chain(v, sem("v_build"))
            over_chunks(v, lambda c, par: build_vector(v, c, par, ch), ch, 2 * BATCHES, first=3)
            branch(v, fast_vector, general_vector)

        @block.tensor
        def _(pe):
            prepare_tensor(pe)
            build_all_tensor(pe)
            branch(pe, fast_tensor, general_tensor)


def kernel(x, src, dst, edge_type_9, L0_gnn_W, L0_gnn_b, L1_gnn_W_msg, L1_gnn_b_msg, L1_gnn_edge_embed,
           L1_gnn_W_ih, L1_gnn_W_hh, L1_gnn_b_ih, L1_gnn_b_hh):
    import concourse.bacc as bacc
    from concourse.bass_utils import run_bass_kernel_spmd

    turned = lambda a: np.ascontiguousarray(np.asarray(a).T)
    by_gate = lambda a: np.ascontiguousarray(np.asarray(a).reshape(3, D).T)
    arrays = {
        "x": np.asarray(x), "src": np.asarray(src), "dst": np.asarray(dst), "typ": np.asarray(edge_type_9),
        "w0t": turned(L0_gnn_W), "b0": np.asarray(L0_gnn_b), "wmt": turned(L1_gnn_W_msg),
        "bm": np.asarray(L1_gnn_b_msg), "emb": np.asarray(L1_gnn_edge_embed), "wiht": turned(L1_gnn_W_ih),
        "whht": turned(L1_gnn_W_hh), "bih": by_gate(L1_gnn_b_ih), "bhh": by_gate(L1_gnn_b_hh),
    }
    nc = bacc.Bacc("TRN2", target_bir_lowering=False, num_devices=1)
    args = [nc.dram_tensor(n, a.shape, mybir.dt.from_np(a.dtype), kind="ExternalInput").ap()
            for n, a in arrays.items()]
    out = nc.dram_tensor("out", (N, D), F32, kind="ExternalOutput").ap()
    gnn(nc, *args, out)
    r = run_bass_kernel_spmd(nc, [arrays], core_ids=[0])
    return r.results[0]["out"]
```

```python
import numpy as np
from contextlib import ExitStack, contextmanager

import concourse.bass as bass
from concourse import mybir

F32, F16, I32, I16 = mybir.dt.float32, mybir.dt.float16, mybir.dt.int32, mybir.dt.int16
ALU = mybir.AluOpType
ACT = mybir.ActivationFunctionType
AX = mybir.AxisListType.X

N, D, E, TYPES = 6250, 128, 206250, 9
LO = 125
BLOCKS = N // LO
EPS = 1e-5

CH = 250
CHUNKS = N // CH
CB = CH // LO

WIN = 2
CHWIN = CH // WIN
WINDOWS = N // WIN
EDGES_MAX = 128
TA, TB = 3, 3
SLOTS = BLOCKS + TB
WCOLS = WIN * SLOTS
BATCH = 25
BATCHES = CHWIN // BATCH
BANKW = 4
UNIT = 2 * BANKW
UNITS = (CHWIN + UNIT - 1) // UNIT
PSLOTS = 3

PARTE = E // LO
HEADS, HLEN = 1250, 165
HPART = HEADS // LO
SB = 5
STEPS = CHUNKS // SB
NOWHERE = 8191
MAGIC = 12582912.0
HSCALE = 4096.0
PARTS = [(0, 14), (14, 27), (27, 40), (40, SLOTS)]
PARTS0 = PARTS[:-1] + [(40, BLOCKS)]


SEMAPHORES = """
heads_in col_set dst_in x_in0 x_in1 x_in2 x_in3 x_in4 weights_in sq_sum eps_set
wm_norm sums0 mean0 var0 std0 nmr0 h0_done turned consts thresholds heads_f compared counted squares scaled g_col
flags flag_sum fields g0 rows_i0 rows_i1 rows_i2 rows_i3 rows_i4 cand_in0 cand_in1 cand_in2 cand_in3 cand_in4
run_i runs_in0 runs_in1 x_b v_prep flag_set x1 aggr psX hst h1 psT tbs psM pvar pstd
pnm h1T tab_hi x1_kept tab_lo msg rz nin psRZ psN hnew result psO nn out deg deg_root onehot evac built degree
adj_out0 adj_out1 mch used0 used1 spent degrees tab0 tab0_hi emb_in norm tab1_zero v_fast v_general g_seen
flat_in tab_zero sum_zero gemb_out h0_scaled table_out table1_out g1 ghist ghot gerows gturned0 gturned1
sum_in0 sum_in1 gadded0 gadded1 gindex0 gindex1 grows0 grows1 gsums0 gsums1 gdiag0 gdiag1 gacross0 gacross1
gsame0 gsame1 gproduct0 gproduct1 load0_0_0
load0_0_1 load0_0_2 load0_0_3 load0_1_0 load0_1_1 load0_1_2 load0_1_3 load1_0_0 load1_0_1 load1_0_2 load1_0_3
load1_1_0 load1_1_1 load1_1_2 load1_1_3
""".split()


class Chain:

    def __init__(self, eng, sem):
        self.eng, self.sem, self.base, self.k = eng, sem, 0, 0

    def did(self, ins):
        ins.then_inc(self.sem, 1)
        self.k += 1
        return ins

    def wait(self, but=0):
        self.eng.wait_ge(self.sem, self.base + self.k - but)

    @contextmanager
    def loop(self, i, times, steps):
        before = self.base + self.k
        self.base, self.k = before + steps * i, 0
        yield
        assert self.k == steps, (self.k, steps)
        self.base, self.k = before + steps * times, 0


def over_chunks(eng, body, chain=None, steps=0, first=1, last=0):
    def pair(i):
        body(2 * i + first, 1)
        body(2 * i + first + 1, 0)

    for c in range(first):
        body(c, c % 2)
    n = (CHUNKS - first - last) // 2
    with eng.Fori(0, n) as i:
        if chain is not None:
            with chain.loop(i, n, 2 * steps):
                pair(i)
        else:
            pair(i)
    for c in range(CHUNKS - last, CHUNKS):
        body(c, c % 2)


def over_tiles(eng, body, chain=None, steps=0):
    body(0)
    with eng.Fori(0, PARTE - 1) as i:
        if chain is not None:
            with chain.loop(i, PARTE - 1, steps):
                body(i + 1)
        else:
            body(i + 1)


def positive(eng, sem, value):
    if not isinstance(value, int) or value > 0:
        eng.wait_ge(sem, value)


def gnn(nc, x, src, dst, typ, w0t, b0, wmt, bm, emb, wiht, whht, bih, bhh, out):
    ctx = ExitStack()
    sems = {name: ctx.enter_context(nc.semaphore(name)) for name in SEMAPHORES}

    def sem(name):
        return sems[name]

    def sb(name, shape, dt):
        return ctx.enter_context(nc.sbuf_tensor(name, shape, dt))

    def dram(name, shape, dt):
        return nc.dram_tensor(name, shape, dt).ap()

    with ctx:
        adj_d = dram("adjacency", (CHUNKS, 128, SLOTS * CH), F16)
        table_d = dram("rows", (N, D), F32)
        sum_d = [dram(f"row_sums{L}", (N + LO, D), F32) for L in range(2)]
        emb_d = dram("scaled_embedding", (TYPES, D), F32)

        x_sb = sb("x_sb", [128, BLOCKS, D], F32)
        h_sb = sb("h_sb", [128, BLOCKS * D], F32)
        h0 = h_sb[:, :].rearrange("p (b f) -> p b f", f=D)
        h1T = h_sb[:, 0:N]
        ring = sb("ring", [128, 2, SLOTS * CH], F16)
        adj = [ring[:, k, :].rearrange("p (h n) -> p h n", n=CH) for k in range(2)]
        TW = SLOTS * 2 * D
        tabs = sb("tabs", [128, 2 * TW], F16)
        tab = [tabs[:, k * TW:(k + 1) * TW] for k in range(2)]
        tabv = [t.rearrange("p (h s f) -> p h s f", s=2, f=D) for t in tab]
        COMBO, LOHOT = 2 * BATCH * WCOLS, 2 * BATCH * 128
        work = sb("work", [128, (COMBO + LOHOT) // 2], F32)
        work16 = work[:, :].bitcast(F16)
        combo = work16[:, 0:COMBO].rearrange("p (s k n) -> p s k n", s=2, k=BATCH)
        lohot = work16[:, COMBO:COMBO + LOHOT].rearrange("p (s k n) -> p s k n", s=2, k=BATCH)
        ring32 = ring[:, :, :].rearrange("p a n -> p (a n)").bitcast(I32)

        RUNW = CHUNKS * 3 * EDGES_MAX
        tabs32 = tabs[:, :].bitcast(F32)
        runs = tabs32[:, 0:RUNW].bitcast(I32).rearrange("p (g k e) -> p g k e", g=CHUNKS, k=3)
        fields = tabs32[:, 0:RUNW].bitcast(F16).rearrange("p (g k e) -> p g k e", g=CHUNKS, k=6)
        F_TA, F_SMALL, F_LO, F_COL = range(4)
        UW = SB * EDGES_MAX
        unp = tabs32[:, RUNW:RUNW + 5 * UW].rearrange("p (k n) -> p k n", k=5)

        mch = sb("mch", [128, 2, 2, CHWIN, 2], F16)
        mch_s = sb("mch_s", [128, 2, 2, CHWIN], F16)
        iota_w = sb("iota_w", [128, WCOLS], F16)
        iota_lo = sb("iota_lo", [128, 128], F16)
        iota_s = sb("iota_s", [128, WIN, TB], F16)
        iota_t = sb("iota_t", [128, TA], F16)
        ident = sb("ident", [128, 128], F32)
        identh = sb("identh", [128, 128], F16)
        zeroh = sb("zeroh", [128, 512], F16)
        zeroh2 = sb("ghot", [128, 192], F16)
        ones = sb("ones", [128, 128], F32)
        thr = sb("thr", [128, CHUNKS], F32)
        thr16 = work[:, 0:(WINDOWS + 1) // 2].bitcast(I16)[:, 0:WINDOWS]
        heads_i = sb("heads_i", [LO, HPART], I32)
        heads = sb("heads", [LO, HPART], F32)
        onesh = sb("onesh", [128, 1], F16)
        cnt = sb("cnt", [128, CHUNKS], F32)
        row = sb("row", [128, CHUNKS], F32)
        row_i = sb("row_i", [128, CHUNKS], I32)
        run0 = sb("run0", [128, CHUNKS], F32)
        run_i = sb("run_i", [128, CHUNKS], I32)
        inside = sb("inside", [128, CHUNKS], F32)
        over = sb("over", [128, CHUNKS], F32)
        flags = sb("flags", [128, 4], F32)
        flag_i = sb("flag_i", [1, 1], I32)
        xsum = sb("xsum", [128, BLOCKS], F32)
        xvar = sb("xvar", [128, BLOCKS], F32)
        nmean = sb("nmean", [128, BLOCKS], F32)
        rstd = sb("rstd", [128, BLOCKS], F32)
        nmr = sb("nmr", [128, BLOCKS], F32)
        epst = sb("epst", [128, 1], F32)
        deg = sb("deg", [128, BLOCKS], F32)
        norm = sb("norm", [128, BLOCKS], F32)
        w0_sb = sb("w0_sb", [128, D], F32)
        b0_sb = sb("b0_sb", [128, D], F32)
        wm_sb = sb("wm_sb", [128, D], F32)
        bm_sb = sb("bm_sb", [128, D], F32)
        wih_sb = sb("wih_sb", [128, 3 * D], F32)
        whh_sb = sb("whh_sb", [128, 3 * D], F32)
        bg_i = sb("bg_i", [128, 3], F32)
        bg_h = sb("bg_h", [128, 3], F32)
        bg = sb("bg", [128, 2], F32)
        gsc = sb("gsc", [128, D], F32)
        ginv = sb("ginv", [128, 1], F32)
        embs = sb("embs", [TYPES, D], F32)
        embh = sb("embh", [TYPES, 2, D], F16)
        pst = sb("pst", [128, CB, 6], F32)
        pmv = sb("pmv", [128, CB, 2], F32)
        pm2 = sb("pm2", [128, CB], F32)
        prs = sb("prs", [128, CB], F32)
        pnm = sb("pnm", [128, CB], F32)

        SW = SB * CHWIN
        compared = ring[:, 0, 0:2 * HPART * SW].rearrange("p (s j n) -> p s j n", s=2, j=HPART)
        second = ring32[:, SLOTS * CH // 2:SLOTS * CH]
        cand = second[:, 0:CHUNKS * HLEN].rearrange("p (g n) -> p g n", g=CHUNKS)
        raw_dst = second[:, CHUNKS * HLEN:CHUNKS * HLEN + PARTE + 1]
        at = CHUNKS * HLEN + PARTE + 1
        below = second[:, at:at + (SB * HLEN + 1) // 2].bitcast(F16)[:, 0:SB * HLEN].rearrange("p (g n) -> p g n", g=SB)
        junk = tabs32[:, RUNW:RUNW + D]
        unsorted = tabs32[:, RUNW:RUNW + PARTE]

        def carve(words, at, *shape):
            n = int(np.prod(shape))
            a = words[:, at:at + n]
            if len(shape) > 1:
                a = a.rearrange("p (a b) -> p a b", a=shape[0])
            return a, at + n

        emb_sb, at = carve(work, (WINDOWS + 1) // 2, TYPES, D)
        sq, at = carve(work, at, D)
        gtmp, at = carve(work, at, D)
        late = work
        x1s, at = carve(late, 2048, CB, D)
        h1s, at = carve(late, at, CB, D)
        tbs, at = carve(late, at, CB, D)
        rz, at = carve(late, at, 2, CH)
        aggr, at = carve(late, at, CH)
        hst, at = carve(late, at, CH)
        msgs, at = carve(late, at, CH)
        nin, at = carve(late, at, CH)
        nn, at = carve(late, at, CH)
        hnew, at = carve(late, at, CH)

        ps = ctx.enter_context(nc.psum_tensor("ps", [128, 8, 512], F32))
        psD = [ps[:, k, 0:CH] for k in range(2)]
        psX = ps[0:LO, 2, 0:CB * D].rearrange("p (b f) -> p b f", f=D)
        psT = ps[:, 3, 0:CH]
        psM = ps[0:LO, 4, 0:CB * D].rearrange("p (b f) -> p b f", f=D)
        psRZ = ps[:, 2, :].rearrange("p (a n) -> p a n", a=2)[:, :, 0:CH]
        psN = ps[:, 3, :].rearrange("p (a n) -> p a n", a=2)[:, :, 0:CH]
        psO = psM
        psDeg = ps[:, 6, 0:BLOCKS * 10]
        psG = ps[:, 4, 0:1]
        psCnt = [ps[0:LO, k, 0:SB] for k in (0, 1, 2, 3, 7)]
        psTurn = ps[:, 7, 0:4 * CHWIN].rearrange("p (k w) -> p k w", k=4)
        psFlag = ps[0:1, 7, 508:509]

        x_v = x.rearrange("(b p) f -> p b f", p=LO)
        out_v = out.rearrange("(b p) f -> p b f", p=LO)
        table_v = table_d.rearrange("(b p) f -> p b f", p=LO)
        XP = 5
        XB = BLOCKS // XP

        flat_i = ring32[:, 0:3 * PARTE].rearrange("p (a n) -> p a n", a=3)
        flat_f = ring32[:, 3 * PARTE:7 * PARTE].bitcast(F32).rearrange("p (a n) -> p a n", a=4)
        src_f, dst_f, q_f, lo_f = (flat_f[:, k, :] for k in range(4))
        gbuf = work[:, 0:2048]
        cut = lambda k, n: gbuf[:, 128 * k:128 * k + n]
        rows_in, erows_in, diag, same, lower, sums, before = (cut(k, 128) for k in range(7))
        small = cut(7, 8)
        count_c, dup_c, toward_c, trash_c = (small[:, k:k + 1] for k in range(4))
        ints = cut(8, 8).bitcast(I32)
        isrc, itype, idst = (ints[:, k:k + 1] for k in range(3))
        sum_in = cut(9, 256).rearrange("p (b f) -> p b f", f=D)
        psB = ps[:, 5, 0:128]
        psS = ps[:, 7, 0:128]
        NE = LO
        ghot = zeroh2[:, :]
        sum_v = [sum_d[L][0:N, :].rearrange("(b p) f -> p b f", p=LO) for L in range(2)]

        def spread(a, shape):
            return a.unsqueeze(2).broadcast_to(shape)


        def prepare_sync(sp):
            sp.dma_start(heads_i[:, :], dst.rearrange("(p j n) -> p j n", j=HPART, n=HLEN)[:, :, 0:1]
                         .rearrange("p j n -> p (j n)"), allow_slow_non_contiguous=True).then_inc(sem("heads_in"), 16)
            sp.wait_ge(sem("col_set"), 1)
            halo = bass.AP(tensor=dst.tensor, offset=dst.offset, ap=[[PARTE, LO - 1], [1, PARTE + 1]])
            sp.dma_start(raw_dst[0:LO - 1, :], halo).then_inc(sem("dst_in"), 16)
            sp.dma_start(raw_dst[LO - 1:LO, 0:PARTE], dst.rearrange("(p n) -> p n", p=LO)[LO - 1:LO, :])\
              .then_inc(sem("dst_in"), 16)

        def prepare_scalar(act):
            P = slice(0, LO)
            row_of = lambda a: a.rearrange("(a n) -> a n", a=1)
            for k in range(XP):
                act.dma_start(x_sb[0:LO, k * XB:(k + 1) * XB, :], x_v[:, k * XB:(k + 1) * XB, :])\
                   .then_inc(sem(f"x_in{k}"), 16)
            for to, a in ((w0_sb, w0t), (wm_sb, wmt), (wih_sb, wiht), (whh_sb, whht), (bg_i, bih), (bg_h, bhh),
                          (embs, emb)):
                act.dma_start(to[:, :], a).then_inc(sem("weights_in"), 16)
            for to, a in ((b0_sb[:, :], b0), (bm_sb[:, :], bm),
                          (emb_sb[:, :, :].rearrange("p t f -> p (t f)"), emb.rearrange("t f -> (t f)"))):
                act.dma_start(to, a.partition_broadcast(128)).then_inc(sem("weights_in"), 16)
            for k in range(XP):
                act.wait_ge(sem(f"x_in{k}"), 16)
                for b in range(k * XB, (k + 1) * XB):
                    last = act.activation(h0[P, b, :], x_sb[P, b, :], ACT.Copy, accum_out=xsum[P, b:b + 1])
            last.then_inc(sem("sums0"), 1)
            act.wait_ge(sem("sums0"), 1)
            act.activation(nmean[P, :], xsum[P, :], ACT.Copy, scale=-1.0 / D).then_inc(sem("mean0"), 1)
            act.wait_ge(sem("sq_sum"), 1)
            act.wait_ge(sem("eps_set"), 1)
            act.activation(gsc[:, :], psB, ACT.Sqrt).then_inc(sem("wm_norm"), 1)
            act.wait_ge(sem("mean0"), 1)
            for b in range(BLOCKS):
                last = act.activation(h0[P, b, :], x_sb[P, b, :], ACT.Square, bias=nmean[P, b:b + 1],
                                      accum_out=xvar[P, b:b + 1])
            last.then_inc(sem("var0"), 1)
            act.wait_ge(sem("var0"), 1)
            act.activation(rstd[P, :], xvar[P, :], ACT.Sqrt, bias=epst[P, :], scale=1.0 / D).then_inc(sem("std0"), 1)

        def prepare_tensor(pe):
            pe.wait_ge(sem("consts"), 1)
            for m in range(STEPS):
                pe.wait_ge(sem("compared"), m + 1)
                for g in range(SB):
                    for j in range(HPART):
                        last = pe.matmul(psCnt[m][:, g:g + 1],
                                         compared[0:LO, m % 2, j, CHWIN * g:CHWIN * (g + 1)], onesh[0:LO, :],
                                         start=j == 0, stop=j == HPART - 1)
                last.then_inc(sem("counted"), 1)
            pe.wait_ge(sem("squares"), 1)
            pe.matmul(psB, ones[:, :], sq[:, :], start=True, stop=True).then_inc(sem("sq_sum"), 1)
            pe.wait_ge(sem("scaled"), 1)
            pe.matmul(psG, gsc[0:1, :], ones[0:1, 0:1], start=True, stop=True).then_inc(sem("g_col"), 1)

        def prepare_gpsimd(gp):
            gp.iota(thr16, [[WIN, WINDOWS]], base=0, channel_multiplier=0).then_inc(sem("thresholds"), 1)
            gp.memset(onesh[:, :], 1.0)
            gp.memset(raw_dst[:, PARTE:PARTE + 1], NOWHERE).then_inc(sem("col_set"), 1)
            gp.memset(ones[:, :], 1.0)
            gp.memset(ident[:, :], 0.0).then_inc(sem("g0"), 1)
            gp.memset(zeroh[:, :], 0.0)
            gp.wait_ge(sem("g0"), 1)
            gp.affine_select(out=ident[:, :], in_=ident[:, :], compare_op=ALU.not_equal, fill=1.0, base=0,
                             pattern=[[-1, 128]], channel_multiplier=1).then_inc(sem("g0"), 1)
            gp.iota(thr[:, :], [[CH, CHUNKS]], base=0, channel_multiplier=WIN, allow_small_or_imprecise_dtypes=True)
            gp.iota(iota_w[:, :], [[1, WCOLS]], base=0, channel_multiplier=0, allow_small_or_imprecise_dtypes=True)
            gp.iota(iota_lo[:, :], [[1, 128]], base=0, channel_multiplier=0, allow_small_or_imprecise_dtypes=True)
            gp.iota(iota_s[:, :, :], [[TB, WIN], [1, TB]], base=0, channel_multiplier=0,
                    allow_small_or_imprecise_dtypes=True)
            gp.iota(iota_t[:, :], [[1, TA]], base=0, channel_multiplier=0, allow_small_or_imprecise_dtypes=True)
            gp.wait_ge(sem("g0"), 2)
            gp.tensor_copy(identh[:, :], ident[:, :]).then_inc(sem("consts"), 1)

            def elements(a):
                return a.rearrange("(a n) -> a n", a=1)

            def candidates(m):
                gp.wait_ge(sem(f"rows_i{m}"), 1)
                for g in range(SB * m, SB * (m + 1)):
                    gp.indirect_dma_start(cand[0:LO, g, :], None, elements(dst),
                                          bass.IndirectOffsetOnAxis(row_i[0:LO, g:g + 1], 1))\
                      .then_inc(sem(f"cand_in{m}"), 16)

            def run_edges(m):
                gp.wait_ge(sem("run_i"), m + 1)
                for g in range(SB * m, SB * (m + 1)):
                    for k, a in enumerate((src, dst, typ)):
                        gp.indirect_dma_start(runs[0:LO, g, k, :], None, elements(a),
                                              bass.IndirectOffsetOnAxis(run_i[0:LO, g:g + 1], 1))\
                          .then_inc(sem("runs_in1" if m else "runs_in0"), 16)

            candidates(0)
            candidates(1)
            run_edges(0)
            for m in range(2, STEPS):
                candidates(m)
            for m in range(1, STEPS):
                run_edges(m)

        def search_scalars(v, ch, m):
            P, at = slice(0, LO), slice(SB * m, SB * (m + 1))
            v.wait_ge(sem("counted"), m + 1)
            ch.did(v.tensor_scalar(row[P, at], psCnt[m], -1.0, 0.0, ALU.add, ALU.max))
            ch.wait()
            ch.did(v.tensor_scalar(row[P, at], row[P, at], float(HLEN), None, ALU.mult))
            ch.wait()
            v.tensor_copy(row_i[P, at], row[P, at]).then_inc(sem(f"rows_i{m}"), 1)

        def search_runs(v, ch, m):
            P, at = slice(0, LO), slice(SB * m, SB * (m + 1))
            v.wait_ge(sem(f"cand_in{m}"), 16 * SB)
            ch.did(v.tensor_tensor(below[P, :, :], cand[P, at, :], spread(thr[P, at], [LO, SB, HLEN]), ALU.is_lt))
            ch.wait()
            ch.did(v.tensor_reduce(cnt[P, at], below[P, :, :], AX, ALU.add))
            ch.wait()
            ch.did(v.tensor_tensor(run0[P, at], row[P, at], cnt[P, at], ALU.add))
            ch.wait()
            ch.did(v.tensor_scalar(run0[P, at], run0[P, at], float(E - EDGES_MAX), None, ALU.min))
            ch.wait()
            ch.did(v.tensor_scalar(inside[P, at], run0[P, at], float(E - EDGES_MAX), None, ALU.is_lt))
            v.tensor_copy(run_i[P, at], run0[P, at]).then_inc(sem("run_i"), 1)

        UNPACK = 12

        def unpack(v, ch, g, n):
            P = slice(0, LO)
            at = bass.ds(g, n) if not isinstance(g, int) else slice(g, g + n)
            own = lambda k: runs[P, at, k, :]
            field = lambda k: fields[P, at, k, :]
            t0, t1, t2, t3, t4 = (unp[P, k, 0:n * EDGES_MAX].rearrange("p (g e) -> p g e", g=n) for k in range(5))
            ch.did(v.tensor_scalar(t0, own(0), 1.0 / LO, 0.5 / LO - 0.5, ALU.mult, ALU.add))
            for k in range(n):
                one = bass.ds(g + k, 1) if not isinstance(g, int) else slice(g + k, g + k + 1)
                ch.did(v.tensor_scalar(t2[:, k, :], runs[P, one, 1, :].rearrange("p g e -> p (g e)"), thr[P, one],
                                       -1.0, ALU.subtract, ALU.max))
            ch.did(v.tensor_scalar(t3, own(2), 0.0, float(TYPES - 1), ALU.max, ALU.min))
            ch.wait()
            ch.did(v.tensor_scalar(t0, t0, MAGIC, MAGIC, ALU.add, ALU.subtract))
            ch.did(v.tensor_scalar(t2, t2, float(WIN), None, ALU.min))
            ch.did(v.tensor_scalar(t4, t3, float(TB), None, ALU.is_ge))
            ch.wait()
            ch.did(v.scalar_tensor_tensor(t1, t0, -float(LO), own(0), ALU.mult, ALU.add))
            ch.did(v.scalar_tensor_tensor(field(F_COL), t2, float(SLOTS), t0, ALU.mult, ALU.add))
            ch.did(v.scalar_tensor_tensor(t4, t3, float(2 * TB), t4, ALU.is_ge, ALU.add))
            ch.did(v.scalar_tensor_tensor(over[P, at], t2[:, :, EDGES_MAX - 1], float(WIN), inside[P, at],
                                          ALU.is_lt, ALU.mult))
            ch.wait()
            ch.did(v.tensor_copy(field(F_LO), t1))
            ch.did(v.scalar_tensor_tensor(t3, t4, -float(TB), t3, ALU.mult, ALU.add))
            ch.did(v.tensor_copy(field(F_TA), t4))
            ch.wait()
            v.scalar_tensor_tensor(field(F_SMALL), t2, float(TB), t3, ALU.mult, ALU.add).then_inc(sem("fields"), n)

        def prepare_vector(v, ch):
            P = slice(0, LO)
            v.memset(epst[:, :], EPS).then_inc(sem("eps_set"), 1)
            v.wait_ge(sem("heads_in"), 16)
            ch.did(v.tensor_copy(heads[:, :], heads_i[:, :]))
            v.wait_ge(sem("thresholds"), 1)
            ch.wait()
            for m in range(STEPS):
                if m >= 2:
                    v.wait_ge(sem("counted"), m - 1)
                for j in range(HPART):
                    last = v.tensor_scalar(compared[P, m % 2, j, :], thr16[P, SW * m:SW * (m + 1)],
                                           heads[P, j:j + 1], None, ALU.is_gt)
                last.then_inc(sem("compared"), 1)
                if m:
                    search_scalars(v, ch, m - 1)
            search_scalars(v, ch, STEPS - 1)
            v.wait_ge(sem("consts"), 1)
            search_runs(v, ch, 0)
            v.wait_ge(sem("weights_in"), 160)
            v.tensor_tensor(sq[:, :], wm_sb[:, :], wm_sb[:, :], ALU.mult).then_inc(sem("squares"), 1)
            search_runs(v, ch, 1)
            v.wait_ge(sem("sq_sum"), 1)
            ch.did(v.tensor_reduce(gtmp[:, :], emb_sb[:, :, :].rearrange("p t f -> p f t"), AX, ALU.max,
                                   apply_absolute_value=True))
            ch.did(v.scalar_tensor_tensor(sq[:, :], bm_sb[:, :], -1.0, bm_sb[:, :], ALU.mult, ALU.max))
            ch.wait()
            ch.did(v.tensor_tensor(gtmp[:, :], gtmp[:, :], sq[:, :], ALU.add))
            v.wait_ge(sem("wm_norm"), 1)
            ch.wait()
            ch.did(v.scalar_tensor_tensor(gsc[:, :], gsc[:, :], 11.4, gtmp[:, :], ALU.mult, ALU.add))
            ch.wait()
            ch.did(v.tensor_scalar(gsc[:, :], gsc[:, :], 1e-20, 1.0 / 32768, ALU.add, ALU.mult))
            ch.wait()
            ch.did(v.reciprocal(gsc[:, :], gsc[:, :]))
            ch.wait()
            ch.did(v.tensor_tensor(wm_sb[:, :], wm_sb[:, :], gsc[:, :], ALU.mult))
            ch.did(v.tensor_tensor(bm_sb[:, :], bm_sb[:, :], gsc[:, :], ALU.mult))
            ch.did(v.tensor_tensor(embs[:, :], embs[:, :], gsc[0:TYPES, :], ALU.mult))
            ch.did(v.tensor_tensor(bg[:, :], bg_i[:, 0:2], bg_h[:, 0:2], ALU.add))
            ch.wait()
            ch.did(v.tensor_copy(embh[:, 0, :], embs[:, :]))
            ch.wait()
            v.tensor_tensor(embh[:, 1, :], embs[:, :], embh[:, 0, :], ALU.subtract).then_inc(sem("scaled"), 1)
            v.wait_ge(sem("g_col"), 1)
            ch.did(v.reciprocal(ginv[:, :], psG))
            v.wait_ge(sem("runs_in0"), 16 * 3 * SB)
            unpack(v, ch, 0, SB)

        def norm0_vector(v, ch):
            P = slice(0, LO)
            v.wait_ge(sem("std0"), 1)
            ch.did(v.reciprocal(rstd[P, :], rstd[P, :]))
            ch.wait()
            v.tensor_tensor(nmr[P, :], nmean[P, :], rstd[P, :], ALU.mult).then_inc(sem("nmr0"), 1)

        def check_sorted(v, ch):
            P = slice(0, LO)
            v.wait_ge(sem("dst_in"), 32)
            ch.did(v.tensor_tensor(unsorted[P, :], raw_dst[P, 1:PARTE + 1], raw_dst[P, 0:PARTE], ALU.is_lt))
            ch.wait()
            ch.did(v.tensor_reduce(flags[P, 1:2], unsorted[P, :], AX, ALU.max))
            ch.wait()

        def build_all_vector(v, ch):
            build_vector(v, 0, 0, ch)
            norm0_vector(v, ch)
            for m in range(2, STEPS):
                search_runs(v, ch, m)
            check_sorted(v, ch)
            build_vector(v, 1, 1, ch)
            build_vector(v, 2, 0, ch)
            v.wait_ge(sem("runs_in1"), 16 * 3 * (CHUNKS - SB))
            first, last = 3, 2
            n = (CHUNKS - first - last) // 2
            with v.Fori(0, n) as i:
                with ch.loop(i, n, 2 * 2 * BATCHES + UNPACK + 2):
                    unpack(v, ch, 2 * i + first + 2, 2)
                    build_vector(v, 2 * i + first, 1, ch)
                    build_vector(v, 2 * i + first + 1, 0, ch)
            build_vector(v, CHUNKS - 2, 1, ch)
            P = slice(0, LO)
            ch.did(v.tensor_reduce(flags[P, 0:1], over[P, :], AX, ALU.max))
            ch.wait()
            v.tensor_tensor(flags[P, 2:3], flags[P, 0:1], flags[P, 1:2], ALU.add).then_inc(sem("flags"), 1)
            build_vector(v, CHUNKS - 1, 0, ch)
            v.wait_ge(sem("flag_sum"), 1)
            v.tensor_scalar(flag_i[:, :], psFlag, 0.0, None, ALU.is_gt).then_inc(sem("flag_set"), 1)

        def block_of(v, ch, q, s):
            ch.did(v.tensor_scalar(q, s, 1.0 / LO, 0.5 / LO - 0.5, ALU.mult, ALU.add))
            ch.wait()
            ch.did(v.tensor_scalar(q, q, MAGIC, MAGIC, ALU.add, ALU.subtract))
            ch.wait()


        def blocks(n):
            return bass.ds(CB * n, CB) if not isinstance(n, int) else slice(CB * n, CB * n + CB)

        def nodes(n):
            return bass.ds(CH * n, CH) if not isinstance(n, int) else slice(CH * n, CH * n + CH)

        def post0_tensor(pe, n, t):
            if t == 0:
                positive(pe, sem("x1"), n)
                pe.wait_ge(sem("aggr"), n + 1)
                for j in range(CB):
                    last = pe.matmul(psX[:, j, :], aggr[:, LO * j:LO * (j + 1)], w0_sb[:, :], start=True, stop=True)
                last.then_inc(sem("psX"), 1)
            if t == 1:
                positive(pe, sem("hst"), n)
                pe.wait_ge(sem("h1"), n + 1)
                for j in range(CB):
                    last = pe.transpose(psT[:, LO * j:LO * (j + 1)], h1s[0:LO, j, :], ident[0:LO, 0:LO])
                last.then_inc(sem("psT"), 1)
            if t == 2:
                positive(pe, sem("tbs"), n)
                pe.wait_ge(sem("hst"), n + 1)
                for j in range(CB):
                    last = pe.matmul(psM[:, j, :], hst[:, LO * j:LO * (j + 1)], wm_sb[:, :], start=True, stop=True)
                last.then_inc(sem("psM"), 1)

        def post0_scalar(act, n, par, summed, split):
            P = slice(0, LO)
            summed(act, n)
            positive(act, sem("psX"), n)
            act.activation(aggr[:, :], psD[par], ACT.Relu, scale=1.0 / HSCALE).then_inc(sem("aggr"), 1)
            act.wait_ge(sem("pvar"), n + 1)
            act.activation(prs[P, :], pmv[P, :, 1], ACT.Sqrt, bias=epst[P, :]).then_inc(sem("pstd"), 1)
            act.wait_ge(sem("pnm"), n + 1)
            positive(act, sem("psT"), n)
            for j in range(CB):
                last = act.activation(h1s[P, j, :], x1s[P, j, :], ACT.Relu, bias=pnm[P, j:j + 1],
                                      scale=prs[P, j:j + 1])
            last.then_inc(sem("h1"), 1)
            act.wait_ge(sem("psT"), n + 1)
            positive(act, sem("psM"), n)
            positive(act, sem("h1T"), n)
            act.activation(hst[:, :], psT, ACT.Copy).then_inc(sem("hst"), 1)
            if split:
                act.wait_ge(sem("tbs"), n + 1)
                act.activation(tabv[1][P, blocks(n), 0, :], tbs[P, :, :], ACT.Copy).then_inc(sem("tab_hi"), 1)

        def post0_gpsimd(gp, n, split):
            gp.wait_ge(sem("x1"), n + 1)
            gp.tensor_copy(x_sb[0:LO, blocks(n), :], x1s[0:LO, :, :]).then_inc(sem("x1_kept"), 1)
            gp.wait_ge(sem("hst"), n + 1)
            gp.tensor_copy(h1T[:, nodes(n)], hst[:, :]).then_inc(sem("h1T"), 1)
            if split:
                gp.wait_ge(sem("tab_hi"), n + 1)
                gp.tensor_tensor(tabv[1][0:LO, blocks(n), 1, :], tbs[0:LO, :, :], tabv[1][0:LO, blocks(n), 0, :],
                                 ALU.subtract).then_inc(sem("tab_lo"), 1)

        def post0_vector(v, n, ch, spent):
            P = slice(0, LO)
            v.wait_ge(sem("psX"), n + 1)
            positive(v, sem("h1"), n)
            positive(v, sem("x1_kept"), n)
            v.tensor_tensor(x1s[P, :, :], psX, x_sb[P, blocks(n), :], ALU.add).then_inc(sem("x1"), 1)
            v.wait_ge(sem("x1"), n + 1)
            for j in range(CB):
                ch.did(v.bn_stats(pst[P, j, :], x1s[P, j, :]))
            ch.wait()
            ch.did(v.tensor_tensor(pmv[P, :, 0], pst[P, :, 1], pst[P, :, 4], ALU.add))
            ch.did(v.tensor_tensor(pmv[P, :, 1], pst[P, :, 1], pst[P, :, 4], ALU.subtract))
            ch.did(v.tensor_tensor(pm2[P, :], pst[P, :, 2], pst[P, :, 5], ALU.add))
            ch.wait()
            ch.did(v.scalar_tensor_tensor(pmv[P, :, 1], pmv[P, :, 1], 0.25, pmv[P, :, 1], ALU.mult, ALU.mult))
            ch.wait()
            v.scalar_tensor_tensor(pmv[P, :, 1], pm2[P, :], 1.0 / D, pmv[P, :, 1], ALU.mult, ALU.add)\
             .then_inc(sem("pvar"), 1)
            v.wait_ge(sem("pstd"), n + 1)
            ch.did(v.reciprocal(prs[P, :], prs[P, :]))
            ch.wait()
            v.scalar_tensor_tensor(pnm[P, :], pmv[P, :, 0], -0.5, prs[P, :], ALU.mult, ALU.mult).then_inc(sem("pnm"), 1)
            v.wait_ge(sem("psM"), n + 1)
            spent(n)
            v.tensor_tensor(tbs[P, :, :], psM, bm_sb[P, :].unsqueeze(1).broadcast_to([LO, CB, D]), ALU.add)\
             .then_inc(sem("tbs"), 1)

        def post1_tensor(pe, n, t):
            if t == 0:
                pe.wait_ge(sem("msg"), n + 1)
                positive(pe, sem("rz"), n)
                positive(pe, sem("nin"), n)
                for a in range(2):
                    w = slice(D * a, D * (a + 1))
                    pe.matmul(psRZ[:, a, :], wih_sb[:, w], msgs[:, :], start=True, stop=False)
                    last = pe.matmul(psRZ[:, a, :], whh_sb[:, w], h1T[:, nodes(n)], start=False, stop=True)
                last.then_inc(sem("psRZ"), 1)
                w = slice(2 * D, 3 * D)
                pe.matmul(psN[:, 0, :], wih_sb[:, w], msgs[:, :], start=True, stop=True)
                pe.matmul(psN[:, 1, :], whh_sb[:, w], h1T[:, nodes(n)], start=True, stop=True).then_inc(sem("psN"), 1)
            if t == 1:
                pe.wait_ge(sem("hnew"), n + 1)
                positive(pe, sem("result"), n)
                for j in range(CB):
                    last = pe.transpose(psO[:, j, :], hnew[:, LO * j:LO * (j + 1)], ident[:, :])
                last.then_inc(sem("psO"), 1)

        def post1_scalar(act, n, par, summed):
            summed(act, n)
            positive(act, sem("psN"), n)
            act.activation(msgs[:, :], psD[par], ACT.Copy, scale=ginv[:, 0:1]).then_inc(sem("msg"), 1)
            act.wait_ge(sem("psRZ"), n + 1)
            positive(act, sem("hnew"), n)
            for a in range(2):
                last = act.activation(rz[:, a, :], psRZ[:, a, :], ACT.Sigmoid, bias=bg[:, a:a + 1])
            last.then_inc(sem("rz"), 1)
            act.wait_ge(sem("nin"), n + 1)
            act.activation(nn[:, :], nin[:, :], ACT.Tanh, bias=bg_i[:, 2:3]).then_inc(sem("nn"), 1)

        def post1_vector(v, n, ch):
            v.wait_ge(sem("psN"), n + 1)
            v.wait_ge(sem("rz"), n + 1)
            ch.did(v.scalar_tensor_tensor(nin[:, :], psN[:, 1, :], bg_h[:, 2:3], rz[:, 0, :], ALU.add, ALU.mult))
            ch.wait()
            v.tensor_tensor(nin[:, :], nin[:, :], psN[:, 0, :], ALU.add).then_inc(sem("nin"), 1)
            v.wait_ge(sem("nn"), n + 1)
            positive(v, sem("psO"), n)
            ch.did(v.tensor_tensor(hnew[:, :], h1T[:, nodes(n)], nn[:, :], ALU.subtract))
            ch.wait()
            ch.did(v.tensor_tensor(hnew[:, :], rz[:, 1, :], hnew[:, :], ALU.mult))
            ch.wait()
            v.tensor_tensor(hnew[:, :], nn[:, :], hnew[:, :], ALU.add).then_inc(sem("hnew"), 1)
            v.wait_ge(sem("psO"), n + 1)
            v.tensor_tensor(x_sb[0:LO, blocks(n), :], psO, x_sb[0:LO, blocks(n), :], ALU.add).then_inc(sem("result"), 1)

        def store_result(sp, n):
            sp.wait_ge(sem("result"), n + 1)
            sp.dma_start(out_v[:, blocks(n), :], x_sb[0:LO, blocks(n), :]).then_inc(sem("out"), 16)


        def norm_vector(v, ch, reduced):
            reduced()
            ch.wait()
            P = slice(0, LO)
            v.tensor_scalar(deg[P, :], deg[P, :], 1.0, None, ALU.max).then_inc(sem("deg"), 1)
            v.wait_ge(sem("deg_root"), 1)
            ch.did(v.reciprocal(norm[P, :], norm[P, :]))
            ch.wait()
            ch.did(v.tensor_scalar(norm[P, :], norm[P, :], HSCALE, None, ALU.mult))
            ch.wait()

        def norm_scalar(act):
            act.wait_ge(sem("deg"), 1)
            act.activation(norm[0:LO, :], deg[0:LO, :], ACT.Sqrt).then_inc(sem("deg_root"), 1)

        def turn_tensor(pe, g):
            pe.wait_ge(sem("fields"), g + 1)
            positive(pe, sem("mch"), g)
            for k, f in enumerate((F_LO, F_COL, F_TA, F_SMALL)):
                lhs = fields[0:LO, g:g + 1, f, :] if isinstance(g, int) else fields[0:LO, bass.ds(g, 1), f, :]
                last = pe.matmul(psTurn[:, k, :], lhs.rearrange("p g e -> p (g e)"), identh[0:LO, 0:LO],
                                 start=True, stop=True)
            last.then_inc(sem("turned"), 1)

        def turn_scalar(act, g, par):
            act.wait_ge(sem("turned"), g + 1)
            positive(act, sem("onehot"), BATCHES * (g - 1))
            for k in range(2):
                act.activation(mch[:, par, k, :, :], spread(psTurn[:, k, :], [128, CHWIN, 2]), ACT.Copy)
            act.activation(mch_s[:, par, :, :], psTurn[:, 2:4, :], ACT.Copy).then_inc(sem("mch"), 1)

        def build_tensor(pe, c, par):
            for w in range(CHWIN):
                b, k = divmod(w, BATCH)
                u, i = divmod(w, UNIT)
                slot = (par + b) % 2
                if k == 0:
                    pe.wait_ge(sem("onehot"), BATCHES * c + b + 1)
                if i == 0:
                    back = (1, 0, 2) if par == 0 else (2, 1, 0)
                    positive(pe, sem("evac"), UNITS * c + (u - 2 if u >= PSLOTS else -back[u]))
                o = WCOLS * (i % BANKW)
                last = pe.matmul(ps[:, 2 * ((u + par) % PSLOTS) + i // BANKW, o:o + WCOLS], lohot[:, slot, k, :],
                                 combo[:, slot, k, :], start=True, stop=True)
                if i == UNIT - 1 or w == CHWIN - 1:
                    last.then_inc(sem("built"), 1)
                elif k == BATCH - 1:
                    last.then_inc(sem("spent"), 1)
                if not (isinstance(c, int) and c == 0) and i % 4 == 3 and w // 4 < CH // 10:
                    degree_tensor(pe, 1 - par, w // 4)
                if w == UNIT and not (isinstance(c, int) and c == CHUNKS - 1):
                    turn_tensor(pe, c + 1)

        def degree_tensor(pe, par, j):
            last = pe.matmul(psDeg, identh[:, :], adj[par][:, 0:BLOCKS, 10 * j:10 * j + 10], start=False, stop=False,
                             skip_group_check=True)
            if j == CH // 10 - 1:
                last.then_inc(sem("degree"), 1)

        def build_scalar(act, c, par):
            for u in range(UNITS):
                act.wait_ge(sem("built"), UNITS * c + u + 1)
                if u == 0:
                    positive(act, sem("degree"), c - 1)
                    if not (isinstance(c, int) and c == 0):
                        if par:
                            positive(act, sem("adj_out1"), 8 * (c - 1))
                        else:
                            act.wait_ge(sem("adj_out0"), 8 * c)
                s = 2 * ((u + par) % PSLOTS)
                n = CHWIN - UNIT * u
                whole = lambda k, banks, m: (adj[par][:, :, k:k + banks * m]
                                             .rearrange("p h (b x) -> p h b x", b=banks))
                if n >= UNIT:
                    x = WIN * BANKW
                    act.activation(whole(x * 2 * u, 2, x),
                                   ps[:, s:s + 2, 0:x * SLOTS].rearrange("p b (x h) -> p h b x", h=SLOTS),
                                   ACT.Copy).then_inc(sem("evac"), 1)
                else:
                    for b in range(2):
                        x = WIN * (BANKW if b == 0 else n - BANKW)
                        last = act.activation(whole(WIN * (UNIT * u + BANKW * b), 1, x),
                                              ps[:, s + b:s + b + 1, 0:x * SLOTS]
                                              .rearrange("p b (x h) -> p h b x", h=SLOTS), ACT.Copy)
                    last.then_inc(sem("evac"), 1)
                if u == 2 and not (isinstance(c, int) and c == CHUNKS - 1):
                    turn_scalar(act, c + 1, 1 - par)
                if u == 6:
                    if isinstance(c, int) and c == 0:
                        act.wait_ge(sem("nmr0"), 1)
                    for j in range(CB):
                        at = bass.ds(CB * c + j, 1) if not isinstance(c, int) else slice(CB * c + j, CB * c + j + 1)
                        last = act.activation(h0[0:LO, at, :], x_sb[0:LO, at, :], ACT.Relu, bias=nmr[0:LO, at],
                                              scale=rstd[0:LO, at])
                    last.then_inc(sem("h0_done"), 1)

        def build_vector(v, c, par, ch):
            for b in range(BATCHES):
                slot = (par + b) % 2
                if b == 0:
                    v.wait_ge(sem("mch"), c + 1)
                if b == 1:
                    positive(v, sem("built"), UNITS * c)
                else:
                    positive(v, sem("spent"), (BATCHES - 1) * c + max(b - 1, 0))
                at = slice(BATCH * b, BATCH * (b + 1))
                def hot(o, iota, k):
                    n = o.shape[-1] // 2
                    ch.did(v.tensor_tensor(o.rearrange("p k (n t) -> p k n t", t=2),
                                           iota.rearrange("p (n t) -> p n t", t=2).unsqueeze(1)
                                               .broadcast_to([128, BATCH, n, 2]),
                                           mch[:, par, k, at, :].unsqueeze(2).broadcast_to([128, BATCH, n, 2]),
                                           ALU.is_equal))
                hot(lohot[:, slot, :, :], iota_lo[:, :], 0)
                hot(combo[:, slot, :, :], iota_w[:, :], 1)
                ch.wait(but=1)
                v.tensor_tensor(lohot[:, slot, :, LO:128], iota_t[:, :].unsqueeze(1).broadcast_to([128, BATCH, TA]),
                                spread(mch_s[:, par, 0, at], [128, BATCH, TA]), ALU.is_equal)
                ch.wait()
                v.tensor_tensor(
                    combo[:, slot, :, :].rearrange("p k (d h) -> p k d h", h=SLOTS)[:, :, :, BLOCKS:SLOTS],
                    iota_s[:, :, :].unsqueeze(1).broadcast_to([128, BATCH, WIN, TB]),
                    mch_s[:, par, 1, at].unsqueeze(2).unsqueeze(3).broadcast_to([128, BATCH, WIN, TB]),
                    ALU.is_equal).then_inc(sem("onehot"), 1)

        def build_sync(sp, c, par):
            sp.wait_ge(sem("evac"), UNITS * (c + 1))
            at = slice(c, c + 1) if isinstance(c, int) else bass.ds(c, 1)
            sp.dma_start(adj_d[at, :, :].rearrange("a p n -> (a p) n"), ring[:, par, :]).then_inc(sem(f"adj_out{par}"), 16)

        def load_sync(sp, L, c, par, slot):
            at = slice(c, c + 1) if isinstance(c, int) else bass.ds(c, 1)
            for j, (a, b) in enumerate((PARTS0, PARTS)[L]):
                if isinstance(c, int) and c < 2:
                    if L:
                        sp.wait_ge(sem("used0"), 4 * (CHUNKS - 2 + c) + j + 1)
                else:
                    sp.wait_ge(sem(f"used{L}"), 4 * (c - 2) + j + 1)
                sp.dma_start(ring[:, slot, a * CH:b * CH],
                             adj_d[at, :, a * CH:b * CH].rearrange("a p n -> (a p) n"))\
                  .then_inc(sem(f"load{L}_{slot}_{j}"), 16)

        def product_tensor(pe, L, c, par, between, ready):
            parts = (PARTS0, PARTS)[L]
            slot = par if L else 1 - par
            K = (LO, 128)[L]
            for j, (a, b) in enumerate(parts):
                pe.wait_ge(sem(f"load{L}_{slot}_{j}"), 8 * c + 8 + 8 * (1 - par))
                for h in range(a, b):
                    if isinstance(c, int) and c == 0:
                        ready(h)
                    for s in range(2):
                        last = pe.matmul(psD[slot], tabv[L][0:K, h, s, :], adj[slot][0:K, h, :],
                                         start=h == 0 and s == 0, stop=h == parts[-1][1] - 1 and s == 1)
                last.then_inc(sem(f"used{L}"), 1)
                between(j)

        fast_summed = [lambda eng, n: eng.wait_ge(sem("used0"), 4 * n + 4),
                       lambda eng, n: eng.wait_ge(sem("used1"), 4 * n + 4)]

        def build_all_tensor(pe):
            pe.matmul(psDeg, zeroh[:, 0:128], zeroh[:, 0:BLOCKS * 10], start=True, stop=False, skip_group_check=True)
            turn_tensor(pe, 0)
            def body(c, par):
                if isinstance(c, int) and c == CHUNKS - 1:
                    pe.wait_ge(sem("flags"), 1)
                    pe.matmul(psFlag, flags[0:LO, 2:3], ones[0:LO, 0:1], start=True, stop=True)\
                      .then_inc(sem("flag_sum"), 1)
                build_tensor(pe, c, par)
            over_chunks(pe, body, first=3, last=2)
            pe.wait_ge(sem("evac"), UNITS * CHUNKS)
            for j in range(CH // 10):
                degree_tensor(pe, 0, j)
            pe.matmul(psDeg, zeroh[:, 0:128], zeroh[:, 0:BLOCKS * 10], start=False, stop=True, skip_group_check=True)\
              .then_inc(sem("degrees"), 1)

        def fast_tensor(pe):
            def ready0(h):
                pe.wait_ge(sem("tab0"), h + 1)

            def ready1(h):
                if h == 0:
                    pe.wait_ge(sem("tab_lo"), CHUNKS - 1)
                if h == CB * (CHUNKS - 1):
                    pe.wait_ge(sem("tab_lo"), CHUNKS)
                    pe.wait_ge(sem("emb_in"), 16 * TA)

            def body0(c, par):
                def between(j):
                    if not (isinstance(c, int) and c == 0) and j < 3:
                        post0_tensor(pe, c - 1, j)
                product_tensor(pe, 0, c, par, between, ready0)

            def body1(c, par):
                def between(j):
                    if isinstance(c, int) and c == 0:
                        if j < 3:
                            post0_tensor(pe, CHUNKS - 1, j)
                    elif j in (1, 3):
                        post1_tensor(pe, c - 1, j // 2)
                product_tensor(pe, 1, c, par, between, ready1)

            over_chunks(pe, body0)
            over_chunks(pe, body1)
            for t in range(2):
                post1_tensor(pe, CHUNKS - 1, t)

        def fast_scalar(act):
            norm_scalar(act)
            act.wait_ge(sem("norm"), 1)
            for b in range(BLOCKS):
                act.activation(tabv[0][0:LO, b, 0, :], h0[0:LO, b, :], ACT.Copy, scale=norm[0:LO, b:b + 1])\
                   .then_inc(sem("tab0_hi"), 1)
            over_chunks(act, lambda c, par: post0_scalar(act, c, 1 - par, fast_summed[0], True))
            over_chunks(act, lambda c, par: post1_scalar(act, c, par, fast_summed[1]))

        def build_all_gpsimd(gp):
            def add_bias(c, par):
                gp.wait_ge(sem("h0_done"), c + 1)
                a = x_sb[0:LO, blocks(c), :]
                gp.tensor_tensor(a, a, b0_sb[0:LO, :].unsqueeze(1).broadcast_to([LO, CB, D]), ALU.add)\
                  .then_inc(sem("x_b"), 1)
            over_chunks(gp, add_bias)

        def fast_gpsimd(gp):
            gp.wait_ge(sem("turned"), CHUNKS)
            gp.memset(tab[1].bitcast(I32), 0).then_inc(sem("tab1_zero"), 1)
            gp.wait_ge(sem("tab1_zero"), 1)
            over_chunks(gp, lambda c, par: post0_gpsimd(gp, c, True))

        def fast_vector(v):
            ch = Chain(v, sem("v_fast"))
            def reduced():
                v.wait_ge(sem("degrees"), 1)
                ch.did(v.tensor_reduce(deg[:, :], psDeg.rearrange("p (h n) -> p h n", n=10), AX, ALU.add))
            norm_vector(v, ch, reduced)
            v.memset(nmr[:, :], 0.0).then_inc(sem("norm"), 1)
            for b in range(BLOCKS):
                v.wait_ge(sem("tab0_hi"), b + 1)
                v.scalar_tensor_tensor(tabv[0][0:LO, b, 1, :], h0[0:LO, b, :], norm[0:LO, b:b + 1],
                                       tabv[0][0:LO, b, 0, :], ALU.mult, ALU.subtract).then_inc(sem("tab0"), 1)
            v.wait_ge(sem("x_b"), CHUNKS)
            spent = lambda n: positive(v, sem("tab_lo"), n)
            over_chunks(v, lambda c, par: post0_vector(v, c, ch, spent), ch, 7)
            over_chunks(v, lambda c, par: post1_vector(v, c, ch), ch, 3)

        def fast_sync(sp):
            sp.wait_ge(sem("tab1_zero"), 1)
            sp.wait_ge(sem("scaled"), 1)
            for k in range(TA):
                sp.dma_start(tabv[1][LO + k:LO + k + 1, BLOCKS:SLOTS, :, :],
                             embh[TB * k:TB * (k + 1), :, :]).then_inc(sem("emb_in"), 16)
            sp.wait_ge(sem("adj_out0"), 16)
            sp.wait_ge(sem("adj_out1"), 16 * (CHUNKS // 2))
            sp.wait_ge(sem("degree"), CHUNKS - 1)
            load_sync(sp, 0, 0, 0, 1)
            sp.wait_ge(sem("adj_out0"), 16 * ((CHUNKS + 1) // 2))
            sp.wait_ge(sem("degrees"), 1)
            load_sync(sp, 0, 1, 1, 0)
            load_sync(sp, 0, 2, 0, 1)
            with sp.Fori(0, (CHUNKS - 3) // 2) as i:
                load_sync(sp, 0, 2 * i + 3, 1, 0)
                load_sync(sp, 0, 2 * i + 4, 0, 1)
            over_chunks(sp, lambda c, par: load_sync(sp, 1, c, par, par), first=3)
            over_chunks(sp, lambda c, par: store_result(sp, c))
            sp.wait_ge(sem("emb_in"), 16 * TA)
            sp.wait_ge(sem("out"), 16 * CHUNKS)


        def general_sync(sp):
            sp.wait_ge(sem("adj_out0"), 16 * ((CHUNKS + 1) // 2))
            sp.wait_ge(sem("adj_out1"), 16 * (CHUNKS // 2))
            sp.wait_ge(sem("degrees"), 1)
            for k, a in enumerate((src, dst, typ)):
                sp.dma_start(flat_i[0:LO, k, :], a.rearrange("(p n) -> p n", p=LO)).then_inc(sem("flat_in"), 16)
            sp.wait_ge(sem("tab_zero"), 1)
            zero = tab[0].bitcast(F32)[0:LO, :][:, 0:(N + LO) // LO * D]
            for k in range(2):
                sp.dma_start(sum_d[k].rearrange("(p r) f -> p (r f)", p=LO), zero).then_inc(sem("sum_zero"), 16)
            sp.wait_ge(sem("scaled"), 1)
            sp.dma_start(emb_d, embs[:, :]).then_inc(sem("gemb_out"), 16)
            sp.wait_ge(sem("h0_scaled"), 1)
            sp.dma_start(table_v, h0[0:LO, :, :]).then_inc(sem("table_out"), 16)

            def sums_in(L, n):
                positive(sp, sem(f"gturned{L}"), n)
                sp.dma_start(sum_in[0:LO, :, :], sum_v[L][:, blocks(n), :]).then_inc(sem(f"sum_in{L}"), 16)

            def body0(n, par):
                sums_in(0, n)
                sp.wait_ge(sem("tbs"), n + 1)
                sp.dma_start(table_v[:, blocks(n), :], tbs[0:LO, :, :]).then_inc(sem("table1_out"), 16)

            sp.wait_ge(sem("gadded0"), 16 * PARTE)
            over_chunks(sp, body0)
            sp.wait_ge(sem("gadded1"), 16 * PARTE)

            def body1(n, par):
                sums_in(1, n)
                store_result(sp, n)

            over_chunks(sp, body1)
            sp.wait_ge(sem("out"), 16 * CHUNKS)

        def general_scalar(act):
            norm_scalar(act)
            done = lambda L: lambda eng, n: eng.wait_ge(sem(f"gturned{L}"), n + 1)
            over_chunks(act, lambda n, par: post0_scalar(act, n, par, done(0), False))
            over_chunks(act, lambda n, par: post1_scalar(act, n, par, done(1)))

        def general_gpsimd(gp):
            gp.wait_ge(sem("degrees"), 1)
            gp.memset(before[:, :], 1.0).then_inc(sem("g1"), 1)
            gp.memset(tab[0].bitcast(I32), 0).then_inc(sem("tab_zero"), 1)
            gp.wait_ge(sem("g1"), 1)
            gp.affine_select(out=before[:, :], in_=before[:, :], compare_op=ALU.is_gt, fill=0.0, base=0,
                             pattern=[[-1, 128]], channel_multiplier=1)
            gp.iota(trash_c, [[1, 1]], base=N, channel_multiplier=1,
                    allow_small_or_imprecise_dtypes=True).then_inc(sem("g1"), 1)
            gp.wait_ge(sem("sum_zero"), 32)
            gp.wait_ge(sem("gemb_out"), 16)
            for L in range(2):
                if L:
                    gp.wait_ge(sem("table1_out"), 16 * CHUNKS)
                else:
                    gp.wait_ge(sem("table_out"), 16)

                def tile(t):
                    gp.wait_ge(sem(f"gindex{L}"), t + 1)
                    gp.sem_inc(sem("g_seen"), 1)
                    gp.indirect_dma_start(rows_in[0:NE, :], None, table_d,
                                          bass.IndirectOffsetOnAxis(isrc[0:NE, :], 0)).then_inc(sem(f"grows{L}"), 16)
                    if L:
                        gp.indirect_dma_start(erows_in[0:NE, :], None, emb_d,
                                              bass.IndirectOffsetOnAxis(itype[0:NE, :], 0)).then_inc(sem("gerows"), 16)
                    gp.wait_ge(sem(f"gsums{L}"), t + 1)
                    gp.sem_inc(sem("g_seen"), 1)
                    gp.indirect_dma_start(sum_d[L], bass.IndirectOffsetOnAxis(idst[0:NE, :], 0),
                                          sums[0:NE, :], None, compute_op=ALU.add).then_inc(sem(f"gadded{L}"), 16)

                over_tiles(gp, tile)
                if L == 0:
                    over_chunks(gp, lambda n, par: post0_gpsimd(gp, n, False))

        def general_vector(v):
            ch = Chain(v, sem("v_general"))
            P = slice(0, LO)
            v.wait_ge(sem("flat_in"), 48)
            v.wait_ge(sem("g1"), 2)
            ch.did(v.tensor_copy(src_f[P, :], flat_i[P, 0, :]))
            ch.did(v.tensor_copy(dst_f[P, :], flat_i[P, 1, :]))
            ch.did(v.tensor_scalar(flat_i[P, 2, :], flat_i[P, 2, :], 0.0, float(TYPES - 1), ALU.max, ALU.min))
            ch.wait()
            block_of(v, ch, q_f[P, :], src_f[P, :])
            ch.did(v.scalar_tensor_tensor(lo_f[P, :], q_f[P, :], -float(LO), src_f[P, :], ALU.mult, ALU.add))
            ch.wait()
            with v.Fori(0, PARTE) as t:
                at = bass.ds(t, 1)
                v.wait_ge(sem("ghist"), t + 1)
                v.tensor_scalar(ghot[P, 0:LO], iota_lo[P, 0:LO], lo_f[P, at], None, ALU.is_equal)
                v.tensor_scalar(ghot[P, 128:128 + BLOCKS], iota_lo[P, 0:BLOCKS], q_f[P, at], None, ALU.is_equal)\
                 .then_inc(sem("ghot"), 1)

            def reduced():
                v.wait_ge(sem("ghist"), PARTE + 2)
                ch.did(v.tensor_copy(deg[P, :], psDeg[P, 0:BLOCKS]))
            norm_vector(v, ch, reduced)
            v.wait_ge(sem("h0_done"), CHUNKS)
            v.tensor_tensor(h0[P, :, :], h0[P, :, :], spread(norm[P, :], [LO, BLOCKS, D]), ALU.mult)\
             .then_inc(sem("h0_scaled"), 1)
            v.wait_ge(sem("x_b"), CHUNKS)
            for L in range(2):
                def tile(t):
                    at = bass.ds(t, 1) if not isinstance(t, int) else slice(t, t + 1)
                    positive(v, sem(f"gadded{L}"), 16 * t)
                    v.tensor_copy(itype[P, :], flat_i[P, 2, at])
                    v.tensor_copy(isrc[P, :], flat_i[P, 0, at]).then_inc(sem(f"gindex{L}"), 1)
                    v.tensor_scalar(diag[P, 0:NE], ident[P, 0:NE], dst_f[P, at], None, ALU.mult)\
                     .then_inc(sem(f"gdiag{L}"), 1)
                    v.wait_ge(sem(f"gacross{L}"), t + 1)
                    v.tensor_scalar(same[P, 0:NE], psB[P, 0:NE], dst_f[P, at], None, ALU.is_equal)\
                     .then_inc(sem(f"gsame{L}"), 1)
                    v.wait_ge(sem(f"gsame{L}"), t + 1)
                    ch.did(v.tensor_tensor(lower[P, 0:NE], same[P, 0:NE], before[P, 0:NE], ALU.mult))
                    ch.wait()
                    ch.did(v.tensor_reduce(count_c[P, :], lower[P, 0:NE], AX, ALU.max))
                    ch.did(v.tensor_tensor(toward_c[P, :], trash_c[P, :], dst_f[P, at], ALU.subtract))
                    ch.wait()
                    ch.did(v.tensor_tensor(dup_c[P, :], toward_c[P, :], count_c[P, :], ALU.mult))
                    ch.wait()
                    ch.did(v.tensor_tensor(idst[P, :], dup_c[P, :], dst_f[P, at], ALU.add))
                    v.wait_ge(sem(f"gproduct{L}"), t + 1)
                    ch.wait()
                    v.tensor_copy(sums[P, :], psS[P, :]).then_inc(sem(f"gsums{L}"), 1)

                over_tiles(v, tile, ch, 5)
                if L:
                    v.wait_ge(sem("h1T"), CHUNKS)
                if L == 0:
                    spent = lambda n: positive(v, sem("table1_out"), 16 * n)
                    over_chunks(v, lambda n, par: post0_vector(v, n, ch, spent), ch, 7)
                else:
                    over_chunks(v, lambda n, par: post1_vector(v, n, ch), ch, 3)

        def general_tensor(pe):
            psHist = ps[0:LO, 6, 0:BLOCKS]
            pe.matmul(psHist, zeroh[0:LO, 0:LO], zeroh[0:LO, 0:BLOCKS], start=True, stop=False,
                      skip_group_check=True).then_inc(sem("ghist"), 1)
            with pe.Fori(0, PARTE) as t:
                pe.wait_ge(sem("ghot"), t + 1)
                pe.matmul(psHist, ghot[0:LO, 0:LO], ghot[0:LO, 128:128 + BLOCKS], start=False, stop=False,
                          skip_group_check=True).then_inc(sem("ghist"), 1)
            pe.matmul(psHist, zeroh[0:LO, 0:LO], zeroh[0:LO, 0:BLOCKS], start=False, stop=True,
                      skip_group_check=True).then_inc(sem("ghist"), 1)
            for L, post, steps in ((0, post0_tensor, 3), (1, post1_tensor, 2)):
                def tile(t):
                    pe.wait_ge(sem(f"gdiag{L}"), t + 1)
                    pe.matmul(psB[0:NE, 0:NE], ones[0:NE, 0:NE], diag[0:NE, 0:NE], start=True, stop=True)\
                      .then_inc(sem(f"gacross{L}"), 1)
                    pe.wait_ge(sem(f"gsame{L}"), t + 1)
                    pe.wait_ge(sem(f"grows{L}"), 16 * t + 16)
                    last = pe.matmul(psS[0:NE, :], same[0:NE, 0:NE], rows_in[0:NE, :], start=True, stop=L == 0)
                    if L:
                        pe.wait_ge(sem("gerows"), 16 * t + 16)
                        last = pe.matmul(psS[0:NE, :], same[0:NE, 0:NE], erows_in[0:NE, :], start=False, stop=True)
                    last.then_inc(sem(f"gproduct{L}"), 1)

                over_tiles(pe, tile)

                if L:
                    pe.wait_ge(sem("h1T"), CHUNKS)

                def body(n, par):
                    pe.wait_ge(sem(f"sum_in{L}"), 16 * n + 16)
                    for j in range(CB):
                        last = pe.transpose(psD[par][:, LO * j:LO * (j + 1)], sum_in[0:LO, j, :], ident[0:LO, 0:LO])
                    last.then_inc(sem(f"gturned{L}"), 1)
                    for k in range(steps):
                        post(pe, n, k)

                over_chunks(pe, body)

        block = ctx.enter_context(nc.Block())

        def branch(eng, fast, general):
            eng.wait_ge(sem("flag_set"), 1)
            flag = eng.value_load(flag_i[0:1, 0:1], min_val=0, max_val=1)
            with eng.If(flag == 0):
                fast(eng)
            with eng.Else():
                general(eng)

        @block.sync
        def _(sp):
            prepare_sync(sp)
            over_chunks(sp, lambda c, par: build_sync(sp, c, par), first=3)
            branch(sp, fast_sync, general_sync)

        @block.scalar
        def _(act):
            prepare_scalar(act)
            turn_scalar(act, 0, 0)
            over_chunks(act, lambda c, par: build_scalar(act, c, par), first=3, last=2)
            branch(act, fast_scalar, general_scalar)

        @block.gpsimd
        def _(gp):
            prepare_gpsimd(gp)
            build_all_gpsimd(gp)
            branch(gp, fast_gpsimd, general_gpsimd)

        @block.vector
        def _(v):
            ch = Chain(v, sem("v_prep"))
            prepare_vector(v, ch)
            build_all_vector(v, ch)
            branch(v, fast_vector, general_vector)

        @block.tensor
        def _(pe):
            prepare_tensor(pe)
            build_all_tensor(pe)
            branch(pe, fast_tensor, general_tensor)


def kernel(x, src, dst, edge_type_9, L0_gnn_W, L0_gnn_b, L1_gnn_W_msg, L1_gnn_b_msg, L1_gnn_edge_embed,
           L1_gnn_W_ih, L1_gnn_W_hh, L1_gnn_b_ih, L1_gnn_b_hh):
    import concourse.bacc as bacc
    from concourse.bass_utils import run_bass_kernel_spmd

    turned = lambda a: np.ascontiguousarray(np.asarray(a).T)
    by_gate = lambda a: np.ascontiguousarray(np.asarray(a).reshape(3, D).T)
    arrays = {
        "x": np.asarray(x), "src": np.asarray(src), "dst": np.asarray(dst), "typ": np.asarray(edge_type_9),
        "w0t": turned(L0_gnn_W), "b0": np.asarray(L0_gnn_b), "wmt": turned(L1_gnn_W_msg),
        "bm": np.asarray(L1_gnn_b_msg), "emb": np.asarray(L1_gnn_edge_embed), "wiht": turned(L1_gnn_W_ih),
        "whht": turned(L1_gnn_W_hh), "bih": by_gate(L1_gnn_b_ih), "bhh": by_gate(L1_gnn_b_hh),
    }
    nc = bacc.Bacc("TRN2", target_bir_lowering=False, num_devices=1)
    args = [nc.dram_tensor(n, a.shape, mybir.dt.from_np(a.dtype), kind="ExternalInput").ap()
            for n, a in arrays.items()]
    out = nc.dram_tensor("out", (N, D), F32, kind="ExternalOutput").ap()
    gnn(nc, *args, out)
    r = run_bass_kernel_spmd(nc, [arrays], core_ids=[0])
    return r.results[0]["out"]
```

```python
import numpy as np
from contextlib import ExitStack, contextmanager

import concourse.bass as bass
from concourse import mybir

F32, F16, I32, I16 = mybir.dt.float32, mybir.dt.float16, mybir.dt.int32, mybir.dt.int16
ALU = mybir.AluOpType
ACT = mybir.ActivationFunctionType
AX = mybir.AxisListType.X

N, D, E, TYPES = 6250, 128, 206250, 9
LO = 125
BLOCKS = N // LO
EPS = 1e-5

CH = 250
CHUNKS = N // CH
CB = CH // LO

WIN = 2
CHWIN = CH // WIN
WINDOWS = N // WIN
EDGES_MAX = 128
TA, TB = 3, 3
SLOTS = BLOCKS + TB
WCOLS = WIN * SLOTS
BATCH = 25
BATCHES = CHWIN // BATCH
BANKW = 4
UNIT = 2 * BANKW
UNITS = (CHWIN + UNIT - 1) // UNIT
PSLOTS = 3

PARTE = E // LO
HEADS, HLEN = 1250, 165
HPART = HEADS // LO
SB = 5
STEPS = CHUNKS // SB
NOWHERE = 8191
MAGIC = 12582912.0
HSCALE = 4096.0
PARTS = [(0, 14), (14, 27), (27, 40), (40, SLOTS)]


SEMAPHORES = """
heads_in col_set dst_in x_in0 x_in1 x_in2 x_in3 x_in4 weights_in sq_sum eps_set
wm_norm sums0 mean0 var0 std0 nmr0 h0_done turned consts thresholds compared counted squares scaled g_col
flags flag_sum fields g0 rows_i0 rows_i1 rows_i2 rows_i3 rows_i4 cand_in0 cand_in1 cand_in2 cand_in3 cand_in4
run_i runs_in0 runs_in1 runs_in2 runs_in3 g_unpack x_b v_prep flag_set x1 aggr psX hst h1 psT tbs psM pvar pstd
pnm h1T tab_hi x1_kept tab_lo msg rz nin psRZ psN hnew result psO nn out deg deg_root onehot evac built degree
adj_out0 adj_out1 mch used0 used1 spent degrees tab0 tab0_hi emb_in norm tab1_zero v_fast v_general g_seen
flat_in tab_zero sum_zero gemb_out h0_scaled table_out table1_out g1 ghist ghot gerows gturned0 gturned1
sum_in0 sum_in1 gadded0 gadded1 gindex0 gindex1 grows0 grows1 gsums0 gsums1 gdiag0 gdiag1 gacross0 gacross1
gsame0 gsame1 gproduct0 gproduct1 load0_0_0
load0_0_1 load0_0_2 load0_0_3 load0_1_0 load0_1_1 load0_1_2 load0_1_3 load1_0_0 load1_0_1 load1_0_2 load1_0_3
load1_1_0 load1_1_1 load1_1_2 load1_1_3
""".split()


class Chain:

    def __init__(self, eng, sem):
        self.eng, self.sem, self.base, self.k = eng, sem, 0, 0

    def did(self, ins):
        ins.then_inc(self.sem, 1)
        self.k += 1
        return ins

    def wait(self, but=0):
        self.eng.wait_ge(self.sem, self.base + self.k - but)

    @contextmanager
    def loop(self, i, times, steps):
        before = self.base + self.k
        self.base, self.k = before + steps * i, 0
        yield
        assert self.k == steps, (self.k, steps)
        self.base, self.k = before + steps * times, 0


def over_chunks(eng, body, chain=None, steps=0, first=1, last=0):
    def pair(i):
        body(2 * i + first, 1)
        body(2 * i + first + 1, 0)

    for c in range(first):
        body(c, c % 2)
    n = (CHUNKS - first - last) // 2
    with eng.Fori(0, n) as i:
        if chain is not None:
            with chain.loop(i, n, 2 * steps):
                pair(i)
        else:
            pair(i)
    for c in range(CHUNKS - last, CHUNKS):
        body(c, c % 2)


def over_tiles(eng, body, chain=None, steps=0):
    body(0)
    with eng.Fori(0, PARTE - 1) as i:
        if chain is not None:
            with chain.loop(i, PARTE - 1, steps):
                body(i + 1)
        else:
            body(i + 1)


def positive(eng, sem, value):
    if not isinstance(value, int) or value > 0:
        eng.wait_ge(sem, value)


def gnn(nc, x, src, dst, typ, w0t, b0, wmt, bm, emb, wiht, whht, bih, bhh, out):
    ctx = ExitStack()
    sems = {name: ctx.enter_context(nc.semaphore(name)) for name in SEMAPHORES}

    def sem(name):
        return sems[name]

    def sb(name, shape, dt):
        return ctx.enter_context(nc.sbuf_tensor(name, shape, dt))

    def dram(name, shape, dt):
        return nc.dram_tensor(name, shape, dt).ap()

    with ctx:
        adj_d = dram("adjacency", (CHUNKS, 128, SLOTS * CH), F16)
        table_d = dram("rows", (N, D), F32)
        sum_d = [dram(f"row_sums{L}", (N + LO, D), F32) for L in range(2)]
        emb_d = dram("scaled_embedding", (TYPES, D), F32)

        x_sb = sb("x_sb", [128, BLOCKS, D], F32)
        h_sb = sb("h_sb", [128, BLOCKS * D], F32)
        h0 = h_sb[:, :].rearrange("p (b f) -> p b f", f=D)
        h1T = h_sb[:, 0:N]
        ring = sb("ring", [128, 2, SLOTS * CH], F16)
        adj = [ring[:, k, :].rearrange("p (h n) -> p h n", n=CH) for k in range(2)]
        TW = SLOTS * 2 * D
        tabs = sb("tabs", [128, 2 * TW], F16)
        tab = [tabs[:, k * TW:(k + 1) * TW] for k in range(2)]
        tabv = [t.rearrange("p (h s f) -> p h s f", s=2, f=D) for t in tab]
        HOT = 128 + WCOLS
        work = sb("work", [128, BATCH * HOT], F32)
        hot = work[:, :].bitcast(F16).rearrange("p (s k n) -> p s k n", s=2, k=BATCH)
        lohot = hot[:, :, :, 0:128]
        combo = hot[:, :, :, 128:HOT]
        typehot = hot[:, :, :, LO - BLOCKS:HOT].rearrange("p s k (m h) -> p s k m h", h=SLOTS)[:, :, :, :, BLOCKS:SLOTS]
        ring32 = ring[:, :, :].rearrange("p a n -> p (a n)").bitcast(I32)

        RUNW = CHUNKS * 3 * EDGES_MAX
        tabs32 = tabs[:, :].bitcast(F32)
        runs = tabs32[:, 0:RUNW].bitcast(I32).rearrange("p (g k e) -> p g k e", g=CHUNKS, k=3)
        fields = tabs32[:, 0:RUNW].bitcast(F16).rearrange("p (g k e) -> p g k e", g=CHUNKS, k=6)
        F_TA, F_SMALL, F_LO, F_COL = range(4)
        UW = (SB - 2) * EDGES_MAX
        unp = tabs32[:, RUNW:RUNW + 8 * UW].rearrange("p (k n) -> p k n", k=8)

        mch = sb("mch", [128, 2, 2, CHWIN, 2], F16)
        mch_s = sb("mch_s", [128, 2, 1 + WIN, CHWIN], F16)
        iota_w = sb("iota_w", [128, WCOLS], F16)
        iota_lo = sb("iota_lo", [128, 128], F16)
        iota_t = sb("iota_t", [128, 1 + WIN, TB], F16)
        ident = sb("ident", [128, 128], F32)
        identh = sb("identh", [128, 128], F16)
        zeroh = sb("zeroh", [128, 512], F16)
        ghot = sb("ghot", [128, 192], F16)
        ones = sb("ones", [128, 128], F32)
        thr = sb("thr", [128, CHUNKS], F32)
        thr16 = work[:, 0:(WINDOWS + 1) // 2].bitcast(I16)[:, 0:WINDOWS]
        heads_i = sb("heads_i", [LO, HPART], I32)
        heads = sb("heads", [LO, HPART], F32)
        onesh = sb("onesh", [128, 1], F16)
        cnt = sb("cnt", [128, CHUNKS], F32)
        row = sb("row", [128, CHUNKS], F32)
        row_i = sb("row_i", [128, CHUNKS], I32)
        run0 = sb("run0", [128, CHUNKS], F32)
        run_i = sb("run_i", [128, CHUNKS], I32)
        two_runs = sb("two_runs", [128, 2, 3, EDGES_MAX], F32)
        two_fields = sb("two_fields", [128, 2, 4, EDGES_MAX], F16)
        two = sb("two", [128, 3, 2], F32)
        inside = sb("inside", [128, CHUNKS], F32)
        over = sb("over", [128, CHUNKS], F32)
        flags = sb("flags", [128, 4], F32)
        flag_i = sb("flag_i", [1, 1], I32)
        xsum = sb("xsum", [128, BLOCKS], F32)
        xvar = sb("xvar", [128, BLOCKS], F32)
        nmean = sb("nmean", [128, BLOCKS], F32)
        rstd = sb("rstd", [128, BLOCKS], F32)
        nmr = sb("nmr", [128, BLOCKS], F32)
        epst = sb("epst", [128, 1], F32)
        deg = sb("deg", [128, BLOCKS], F32)
        norm = sb("norm", [128, BLOCKS], F32)
        w0_sb = sb("w0_sb", [128, D], F32)
        b0_sb = sb("b0_sb", [128, D], F32)
        wm_sb = sb("wm_sb", [128, D], F32)
        bm_sb = sb("bm_sb", [128, D], F32)
        wih_sb = sb("wih_sb", [128, 3 * D], F32)
        whh_sb = sb("whh_sb", [128, 3 * D], F32)
        bg_i = sb("bg_i", [128, 3], F32)
        bg_h = sb("bg_h", [128, 3], F32)
        bg = sb("bg", [128, 2], F32)
        gsc = sb("gsc", [128, D], F32)
        ginv = sb("ginv", [128, 1], F32)
        embs = sb("embs", [TYPES, D], F32)
        embh = sb("embh", [TYPES, 2, D], F16)
        pst = sb("pst", [128, CB, 6], F32)
        pmv = sb("pmv", [128, CB, 2], F32)
        pm2 = sb("pm2", [128, CB], F32)
        prs = sb("prs", [128, CB], F32)
        pnm = sb("pnm", [128, CB], F32)

        SW = SB * CHWIN
        compared = ring[:, 0, 0:2 * HPART * SW].rearrange("p (s j n) -> p s j n", s=2, j=HPART)
        second = ring32[:, SLOTS * CH // 2:SLOTS * CH]
        cand = second[:, 0:CHUNKS * HLEN].rearrange("p (g n) -> p g n", g=CHUNKS)
        raw_dst = second[:, CHUNKS * HLEN:CHUNKS * HLEN + PARTE + 1]
        at = CHUNKS * HLEN + PARTE + 1
        below = second[:, at:at + (SB * HLEN + 1) // 2].bitcast(F16)[:, 0:SB * HLEN].rearrange("p (g n) -> p g n", g=SB)
        unsorted = tabs32[:, RUNW:RUNW + PARTE]

        def carve(words, at, *shape):
            n = int(np.prod(shape))
            a = words[:, at:at + n]
            if len(shape) > 1:
                a = a.rearrange("p (a b) -> p a b", a=shape[0])
            return a, at + n

        emb_sb, at = carve(work, (WINDOWS + 1) // 2, TYPES, D)
        sq, at = carve(work, at, D)
        gtmp, at = carve(work, at, D)
        late = work
        x1s, at = carve(late, 2048, CB, D)
        h1s, at = carve(late, at, CB, D)
        tbs, at = carve(late, at, CB, D)
        rz, at = carve(late, at, 2, CH)
        aggr, at = carve(late, at, CH)
        hst, at = carve(late, at, CH)
        msgs, at = carve(late, at, CH)
        nin, at = carve(late, at, CH)
        nn, at = carve(late, at, CH)
        hnew, at = carve(late, at, CH)

        ps = ctx.enter_context(nc.psum_tensor("ps", [128, 8, 512], F32))
        psD = [ps[:, k, 0:CH] for k in range(2)]
        psX = ps[0:LO, 2, 0:CB * D].rearrange("p (b f) -> p b f", f=D)
        psT = ps[:, 3, 0:CH]
        psM = ps[0:LO, 4, 0:CB * D].rearrange("p (b f) -> p b f", f=D)
        psRZ = ps[:, 2, :].rearrange("p (a n) -> p a n", a=2)[:, :, 0:CH]
        psN = ps[:, 3, :].rearrange("p (a n) -> p a n", a=2)[:, :, 0:CH]
        psO = psM
        psDeg = ps[:, 6, 0:BLOCKS * 10]
        psG = ps[:, 0, SB:SB + 1]
        psCnt = [ps[0:LO, k, 0:SB] for k in range(STEPS)]
        psTurn = ps[:, 7, 0:4 * CHWIN].rearrange("p (k w) -> p k w", k=4)
        psFlag = ps[0:1, 7, 508:509]

        x_v = x.rearrange("(b p) f -> p b f", p=LO)
        out_v = out.rearrange("(b p) f -> p b f", p=LO)
        table_v = table_d.rearrange("(b p) f -> p b f", p=LO)
        XP = 5
        XB = BLOCKS // XP

        flat_i = ring32[:, 0:3 * PARTE].rearrange("p (a n) -> p a n", a=3)
        flat_f = ring32[:, 3 * PARTE:7 * PARTE].bitcast(F32).rearrange("p (a n) -> p a n", a=4)
        src_f, dst_f, q_f, lo_f = (flat_f[:, k, :] for k in range(4))
        gbuf = work[:, 0:2048]
        cut = lambda k, n: gbuf[:, 128 * k:128 * k + n]
        rows_in, erows_in, diag, same, lower, sums, before = (cut(k, 128) for k in range(7))
        small = cut(7, 8)
        count_c, dup_c, toward_c, trash_c = (small[:, k:k + 1] for k in range(4))
        ints = cut(8, 8).bitcast(I32)
        isrc, itype, idst = (ints[:, k:k + 1] for k in range(3))
        sum_in = cut(9, 256).rearrange("p (b f) -> p b f", f=D)
        psB = ps[:, 5, 0:128]
        psS = ps[:, 7, 0:128]
        NE = LO
        sum_v = [sum_d[L][0:N, :].rearrange("(b p) f -> p b f", p=LO) for L in range(2)]

        def spread(a, shape):
            return a.unsqueeze(2).broadcast_to(shape)


        RUNS_PART = ["0"] * 2 + ["1"] * (SB - 2) + ["2"] * SB + ["3"] * (CHUNKS - 2 * SB)

        def prepare_sync(sp):
            sp.dma_start(heads_i[:, :], dst.rearrange("(p j n) -> p j n", j=HPART, n=HLEN)[:, :, 0:1]
                         .rearrange("p j n -> p (j n)"), allow_slow_non_contiguous=True).then_inc(sem("heads_in"), 16)
            sp.wait_ge(sem("col_set"), 1)
            halo = bass.AP(tensor=dst.tensor, offset=dst.offset, ap=[[PARTE, LO - 1], [1, PARTE + 1]])
            sp.dma_start(raw_dst[0:LO - 1, :], halo).then_inc(sem("dst_in"), 16)
            sp.dma_start(raw_dst[LO - 1:LO, 0:PARTE], dst.rearrange("(p n) -> p n", p=LO)[LO - 1:LO, :])\
              .then_inc(sem("dst_in"), 16)

        def prepare_scalar(act):
            P = slice(0, LO)
            for k in range(XP):
                act.dma_start(x_sb[0:LO, k * XB:(k + 1) * XB, :], x_v[:, k * XB:(k + 1) * XB, :])\
                   .then_inc(sem(f"x_in{k}"), 16)
            for to, a in ((w0_sb, w0t), (wm_sb, wmt), (wih_sb, wiht), (whh_sb, whht), (bg_i, bih), (bg_h, bhh),
                          (embs, emb)):
                act.dma_start(to[:, :], a).then_inc(sem("weights_in"), 16)
            for to, a in ((b0_sb[:, :], b0), (bm_sb[:, :], bm),
                          (emb_sb[:, :, :].rearrange("p t f -> p (t f)"), emb.rearrange("t f -> (t f)"))):
                act.dma_start(to, a.partition_broadcast(128)).then_inc(sem("weights_in"), 16)
            for k in range(XP):
                act.wait_ge(sem(f"x_in{k}"), 16)
                for b in range(k * XB, (k + 1) * XB):
                    last = act.activation(h0[P, b, :], x_sb[P, b, :], ACT.Copy, accum_out=xsum[P, b:b + 1])
            last.then_inc(sem("sums0"), 1)
            act.wait_ge(sem("sums0"), 1)
            act.activation(nmean[P, :], xsum[P, :], ACT.Copy, scale=-1.0 / D).then_inc(sem("mean0"), 1)
            act.wait_ge(sem("sq_sum"), 1)
            act.activation(gsc[:, :], psB, ACT.Sqrt).then_inc(sem("wm_norm"), 1)
            act.wait_ge(sem("mean0"), 1)
            for b in range(BLOCKS):
                if b == 35:
                    turn_scalar(act, 0, 0)
                last = act.activation(h0[P, b, :], x_sb[P, b, :], ACT.Square, bias=nmean[P, b:b + 1],
                                      accum_out=xvar[P, b:b + 1])
            last.then_inc(sem("var0"), 1)
            act.wait_ge(sem("var0"), 1)
            act.wait_ge(sem("eps_set"), 1)
            act.activation(rstd[P, :], xvar[P, :], ACT.Sqrt, bias=epst[P, :], scale=1.0 / D).then_inc(sem("std0"), 1)

        def prepare_tensor(pe):
            pe.wait_ge(sem("consts"), 1)
            for m in range(STEPS):
                pe.wait_ge(sem("compared"), m + 1)
                for g in range(SB):
                    for j in range(HPART):
                        last = pe.matmul(psCnt[m][:, g:g + 1],
                                         compared[0:LO, m % 2, j, CHWIN * g:CHWIN * (g + 1)], onesh[0:LO, :],
                                         start=j == 0, stop=j == HPART - 1)
                last.then_inc(sem("counted"), 1)
                if m == 2:
                    pe.wait_ge(sem("squares"), 1)
                    pe.matmul(psB, ones[:, :], sq[:, :], start=True, stop=True).then_inc(sem("sq_sum"), 1)
            turn_tensor(pe, 0)
            pe.wait_ge(sem("scaled"), 1)
            pe.matmul(psG, gsc[0:1, :], ones[0:1, 0:1], start=True, stop=True).then_inc(sem("g_col"), 1)

        def prepare_gpsimd(gp):
            gp.iota(thr16, [[WIN, WINDOWS]], base=0, channel_multiplier=0).then_inc(sem("thresholds"), 1)
            gp.memset(onesh[:, :], 1.0)
            gp.memset(raw_dst[:, PARTE:PARTE + 1], NOWHERE).then_inc(sem("col_set"), 1)
            gp.memset(ones[:, :], 1.0)
            gp.memset(ident[:, :], 0.0).then_inc(sem("g0"), 1)
            gp.memset(zeroh[:, :], 0.0)
            gp.wait_ge(sem("g0"), 1)
            gp.affine_select(out=ident[:, :], in_=ident[:, :], compare_op=ALU.not_equal, fill=1.0, base=0,
                             pattern=[[-1, 128]], channel_multiplier=1).then_inc(sem("g0"), 1)
            gp.iota(thr[:, :], [[CH, CHUNKS]], base=0, channel_multiplier=WIN, allow_small_or_imprecise_dtypes=True)
            gp.iota(iota_w[:, :], [[1, WCOLS]], base=0, channel_multiplier=0, allow_small_or_imprecise_dtypes=True)
            gp.iota(iota_lo[:, :], [[1, 128]], base=0, channel_multiplier=0, allow_small_or_imprecise_dtypes=True)
            gp.iota(iota_t[:, 0, :], [[1, TA]], base=0, channel_multiplier=0, allow_small_or_imprecise_dtypes=True)
            gp.iota(iota_t[:, 1:1 + WIN, :], [[TB, WIN], [1, TB]], base=0, channel_multiplier=0,
                    allow_small_or_imprecise_dtypes=True)
            gp.wait_ge(sem("g0"), 2)
            gp.tensor_copy(identh[:, :], ident[:, :]).then_inc(sem("consts"), 1)

            def elements(a):
                return a.rearrange("(a n) -> a n", a=1)

            def candidates(m):
                gp.wait_ge(sem(f"rows_i{m}"), 1)
                for g in range(SB * m, SB * (m + 1)):
                    gp.indirect_dma_start(cand[0:LO, g, :], None, elements(dst),
                                          bass.IndirectOffsetOnAxis(row_i[0:LO, g:g + 1], 1))\
                      .then_inc(sem(f"cand_in{m}"), 16)

            def run_edges(m):
                gp.wait_ge(sem("run_i"), m + 1)
                for g in range(SB * m, SB * (m + 1)):
                    for k, a in enumerate((src, dst, typ)):
                        gp.indirect_dma_start(runs[0:LO, g, k, :], None, elements(a),
                                              bass.IndirectOffsetOnAxis(run_i[0:LO, g:g + 1], 1))\
                          .then_inc(sem("runs_in" + RUNS_PART[g]), 16)

            candidates(0)
            run_edges(0)
            for m in range(1, STEPS):
                candidates(m)
            for m in range(1, STEPS):
                run_edges(m)

        def search_scalars(v, ch, m):
            P, at = slice(0, LO), slice(SB * m, SB * (m + 1))
            v.wait_ge(sem("counted"), m + 1)
            ch.did(v.tensor_scalar(row[P, at], psCnt[m], -1.0, 0.0, ALU.add, ALU.max))
            ch.wait()
            ch.did(v.tensor_scalar(row[P, at], row[P, at], float(HLEN), None, ALU.mult))
            ch.wait()
            v.tensor_copy(row_i[P, at], row[P, at]).then_inc(sem(f"rows_i{m}"), 1)

        def search_runs(v, ch, m):
            P, at = slice(0, LO), slice(SB * m, SB * (m + 1))
            v.wait_ge(sem(f"cand_in{m}"), 16 * SB)
            ch.did(v.tensor_tensor(below[P, :, :], cand[P, at, :], spread(thr[P, at], [LO, SB, HLEN]), ALU.is_lt))
            ch.wait()
            ch.did(v.tensor_reduce(cnt[P, at], below[P, :, :], AX, ALU.add))
            ch.wait()
            ch.did(v.tensor_tensor(run0[P, at], row[P, at], cnt[P, at], ALU.add))
            ch.wait()
            ch.did(v.tensor_scalar(run0[P, at], run0[P, at], float(E - EDGES_MAX), None, ALU.min))
            ch.wait()
            ch.did(v.tensor_scalar(inside[P, at], run0[P, at], float(E - EDGES_MAX), None, ALU.is_lt))
            v.tensor_copy(run_i[P, at], run0[P, at]).then_inc(sem("run_i"), 1)

        def unpack(eng, ch, n, edges, first, fields_of, over_of, inside_of, wait):
            P = slice(0, LO)
            t0, t1, t2, t3, t4, u0, u1, u2 = (
                unp[P, k, 0:n * EDGES_MAX].rearrange("p (g e) -> p g e", g=n) for k in range(8))
            fused = eng is nc.vector

            def step(*ops):
                for (o, a, scalar, b, op0, op1), u in zip(ops, (u0, u1, u2)):
                    if fused:
                        ch.did(eng.scalar_tensor_tensor(o, a, scalar, b, op0, op1))
                    else:
                        ch.did(eng.tensor_scalar(u[:, :, 0:a.shape[-1]], a, scalar, None, op0))
                wait()
                if not fused:
                    for (o, a, scalar, b, op0, op1), u in zip(ops, (u0, u1, u2)):
                        ch.did(eng.tensor_tensor(o, u[:, :, 0:a.shape[-1]], b, op1))
                    wait()

            ch.did(eng.tensor_scalar(t0, edges[:, :, 0, :], 1.0 / LO, 0.5 / LO - 0.5, ALU.mult, ALU.add))
            for k in range(n):
                ch.did(eng.tensor_scalar(t2[:, k, :], edges[:, k, 1, :], first[:, k:k + 1], -1.0,
                                         ALU.subtract, ALU.max))
            ch.did(eng.tensor_scalar(t3, edges[:, :, 2, :], 0.0, float(TYPES - 1), ALU.max, ALU.min))
            wait()
            ch.did(eng.tensor_scalar(t0, t0, MAGIC, MAGIC, ALU.add, ALU.subtract))
            ch.did(eng.tensor_scalar(t2, t2, float(WIN), None, ALU.min))
            ch.did(eng.tensor_scalar(t4, t3, float(TB), None, ALU.is_ge))
            wait()
            step((t1, t0, -float(LO), edges[:, :, 0, :], ALU.mult, ALU.add),
                 (fields_of(F_COL), t2, float(SLOTS), t0, ALU.mult, ALU.add),
                 (t4, t3, float(2 * TB), t4, ALU.is_ge, ALU.add))
            ch.did(eng.tensor_copy(fields_of(F_LO), t1))
            ch.did(eng.tensor_copy(fields_of(F_TA), t4))
            step((t3, t4, -float(TB), t3, ALU.mult, ALU.add),
                 (over_of, t2[:, :, EDGES_MAX - 1:EDGES_MAX], float(WIN), inside_of, ALU.is_lt, ALU.mult))
            step((fields_of(F_SMALL), t2, float(TB), t3, ALU.mult, ALU.add))

        def unpack_vector(v, ch, g, n):
            P, at = slice(0, LO), slice(g, g + n)
            unpack(v, ch, n, runs[P, at, :, :], thr[P, at], lambda k: fields[P, at, k, :],
                   over[P, at].unsqueeze(2), inside[P, at].unsqueeze(2), ch.wait)
            v.sem_inc(sem("fields"), n)

        UNPACK_STEPS = 3 + 4 + 3 + 6 + 2 + 4 + 2 + 2

        def unpack_gpsimd(gp, ch, g):
            P, at = slice(0, LO), bass.ds(g, 2)

            def wait():
                ch.wait()
                gp.sem_inc(sem("g_seen"), 1)
            ch.did(gp.tensor_copy(two_runs[P, :, :, :], runs[P, at, :, :]))
            ch.did(gp.tensor_copy(two[P, 0, :], thr[P, at]))
            ch.did(gp.tensor_copy(two[P, 1, :], inside[P, at]))
            wait()
            unpack(gp, ch, 2, two_runs[P, :, :, :], two[P, 0, :], lambda k: two_fields[P, :, k, :],
                   two[P, 2, :].unsqueeze(2), two[P, 1, :].unsqueeze(2), wait)
            ch.did(gp.tensor_copy(over[P, at], two[P, 2, :]))
            ch.did(gp.tensor_copy(fields[P, at, 0:4, :], two_fields[P, :, :, :]))
            wait()
            gp.sem_inc(sem("fields"), 2)

        def prepare_vector(v, ch):
            P = slice(0, LO)
            v.memset(epst[:, :], EPS).then_inc(sem("eps_set"), 1)
            v.wait_ge(sem("heads_in"), 16)
            ch.did(v.tensor_copy(heads[:, :], heads_i[:, :]))
            v.wait_ge(sem("thresholds"), 1)
            ch.wait()
            def compare(m):
                if m >= 2:
                    v.wait_ge(sem("counted"), m - 1)
                for j in range(HPART):
                    last = v.tensor_scalar(compared[P, m % 2, j, :], thr16[P, SW * m:SW * (m + 1)],
                                           heads[P, j:j + 1], None, ALU.is_gt)
                last.then_inc(sem("compared"), 1)
            compare(0)
            compare(1)
            search_scalars(v, ch, 0)
            compare(2)
            search_scalars(v, ch, 1)
            v.wait_ge(sem("consts"), 1)
            search_runs(v, ch, 0)
            v.wait_ge(sem("weights_in"), 160)
            v.tensor_tensor(sq[:, :], wm_sb[:, :], wm_sb[:, :], ALU.mult).then_inc(sem("squares"), 1)
            compare(3)
            search_scalars(v, ch, 2)
            compare(4)
            check_sorted(v, ch)
            search_scalars(v, ch, 3)
            v.wait_ge(sem("runs_in0"), 16 * 3 * 2)
            unpack_vector(v, ch, 0, 2)
            search_scalars(v, ch, 4)

        def scale_vector(v, ch):
            v.wait_ge(sem("sq_sum"), 1)
            ch.did(v.tensor_reduce(gtmp[:, :], emb_sb[:, :, :].rearrange("p t f -> p f t"), AX, ALU.max,
                                   apply_absolute_value=True))
            ch.did(v.scalar_tensor_tensor(sq[:, :], bm_sb[:, :], -1.0, bm_sb[:, :], ALU.mult, ALU.max))
            ch.wait()
            ch.did(v.tensor_tensor(gtmp[:, :], gtmp[:, :], sq[:, :], ALU.add))
            v.wait_ge(sem("wm_norm"), 1)
            ch.wait()
            ch.did(v.scalar_tensor_tensor(gsc[:, :], gsc[:, :], 11.4, gtmp[:, :], ALU.mult, ALU.add))
            ch.wait()
            ch.did(v.tensor_scalar(gsc[:, :], gsc[:, :], 1e-20, 1.0 / 32768, ALU.add, ALU.mult))
            ch.wait()
            ch.did(v.reciprocal(gsc[:, :], gsc[:, :]))
            ch.wait()
            ch.did(v.tensor_tensor(wm_sb[:, :], wm_sb[:, :], gsc[:, :], ALU.mult))
            ch.did(v.tensor_tensor(bm_sb[:, :], bm_sb[:, :], gsc[:, :], ALU.mult))
            ch.did(v.tensor_tensor(embs[:, :], embs[:, :], gsc[0:TYPES, :], ALU.mult))
            ch.did(v.tensor_tensor(bg[:, :], bg_i[:, 0:2], bg_h[:, 0:2], ALU.add))
            ch.wait()
            ch.did(v.tensor_copy(embh[:, 0, :], embs[:, :]))
            ch.wait()
            v.tensor_tensor(embh[:, 1, :], embs[:, :], embh[:, 0, :], ALU.subtract).then_inc(sem("scaled"), 1)
            v.wait_ge(sem("g_col"), 1)
            ch.did(v.reciprocal(ginv[:, :], psG))

        def norm0_vector(v, ch):
            P = slice(0, LO)
            v.wait_ge(sem("std0"), 1)
            ch.did(v.reciprocal(rstd[P, :], rstd[P, :]))
            ch.wait()
            v.tensor_tensor(nmr[P, :], nmean[P, :], rstd[P, :], ALU.mult).then_inc(sem("nmr0"), 1)

        def check_sorted(v, ch):
            P = slice(0, LO)
            v.wait_ge(sem("dst_in"), 32)
            ch.did(v.tensor_tensor(unsorted[P, :], raw_dst[P, 1:PARTE + 1], raw_dst[P, 0:PARTE], ALU.is_lt))
            ch.wait()
            ch.did(v.tensor_reduce(flags[P, 1:2], unsorted[P, :], AX, ALU.max))
            ch.wait()

        def build_all_vector(v, ch):
            scale_vector(v, ch)
            build_vector(v, 0, 0, ch)
            norm0_vector(v, ch)
            v.wait_ge(sem("runs_in1"), 16 * 3 * (SB - 2))
            unpack_vector(v, ch, 2, SB - 2)
            for m in range(1, STEPS):
                search_runs(v, ch, m)
            build_vector(v, 1, 1, ch)
            build_vector(v, 2, 0, ch)
            v.wait_ge(sem("runs_in2"), 16 * 3 * SB)
            unpack_vector(v, ch, SB, 2)
            build_vector(v, 3, 1, ch)
            build_vector(v, 4, 0, ch)
            n = (CHUNKS - PEEL - 2) // 2
            with v.Fori(0, n) as i:
                with ch.loop(i, n, 2 * (1 + WIN) * BATCHES):
                    build_vector(v, 2 * i + PEEL, 1, ch)
                    build_vector(v, 2 * i + PEEL + 1, 0, ch)
            build_vector(v, CHUNKS - 2, 1, ch)
            P = slice(0, LO)
            v.wait_ge(sem("fields"), CHUNKS)
            ch.did(v.tensor_reduce(flags[P, 0:1], over[P, :], AX, ALU.max))
            ch.wait()
            v.tensor_tensor(flags[P, 2:3], flags[P, 0:1], flags[P, 1:2], ALU.add).then_inc(sem("flags"), 1)
            build_vector(v, CHUNKS - 1, 0, ch)
            v.wait_ge(sem("flag_sum"), 1)
            v.tensor_scalar(flag_i[:, :], psFlag, 0.0, None, ALU.is_gt).then_inc(sem("flag_set"), 1)

        def block_of(v, ch, q, s):
            ch.did(v.tensor_scalar(q, s, 1.0 / LO, 0.5 / LO - 0.5, ALU.mult, ALU.add))
            ch.wait()
            ch.did(v.tensor_scalar(q, q, MAGIC, MAGIC, ALU.add, ALU.subtract))
            ch.wait()


        def blocks(n):
            return bass.ds(CB * n, CB) if not isinstance(n, int) else slice(CB * n, CB * n + CB)

        def nodes(n):
            return bass.ds(CH * n, CH) if not isinstance(n, int) else slice(CH * n, CH * n + CH)

        def post0_tensor(pe, n, t):
            if t == 0:
                positive(pe, sem("x1"), n)
                pe.wait_ge(sem("aggr"), n + 1)
                for j in range(CB):
                    last = pe.matmul(psX[:, j, :], aggr[:, LO * j:LO * (j + 1)], w0_sb[:, :], start=True, stop=True)
                last.then_inc(sem("psX"), 1)
            if t == 1:
                positive(pe, sem("hst"), n)
                pe.wait_ge(sem("h1"), n + 1)
                for j in range(CB):
                    last = pe.transpose(psT[:, LO * j:LO * (j + 1)], h1s[0:LO, j, :], ident[0:LO, 0:LO])
                last.then_inc(sem("psT"), 1)
            if t == 2:
                positive(pe, sem("tbs"), n)
                pe.wait_ge(sem("hst"), n + 1)
                for j in range(CB):
                    last = pe.matmul(psM[:, j, :], hst[:, LO * j:LO * (j + 1)], wm_sb[:, :], start=True, stop=True)
                last.then_inc(sem("psM"), 1)

        def post0_scalar(act, n, q, par, summed, split):
            P = slice(0, LO)
            summed(act, n)
            positive(act, sem("psX"), n)
            act.activation(aggr[:, :], psD[par], ACT.Relu, scale=1.0 / HSCALE).then_inc(sem("aggr"), 1)
            act.wait_ge(sem("pvar"), n + 1)
            act.activation(prs[P, :], pmv[P, :, 1], ACT.Sqrt, bias=epst[P, :]).then_inc(sem("pstd"), 1)
            act.wait_ge(sem("pnm"), n + 1)
            positive(act, sem("psT"), n)
            for j in range(CB):
                last = act.activation(h1s[P, j, :], x1s[P, j, :], ACT.Relu, bias=pnm[P, j:j + 1],
                                      scale=prs[P, j:j + 1])
            last.then_inc(sem("h1"), 1)
            act.wait_ge(sem("psT"), n + 1)
            positive(act, sem("psM"), n)
            positive(act, sem("h1T"), n)
            act.activation(hst[:, :], psT, ACT.Copy).then_inc(sem("hst"), 1)
            if split:
                act.wait_ge(sem("tbs"), n + 1)
                act.activation(tabv[1][P, blocks(q), 0, :], tbs[P, :, :], ACT.Copy).then_inc(sem("tab_hi"), 1)

        def post0_gpsimd(gp, n, q, split):
            gp.wait_ge(sem("x1"), n + 1)
            gp.tensor_copy(x_sb[0:LO, blocks(q), :], x1s[0:LO, :, :]).then_inc(sem("x1_kept"), 1)
            gp.wait_ge(sem("hst"), n + 1)
            gp.tensor_copy(h1T[:, nodes(q)], hst[:, :]).then_inc(sem("h1T"), 1)
            if split:
                gp.wait_ge(sem("tab_hi"), n + 1)
                gp.tensor_tensor(tabv[1][0:LO, blocks(q), 1, :], tbs[0:LO, :, :], tabv[1][0:LO, blocks(q), 0, :],
                                 ALU.subtract).then_inc(sem("tab_lo"), 1)

        def post0_vector(v, n, q, ch, spent):
            P = slice(0, LO)
            v.wait_ge(sem("psX"), n + 1)
            positive(v, sem("h1"), n)
            positive(v, sem("x1_kept"), n)
            v.tensor_tensor(x1s[P, :, :], psX, x_sb[P, blocks(q), :], ALU.add).then_inc(sem("x1"), 1)
            v.wait_ge(sem("x1"), n + 1)
            for j in range(CB):
                ch.did(v.bn_stats(pst[P, j, :], x1s[P, j, :]))
            ch.wait()
            ch.did(v.tensor_tensor(pmv[P, :, 0], pst[P, :, 1], pst[P, :, 4], ALU.add))
            ch.did(v.tensor_tensor(pmv[P, :, 1], pst[P, :, 1], pst[P, :, 4], ALU.subtract))
            ch.did(v.tensor_tensor(pm2[P, :], pst[P, :, 2], pst[P, :, 5], ALU.add))
            ch.wait()
            ch.did(v.scalar_tensor_tensor(pmv[P, :, 1], pmv[P, :, 1], 0.25, pmv[P, :, 1], ALU.mult, ALU.mult))
            ch.wait()
            v.scalar_tensor_tensor(pmv[P, :, 1], pm2[P, :], 1.0 / D, pmv[P, :, 1], ALU.mult, ALU.add)\
             .then_inc(sem("pvar"), 1)
            v.wait_ge(sem("pstd"), n + 1)
            ch.did(v.reciprocal(prs[P, :], prs[P, :]))
            ch.wait()
            v.scalar_tensor_tensor(pnm[P, :], pmv[P, :, 0], -0.5, prs[P, :], ALU.mult, ALU.mult).then_inc(sem("pnm"), 1)
            v.wait_ge(sem("psM"), n + 1)
            spent(n)
            v.tensor_tensor(tbs[P, :, :], psM, bm_sb[P, :].unsqueeze(1).broadcast_to([LO, CB, D]), ALU.add)\
             .then_inc(sem("tbs"), 1)

        def post1_tensor(pe, n, q, t):
            if t == 0:
                pe.wait_ge(sem("msg"), n + 1)
                positive(pe, sem("rz"), n)
                positive(pe, sem("nin"), n)
                for a in range(2):
                    w = slice(D * a, D * (a + 1))
                    pe.matmul(psRZ[:, a, :], wih_sb[:, w], msgs[:, :], start=True, stop=False)
                    last = pe.matmul(psRZ[:, a, :], whh_sb[:, w], h1T[:, nodes(q)], start=False, stop=True)
                last.then_inc(sem("psRZ"), 1)
                w = slice(2 * D, 3 * D)
                pe.matmul(psN[:, 0, :], wih_sb[:, w], msgs[:, :], start=True, stop=True)
                pe.matmul(psN[:, 1, :], whh_sb[:, w], h1T[:, nodes(q)], start=True, stop=True).then_inc(sem("psN"), 1)
            if t == 1:
                pe.wait_ge(sem("hnew"), n + 1)
                positive(pe, sem("result"), n)
                for j in range(CB):
                    last = pe.transpose(psO[:, j, :], hnew[:, LO * j:LO * (j + 1)], ident[:, :])
                last.then_inc(sem("psO"), 1)

        def post1_scalar(act, n, par, summed):
            summed(act, n)
            positive(act, sem("psN"), n)
            act.activation(msgs[:, :], psD[par], ACT.Copy, scale=ginv[:, 0:1]).then_inc(sem("msg"), 1)
            act.wait_ge(sem("psRZ"), n + 1)
            positive(act, sem("hnew"), n)
            for a in range(2):
                last = act.activation(rz[:, a, :], psRZ[:, a, :], ACT.Sigmoid, bias=bg[:, a:a + 1])
            last.then_inc(sem("rz"), 1)
            act.wait_ge(sem("nin"), n + 1)
            act.activation(nn[:, :], nin[:, :], ACT.Tanh, bias=bg_i[:, 2:3]).then_inc(sem("nn"), 1)

        def post1_vector(v, n, q, ch):
            v.wait_ge(sem("psN"), n + 1)
            v.wait_ge(sem("rz"), n + 1)
            ch.did(v.scalar_tensor_tensor(nin[:, :], psN[:, 1, :], bg_h[:, 2:3], rz[:, 0, :], ALU.add, ALU.mult))
            ch.wait()
            v.tensor_tensor(nin[:, :], nin[:, :], psN[:, 0, :], ALU.add).then_inc(sem("nin"), 1)
            v.wait_ge(sem("nn"), n + 1)
            positive(v, sem("psO"), n)
            ch.did(v.tensor_tensor(hnew[:, :], h1T[:, nodes(q)], nn[:, :], ALU.subtract))
            ch.wait()
            ch.did(v.tensor_tensor(hnew[:, :], rz[:, 1, :], hnew[:, :], ALU.mult))
            ch.wait()
            v.tensor_tensor(hnew[:, :], nn[:, :], hnew[:, :], ALU.add).then_inc(sem("hnew"), 1)
            v.wait_ge(sem("psO"), n + 1)
            v.tensor_tensor(x_sb[0:LO, blocks(q), :], psO, x_sb[0:LO, blocks(q), :], ALU.add).then_inc(sem("result"), 1)

        def store_result(sp, n, q):
            sp.wait_ge(sem("result"), n + 1)
            sp.dma_start(out_v[:, blocks(q), :], x_sb[0:LO, blocks(q), :]).then_inc(sem("out"), 16)


        def norm_vector(v, ch, reduced):
            reduced()
            ch.wait()
            P = slice(0, LO)
            v.tensor_scalar(deg[P, :], deg[P, :], 1.0, None, ALU.max).then_inc(sem("deg"), 1)
            v.wait_ge(sem("deg_root"), 1)
            ch.did(v.reciprocal(norm[P, :], norm[P, :]))
            ch.wait()
            ch.did(v.tensor_scalar(norm[P, :], norm[P, :], HSCALE, None, ALU.mult))
            ch.wait()

        def norm_scalar(act):
            act.wait_ge(sem("deg"), 1)
            act.activation(norm[0:LO, :], deg[0:LO, :], ACT.Sqrt).then_inc(sem("deg_root"), 1)

        def turn_tensor(pe, g):
            pe.wait_ge(sem("fields"), g + 1)
            positive(pe, sem("mch"), g)
            for k, f in enumerate((F_LO, F_COL, F_TA, F_SMALL)):
                lhs = fields[0:LO, g:g + 1, f, :] if isinstance(g, int) else fields[0:LO, bass.ds(g, 1), f, :]
                last = pe.matmul(psTurn[:, k, :], lhs.rearrange("p g e -> p (g e)"), identh[0:LO, 0:LO],
                                 start=True, stop=True)
            last.then_inc(sem("turned"), 1)

        def turn_scalar(act, g, par):
            act.wait_ge(sem("turned"), g + 1)
            positive(act, sem("onehot"), BATCHES * (g - 1))
            for k in range(2):
                act.activation(mch[:, par, k, :, :], spread(psTurn[:, k, :], [128, CHWIN, 2]), ACT.Copy)
            act.activation(mch_s[:, par, 0, :], psTurn[:, 2, :], ACT.Copy)
            act.activation(mch_s[:, par, 1:1 + WIN, :], psTurn[:, 3, :].unsqueeze(1).broadcast_to([128, WIN, CHWIN]),
                           ACT.Copy).then_inc(sem("mch"), 1)

        def build_tensor(pe, c, par):
            own = [0]

            def own_degrees(units):
                if (own[0] + 1) * 10 <= units * UNIT * WIN:
                    degree_tensor(pe, par, own[0])
                    own[0] += 1
            for w in range(CHWIN):
                b, k = divmod(w, BATCH)
                u, i = divmod(w, UNIT)
                slot = (par + b) % 2
                if k == 0:
                    pe.wait_ge(sem("onehot"), BATCHES * c + b + 1)
                if i == 0:
                    back = (1, 0, 2) if par == 0 else (2, 1, 0)
                    positive(pe, sem("evac"), UNITS * c + (u - 2 if u >= PSLOTS else -back[u]))
                o = WCOLS * (i % BANKW)
                last = pe.matmul(ps[:, 2 * ((u + par) % PSLOTS) + i // BANKW, o:o + WCOLS], lohot[:, slot, k, :],
                                 combo[:, slot, k, :], start=True, stop=True)
                if i == UNIT - 1 or w == CHWIN - 1:
                    last.then_inc(sem("built"), 1)
                elif k == BATCH - 1:
                    last.then_inc(sem("spent"), 1)
                if not (isinstance(c, int) and c == 0) and w % 5 == 4:
                    degree_tensor(pe, 1 - par, w // 5)
                if isinstance(c, int) and c == CHUNKS - 1 and w % 5 == 0:
                    own_degrees(u - 2)
                if w == UNIT and not (isinstance(c, int) and c == CHUNKS - 1):
                    turn_tensor(pe, c + 1)
            return own[0]

        def degree_tensor(pe, par, j):
            last = pe.matmul(psDeg, identh[:, :], adj[par][:, 0:BLOCKS, 10 * j:10 * j + 10], start=False, stop=False,
                             skip_group_check=True)
            if j == CH // 10 - 1:
                last.then_inc(sem("degree"), 1)

        def build_scalar(act, c, par):
            for u in range(UNITS):
                act.wait_ge(sem("built"), UNITS * c + u + 1)
                if u == 0:
                    positive(act, sem("degree"), c - 1)
                    if not (isinstance(c, int) and c == 0):
                        if par:
                            positive(act, sem("adj_out1"), 8 * (c - 1))
                        else:
                            act.wait_ge(sem("adj_out0"), 8 * c)
                s = 2 * ((u + par) % PSLOTS)
                n = CHWIN - UNIT * u
                whole = lambda k, banks, m: (adj[par][:, :, k:k + banks * m]
                                             .rearrange("p h (b x) -> p h b x", b=banks))
                if n >= UNIT:
                    x = WIN * BANKW
                    act.activation(whole(x * 2 * u, 2, x),
                                   ps[:, s:s + 2, 0:x * SLOTS].rearrange("p b (x h) -> p h b x", h=SLOTS),
                                   ACT.Copy).then_inc(sem("evac"), 1)
                else:
                    for b in range(2):
                        x = WIN * (BANKW if b == 0 else n - BANKW)
                        last = act.activation(whole(WIN * (UNIT * u + BANKW * b), 1, x),
                                              ps[:, s + b:s + b + 1, 0:x * SLOTS]
                                              .rearrange("p b (x h) -> p h b x", h=SLOTS), ACT.Copy)
                    last.then_inc(sem("evac"), 1)
                if u == 2 and not (isinstance(c, int) and c == CHUNKS - 1):
                    turn_scalar(act, c + 1, 1 - par)
                if u == 6:
                    if isinstance(c, int) and c == 0:
                        act.wait_ge(sem("nmr0"), 1)
                    for j in range(CB):
                        at = bass.ds(CB * c + j, 1) if not isinstance(c, int) else slice(CB * c + j, CB * c + j + 1)
                        last = act.activation(h0[0:LO, at, :], x_sb[0:LO, at, :], ACT.Relu, bias=nmr[0:LO, at],
                                              scale=rstd[0:LO, at])
                    last.then_inc(sem("h0_done"), 1)

        def build_vector(v, c, par, ch):
            for b in range(BATCHES):
                slot = (par + b) % 2
                if b == 0:
                    v.wait_ge(sem("mch"), c + 1)
                if b == 1:
                    positive(v, sem("built"), UNITS * c)
                else:
                    positive(v, sem("spent"), (BATCHES - 1) * c + max(b - 1, 0))
                at = slice(BATCH * b, BATCH * (b + 1))
                lo2, col2 = (mch[:, par, k, at, :] for k in range(2))
                even = LO + 1
                ch.did(v.tensor_tensor(
                    lohot[:, slot, :, 0:even].rearrange("p k (n t) -> p k n t", t=2),
                    iota_lo[:, 0:even].rearrange("p (n t) -> p n t", t=2).unsqueeze(1)
                        .broadcast_to([128, BATCH, even // 2, 2]),
                    lo2.unsqueeze(2).broadcast_to([128, BATCH, even // 2, 2]), ALU.is_equal))
                for d in range(WIN):
                    cols = slice(SLOTS * d, SLOTS * d + BLOCKS)
                    ch.did(v.tensor_tensor(
                        combo[:, slot, :, cols].rearrange("p k (n t) -> p k n t", t=2),
                        iota_w[:, cols].rearrange("p (n t) -> p n t", t=2).unsqueeze(1)
                            .broadcast_to([128, BATCH, BLOCKS // 2, 2]),
                        col2.unsqueeze(2).broadcast_to([128, BATCH, BLOCKS // 2, 2]), ALU.is_equal))
                ch.wait(but=WIN)
                v.tensor_tensor(typehot[:, slot, :, :, :],
                                iota_t[:, :, :].unsqueeze(1).broadcast_to([128, BATCH, 1 + WIN, TB]),
                                mch_s[:, par, :, at].rearrange("p m k -> p k m").unsqueeze(3)
                                    .broadcast_to([128, BATCH, 1 + WIN, TB]),
                                ALU.is_equal).then_inc(sem("onehot"), 1)

        PEEL = 5

        def build_sync(sp, c, par):
            sp.wait_ge(sem("evac"), UNITS * (c + 1))
            at = slice(c, c + 1) if isinstance(c, int) else bass.ds(c, 1)
            sp.dma_start(adj_d[at, :, :].rearrange("a p n -> (a p) n"), ring[:, par, :]).then_inc(sem(f"adj_out{par}"), 16)

        def chunk(L, c):
            if isinstance(c, int):
                if c < 2:
                    return (CHUNKS - 1 - c, CHUNKS - 3 - c)[L]
                if L and c >= CHUNKS - 2:
                    return c
            return c - 2

        def load_sync(sp, L, c, par):
            q = chunk(L, c)
            at = slice(q, q + 1) if isinstance(q, int) else bass.ds(q, 1)
            for j, (a, b) in enumerate(PARTS):
                if L == 0 and not (isinstance(c, int) and c >= CHUNKS - 2):
                    b = min(b, BLOCKS)
                sp.wait_ge(sem(f"used{L}"), 4 * (c - 2) + j + 1)
                sp.dma_start(ring[:, par, a * CH:b * CH],
                             adj_d[at, :, a * CH:b * CH].rearrange("a p n -> (a p) n"))\
                  .then_inc(sem(f"load{L}_{par}_{j}"), 16)

        def product_tensor(pe, L, c, par, between, ready):
            bank = 1 - par if L else par
            K = (LO, 128)[L]
            order = list(range((BLOCKS, SLOTS)[L]))
            if L and isinstance(c, int) and c == 0:
                for h in range(CB * chunk(1, 0), CB * chunk(1, 0) + CB):
                    order.remove(h)
                    order.append(h)
            for j, (a, b) in enumerate(PARTS):
                if not (isinstance(c, int) and c < 2):
                    pe.wait_ge(sem(f"load{L}_{par}_{j}"), 8 * c - 8 * par)
                for h in order[a:b]:
                    if isinstance(c, int) and c == 0:
                        ready(h)
                    for s in range(2):
                        last = pe.matmul(psD[bank], tabv[L][0:K, h, s, :], adj[par][0:K, h, :],
                                         start=h == order[0] and s == 0, stop=h == order[-1] and s == 1)
                last.then_inc(sem(f"used{L}"), 1)
                between(j)

        fast_summed = [lambda eng, n: eng.wait_ge(sem("used0"), 4 * n + 4),
                       lambda eng, n: eng.wait_ge(sem("used1"), 4 * n + 4)]

        def build_all_tensor(pe):
            pe.matmul(psDeg, zeroh[:, 0:128], zeroh[:, 0:BLOCKS * 10], start=True, stop=False, skip_group_check=True)
            own = []
            def body(c, par):
                if isinstance(c, int) and c == CHUNKS - 1:
                    pe.wait_ge(sem("flags"), 1)
                    pe.matmul(psFlag, flags[0:LO, 2:3], ones[0:LO, 0:1], start=True, stop=True)\
                      .then_inc(sem("flag_sum"), 1)
                own.append(build_tensor(pe, c, par))
            over_chunks(pe, body, first=PEEL, last=2)
            pe.wait_ge(sem("evac"), UNITS * CHUNKS)
            for j in range(own[-1], CH // 10):
                degree_tensor(pe, 0, j)
            pe.matmul(psDeg, zeroh[:, 0:128], zeroh[:, 0:BLOCKS * 10], start=False, stop=True, skip_group_check=True)\
              .then_inc(sem("degrees"), 1)

        def fast_tensor(pe):
            def ready0(h):
                pe.wait_ge(sem("tab0"), h + 1)

            def ready1(h):
                if h == 0:
                    pe.wait_ge(sem("tab_lo"), CHUNKS - 1)
                if h == BLOCKS:
                    pe.wait_ge(sem("emb_in"), 16 * TA)
                if h == CB * chunk(1, 0):
                    pe.wait_ge(sem("tab_lo"), CHUNKS)

            def body0(c, par):
                def between(j):
                    if not (isinstance(c, int) and c == 0) and j != 1:
                        post0_tensor(pe, c - 1, (0, None, 1, 2)[j])
                product_tensor(pe, 0, c, par, between, ready0)

            def body1(c, par):
                def between(j):
                    if isinstance(c, int) and c == 0:
                        if j < 3:
                            post0_tensor(pe, CHUNKS - 1, j)
                    elif j in (1, 3):
                        post1_tensor(pe, c - 1, chunk(1, c - 1) if isinstance(c, int) else c - 3, j // 2)
                product_tensor(pe, 1, c, par, between, ready1)

            over_chunks(pe, body0, first=3)
            over_chunks(pe, body1, first=3, last=2)
            for t in range(2):
                post1_tensor(pe, CHUNKS - 1, CHUNKS - 1, t)

        def fast_scalar(act):
            norm_scalar(act)
            act.wait_ge(sem("norm"), 1)
            for b in range(BLOCKS):
                act.activation(tabv[0][0:LO, b, 0, :], h0[0:LO, b, :], ACT.Copy, scale=norm[0:LO, b:b + 1])\
                   .then_inc(sem("tab0_hi"), 1)
            act.wait_ge(sem("tab1_zero"), 1)
            over_chunks(act, lambda c, par: post0_scalar(act, c, chunk(0, c), par, fast_summed[0], True), first=3)
            over_chunks(act, lambda c, par: post1_scalar(act, c, 1 - par, fast_summed[1]))

        def build_all_gpsimd(gp):
            gp.wait_ge(sem("fields"), SB + 2)
            gp.wait_ge(sem("runs_in2"), 16 * 3 * SB)
            gp.wait_ge(sem("runs_in3"), 16 * 3 * (CHUNKS - 2 * SB))
            ch = Chain(gp, sem("g_unpack"))
            n = (CHUNKS - SB - 2) // 2
            with gp.Fori(0, n) as i:
                with ch.loop(i, n, UNPACK_STEPS):
                    unpack_gpsimd(gp, ch, 2 * i + SB + 2)
            def add_bias(c, par):
                gp.wait_ge(sem("h0_done"), c + 1)
                a = x_sb[0:LO, blocks(c), :]
                gp.tensor_tensor(a, a, b0_sb[0:LO, :].unsqueeze(1).broadcast_to([LO, CB, D]), ALU.add)\
                  .then_inc(sem("x_b"), 1)
            over_chunks(gp, add_bias)

        def fast_gpsimd(gp):
            gp.wait_ge(sem("turned"), CHUNKS)
            gp.memset(tab[1].bitcast(I32), 0).then_inc(sem("tab1_zero"), 1)
            gp.wait_ge(sem("tab1_zero"), 1)
            over_chunks(gp, lambda c, par: post0_gpsimd(gp, c, chunk(0, c), True), first=3)

        def fast_vector(v):
            ch = Chain(v, sem("v_fast"))
            def reduced():
                v.wait_ge(sem("degrees"), 1)
                ch.did(v.tensor_reduce(deg[:, :], psDeg.rearrange("p (h n) -> p h n", n=10), AX, ALU.add))
            norm_vector(v, ch, reduced)
            v.sem_inc(sem("norm"), 1)
            for b in range(BLOCKS):
                v.wait_ge(sem("tab0_hi"), b + 1)
                v.scalar_tensor_tensor(tabv[0][0:LO, b, 1, :], h0[0:LO, b, :], norm[0:LO, b:b + 1],
                                       tabv[0][0:LO, b, 0, :], ALU.mult, ALU.subtract).then_inc(sem("tab0"), 1)
            v.wait_ge(sem("x_b"), CHUNKS)
            spent = lambda n: positive(v, sem("tab_lo"), n)
            over_chunks(v, lambda c, par: post0_vector(v, c, chunk(0, c), ch, spent), ch, 7, first=3)
            over_chunks(v, lambda c, par: post1_vector(v, c, chunk(1, c), ch), ch, 3, first=3, last=2)

        def fast_sync(sp):
            sp.wait_ge(sem("tab1_zero"), 1)
            sp.wait_ge(sem("scaled"), 1)
            for k in range(TA):
                sp.dma_start(tabv[1][LO + k:LO + k + 1, BLOCKS:SLOTS, :, :],
                             embh[TB * k:TB * (k + 1), :, :]).then_inc(sem("emb_in"), 16)
            sp.wait_ge(sem("adj_out0"), 16 * ((CHUNKS + 1) // 2))
            sp.wait_ge(sem("adj_out1"), 16 * (CHUNKS // 2))
            for L in range(2):
                load_sync(sp, L, 2, 0)
                with sp.Fori(0, (CHUNKS - 5) // 2) as i:
                    load_sync(sp, L, 2 * i + 3, 1)
                    load_sync(sp, L, 2 * i + 4, 0)
                load_sync(sp, L, CHUNKS - 2, 1)
                load_sync(sp, L, CHUNKS - 1, 0)
            over_chunks(sp, lambda c, par: store_result(sp, c, chunk(1, c)), first=3, last=2)
            sp.wait_ge(sem("emb_in"), 16 * TA)
            sp.wait_ge(sem("out"), 16 * CHUNKS)


        def general_sync(sp):
            sp.wait_ge(sem("adj_out0"), 16 * ((CHUNKS + 1) // 2))
            sp.wait_ge(sem("adj_out1"), 16 * (CHUNKS // 2))
            sp.wait_ge(sem("degrees"), 1)
            for k, a in enumerate((src, dst, typ)):
                sp.dma_start(flat_i[0:LO, k, :], a.rearrange("(p n) -> p n", p=LO)).then_inc(sem("flat_in"), 16)
            sp.wait_ge(sem("tab_zero"), 1)
            zero = tab[0].bitcast(F32)[0:LO, :][:, 0:(N + LO) // LO * D]
            for k in range(2):
                sp.dma_start(sum_d[k].rearrange("(p r) f -> p (r f)", p=LO), zero).then_inc(sem("sum_zero"), 16)
            sp.wait_ge(sem("scaled"), 1)
            sp.dma_start(emb_d, embs[:, :]).then_inc(sem("gemb_out"), 16)
            sp.wait_ge(sem("h0_scaled"), 1)
            sp.dma_start(table_v, h0[0:LO, :, :]).then_inc(sem("table_out"), 16)

            def sums_in(L, n):
                positive(sp, sem(f"gturned{L}"), n)
                sp.dma_start(sum_in[0:LO, :, :], sum_v[L][:, blocks(n), :]).then_inc(sem(f"sum_in{L}"), 16)

            def body0(n, par):
                sums_in(0, n)
                sp.wait_ge(sem("tbs"), n + 1)
                sp.dma_start(table_v[:, blocks(n), :], tbs[0:LO, :, :]).then_inc(sem("table1_out"), 16)

            sp.wait_ge(sem("gadded0"), 16 * PARTE)
            over_chunks(sp, body0)
            sp.wait_ge(sem("gadded1"), 16 * PARTE)

            def body1(n, par):
                sums_in(1, n)
                store_result(sp, n, n)

            over_chunks(sp, body1)
            sp.wait_ge(sem("out"), 16 * CHUNKS)

        def general_scalar(act):
            norm_scalar(act)
            done = lambda L: lambda eng, n: eng.wait_ge(sem(f"gturned{L}"), n + 1)
            over_chunks(act, lambda n, par: post0_scalar(act, n, n, par, done(0), False))
            over_chunks(act, lambda n, par: post1_scalar(act, n, par, done(1)))

        def general_gpsimd(gp):
            gp.wait_ge(sem("degrees"), 1)
            gp.memset(before[:, :], 1.0).then_inc(sem("g1"), 1)
            gp.memset(tab[0].bitcast(I32), 0).then_inc(sem("tab_zero"), 1)
            gp.wait_ge(sem("g1"), 1)
            gp.affine_select(out=before[:, :], in_=before[:, :], compare_op=ALU.is_gt, fill=0.0, base=0,
                             pattern=[[-1, 128]], channel_multiplier=1)
            gp.iota(trash_c, [[1, 1]], base=N, channel_multiplier=1,
                    allow_small_or_imprecise_dtypes=True).then_inc(sem("g1"), 1)
            gp.wait_ge(sem("sum_zero"), 32)
            gp.wait_ge(sem("gemb_out"), 16)
            for L in range(2):
                if L:
                    gp.wait_ge(sem("table1_out"), 16 * CHUNKS)
                else:
                    gp.wait_ge(sem("table_out"), 16)

                def tile(t):
                    gp.wait_ge(sem(f"gindex{L}"), t + 1)
                    gp.sem_inc(sem("g_seen"), 1)
                    gp.indirect_dma_start(rows_in[0:NE, :], None, table_d,
                                          bass.IndirectOffsetOnAxis(isrc[0:NE, :], 0)).then_inc(sem(f"grows{L}"), 16)
                    if L:
                        gp.indirect_dma_start(erows_in[0:NE, :], None, emb_d,
                                              bass.IndirectOffsetOnAxis(itype[0:NE, :], 0)).then_inc(sem("gerows"), 16)
                    gp.wait_ge(sem(f"gsums{L}"), t + 1)
                    gp.sem_inc(sem("g_seen"), 1)
                    gp.indirect_dma_start(sum_d[L], bass.IndirectOffsetOnAxis(idst[0:NE, :], 0),
                                          sums[0:NE, :], None, compute_op=ALU.add).then_inc(sem(f"gadded{L}"), 16)

                over_tiles(gp, tile)
                if L == 0:
                    over_chunks(gp, lambda n, par: post0_gpsimd(gp, n, n, False))

        def general_vector(v):
            ch = Chain(v, sem("v_general"))
            P = slice(0, LO)
            v.wait_ge(sem("flat_in"), 48)
            v.wait_ge(sem("g1"), 2)
            ch.did(v.tensor_copy(src_f[P, :], flat_i[P, 0, :]))
            ch.did(v.tensor_copy(dst_f[P, :], flat_i[P, 1, :]))
            ch.did(v.tensor_scalar(flat_i[P, 2, :], flat_i[P, 2, :], 0.0, float(TYPES - 1), ALU.max, ALU.min))
            ch.wait()
            block_of(v, ch, q_f[P, :], src_f[P, :])
            ch.did(v.scalar_tensor_tensor(lo_f[P, :], q_f[P, :], -float(LO), src_f[P, :], ALU.mult, ALU.add))
            ch.wait()
            with v.Fori(0, PARTE) as t:
                at = bass.ds(t, 1)
                v.wait_ge(sem("ghist"), t + 1)
                v.tensor_scalar(ghot[P, 0:LO], iota_lo[P, 0:LO], lo_f[P, at], None, ALU.is_equal)
                v.tensor_scalar(ghot[P, 128:128 + BLOCKS], iota_lo[P, 0:BLOCKS], q_f[P, at], None, ALU.is_equal)\
                 .then_inc(sem("ghot"), 1)

            def reduced():
                v.wait_ge(sem("ghist"), PARTE + 2)
                ch.did(v.tensor_copy(deg[P, :], psDeg[P, 0:BLOCKS]))
            norm_vector(v, ch, reduced)
            v.wait_ge(sem("h0_done"), CHUNKS)
            v.tensor_tensor(h0[P, :, :], h0[P, :, :], spread(norm[P, :], [LO, BLOCKS, D]), ALU.mult)\
             .then_inc(sem("h0_scaled"), 1)
            v.wait_ge(sem("x_b"), CHUNKS)
            for L in range(2):
                def tile(t):
                    at = bass.ds(t, 1) if not isinstance(t, int) else slice(t, t + 1)
                    positive(v, sem(f"gadded{L}"), 16 * t)
                    v.tensor_copy(itype[P, :], flat_i[P, 2, at])
                    v.tensor_copy(isrc[P, :], flat_i[P, 0, at]).then_inc(sem(f"gindex{L}"), 1)
                    v.tensor_scalar(diag[P, 0:NE], ident[P, 0:NE], dst_f[P, at], None, ALU.mult)\
                     .then_inc(sem(f"gdiag{L}"), 1)
                    v.wait_ge(sem(f"gacross{L}"), t + 1)
                    v.tensor_scalar(same[P, 0:NE], psB[P, 0:NE], dst_f[P, at], None, ALU.is_equal)\
                     .then_inc(sem(f"gsame{L}"), 1)
                    v.wait_ge(sem(f"gsame{L}"), t + 1)
                    ch.did(v.tensor_tensor(lower[P, 0:NE], same[P, 0:NE], before[P, 0:NE], ALU.mult))
                    ch.wait()
                    ch.did(v.tensor_reduce(count_c[P, :], lower[P, 0:NE], AX, ALU.max))
                    ch.did(v.tensor_tensor(toward_c[P, :], trash_c[P, :], dst_f[P, at], ALU.subtract))
                    ch.wait()
                    ch.did(v.tensor_tensor(dup_c[P, :], toward_c[P, :], count_c[P, :], ALU.mult))
                    ch.wait()
                    ch.did(v.tensor_tensor(idst[P, :], dup_c[P, :], dst_f[P, at], ALU.add))
                    v.wait_ge(sem(f"gproduct{L}"), t + 1)
                    ch.wait()
                    v.tensor_copy(sums[P, :], psS[P, :]).then_inc(sem(f"gsums{L}"), 1)

                over_tiles(v, tile, ch, 5)
                if L:
                    v.wait_ge(sem("h1T"), CHUNKS)
                if L == 0:
                    spent = lambda n: positive(v, sem("table1_out"), 16 * n)
                    over_chunks(v, lambda n, par: post0_vector(v, n, n, ch, spent), ch, 7)
                else:
                    over_chunks(v, lambda n, par: post1_vector(v, n, n, ch), ch, 3)

        def general_tensor(pe):
            psHist = ps[0:LO, 6, 0:BLOCKS]
            pe.matmul(psHist, zeroh[0:LO, 0:LO], zeroh[0:LO, 0:BLOCKS], start=True, stop=False,
                      skip_group_check=True).then_inc(sem("ghist"), 1)
            with pe.Fori(0, PARTE) as t:
                pe.wait_ge(sem("ghot"), t + 1)
                pe.matmul(psHist, ghot[0:LO, 0:LO], ghot[0:LO, 128:128 + BLOCKS], start=False, stop=False,
                          skip_group_check=True).then_inc(sem("ghist"), 1)
            pe.matmul(psHist, zeroh[0:LO, 0:LO], zeroh[0:LO, 0:BLOCKS], start=False, stop=True,
                      skip_group_check=True).then_inc(sem("ghist"), 1)
            for L, post, steps in ((0, post0_tensor, 3), (1, post1_tensor, 2)):
                def tile(t):
                    pe.wait_ge(sem(f"gdiag{L}"), t + 1)
                    pe.matmul(psB[0:NE, 0:NE], ones[0:NE, 0:NE], diag[0:NE, 0:NE], start=True, stop=True)\
                      .then_inc(sem(f"gacross{L}"), 1)
                    pe.wait_ge(sem(f"gsame{L}"), t + 1)
                    pe.wait_ge(sem(f"grows{L}"), 16 * t + 16)
                    last = pe.matmul(psS[0:NE, :], same[0:NE, 0:NE], rows_in[0:NE, :], start=True, stop=L == 0)
                    if L:
                        pe.wait_ge(sem("gerows"), 16 * t + 16)
                        last = pe.matmul(psS[0:NE, :], same[0:NE, 0:NE], erows_in[0:NE, :], start=False, stop=True)
                    last.then_inc(sem(f"gproduct{L}"), 1)

                over_tiles(pe, tile)

                if L:
                    pe.wait_ge(sem("h1T"), CHUNKS)

                def body(n, par):
                    pe.wait_ge(sem(f"sum_in{L}"), 16 * n + 16)
                    for j in range(CB):
                        last = pe.transpose(psD[par][:, LO * j:LO * (j + 1)], sum_in[0:LO, j, :], ident[0:LO, 0:LO])
                    last.then_inc(sem(f"gturned{L}"), 1)
                    for k in range(steps):
                        post(pe, n, k) if L == 0 else post(pe, n, n, k)

                over_chunks(pe, body)

        block = ctx.enter_context(nc.Block())

        def branch(eng, fast, general):
            eng.wait_ge(sem("flag_set"), 1)
            flag = eng.value_load(flag_i[0:1, 0:1], min_val=0, max_val=1)
            with eng.If(flag == 0):
                fast(eng)
            with eng.Else():
                general(eng)

        @block.sync
        def _(sp):
            prepare_sync(sp)
            over_chunks(sp, lambda c, par: build_sync(sp, c, par), first=PEEL)
            branch(sp, fast_sync, general_sync)

        @block.scalar
        def _(act):
            prepare_scalar(act)
            over_chunks(act, lambda c, par: build_scalar(act, c, par), first=PEEL, last=2)
            branch(act, fast_scalar, general_scalar)

        @block.gpsimd
        def _(gp):
            prepare_gpsimd(gp)
            build_all_gpsimd(gp)
            branch(gp, fast_gpsimd, general_gpsimd)

        @block.vector
        def _(v):
            ch = Chain(v, sem("v_prep"))
            prepare_vector(v, ch)
            build_all_vector(v, ch)
            branch(v, fast_vector, general_vector)

        @block.tensor
        def _(pe):
            prepare_tensor(pe)
            build_all_tensor(pe)
            branch(pe, fast_tensor, general_tensor)


def kernel(x, src, dst, edge_type_9, L0_gnn_W, L0_gnn_b, L1_gnn_W_msg, L1_gnn_b_msg, L1_gnn_edge_embed,
           L1_gnn_W_ih, L1_gnn_W_hh, L1_gnn_b_ih, L1_gnn_b_hh):
    import concourse.bacc as bacc
    from concourse.bass_utils import run_bass_kernel_spmd

    turned = lambda a: np.ascontiguousarray(np.asarray(a).T)
    by_gate = lambda a: np.ascontiguousarray(np.asarray(a).reshape(3, D).T)
    arrays = {
        "x": np.asarray(x), "src": np.asarray(src), "dst": np.asarray(dst), "typ": np.asarray(edge_type_9),
        "w0t": turned(L0_gnn_W), "b0": np.asarray(L0_gnn_b), "wmt": turned(L1_gnn_W_msg),
        "bm": np.asarray(L1_gnn_b_msg), "emb": np.asarray(L1_gnn_edge_embed), "wiht": turned(L1_gnn_W_ih),
        "whht": turned(L1_gnn_W_hh), "bih": by_gate(L1_gnn_b_ih), "bhh": by_gate(L1_gnn_b_hh),
    }
    nc = bacc.Bacc("TRN2", target_bir_lowering=False, num_devices=1)
    args = [nc.dram_tensor(n, a.shape, mybir.dt.from_np(a.dtype), kind="ExternalInput").ap()
            for n, a in arrays.items()]
    out = nc.dram_tensor("out", (N, D), F32, kind="ExternalOutput").ap()
    gnn(nc, *args, out)
    r = run_bass_kernel_spmd(nc, [arrays], core_ids=[0])
    return r.results[0]["out"]
```
